# Optimizing a Trainium2 kernel written in Bass

```python
import numpy as np
import jax
import jax.numpy as jnp

def _softmax(x, axis=-1):
    return jax.nn.softmax(x, axis=axis)

def _gelu(x):
    return jax.nn.gelu(x, approximate=True)

def _silu(x):
    return jax.nn.silu(x)

def _sigmoid(x):
    return jax.nn.sigmoid(x)

def _layernorm(x, axis=-1, eps=1e-05):
    m = jnp.mean(x, axis=axis, keepdims=True)
    v = jnp.var(x, axis=axis, keepdims=True)
    return (x - m) / jnp.sqrt(v + eps)

def _scatter_add(tgt, idx, src, axis=0):
    return tgt.at[idx].add(src)

def _segment_sum(src, seg, n):
    return jax.ops.segment_sum(src, seg, n)
kernel_name = 'mk_decoder_preln_d4_seqx_r8_57423b'

def setup_inputs(seed: int=0):
    np.random.seed(seed)
    _w = jnp.asarray

    def _rec_inputs():
        import jax
        import jax.numpy as jnp
        _rk = jax.random.key(seed)
        x = 7.22e-05 + 1 * jax.random.normal(jax.random.fold_in(_rk, 1), (32, 100, 128), jnp.float32)
        _lenS = 100 - jax.random.randint(jax.random.fold_in(_rk, 7), (32,), 0, max(1, 100 // 4) + 1, jnp.int32)
        _lenS2 = 1444 - jax.random.randint(jax.random.fold_in(_rk, 8), (32,), 0, max(1, 1444 // 4) + 1, jnp.int32)
        _ctx_1024P = jax.random.normal(jax.random.fold_in(_rk, 11), (32, 16, 128), jnp.float32)
        _ctx_1024c = jax.random.dirichlet(jax.random.fold_in(_rk, 511), 0.3 * jnp.ones((16,), jnp.float32), (32, 1444))
        _ctx_1024t = jnp.einsum('bsk,bkd->bsd', _ctx_1024c, _ctx_1024P)
        _ctx_1024t = _ctx_1024t * jax.lax.rsqrt(jnp.mean(jnp.square(_ctx_1024t)) + 1e-12) * 0.953939
        ctx_1024 = 4.13588e-05 + 0.999923 * (_ctx_1024t + 0.3 * jax.random.normal(jax.random.fold_in(_rk, 611), (32, 1444, 128), jnp.float32))
        _validS = jnp.arange(100)[None, :] < _lenS[:, None]
        _validS2 = jnp.arange(1444)[None, :] < _lenS2[:, None]
        _causal = jnp.tril(jnp.ones((100, 100), dtype=bool))
        mask_Bx1xSxS2_bk1 = jnp.broadcast_to(_validS2[:, None, None, :], (32, 1, 100, 1444))
        return (x, ctx_1024, mask_Bx1xSxS2_bk1)
    x, ctx_1024, mask_Bx1xSxS2_bk1 = _rec_inputs()

    def _L0_attn_setup():
        import jax, jax.numpy as jnp
        import numpy as np
        LN_EPS = 1e-05
        D_HEAD = 64

        def _layernorm(x, w, b):
            x = x - jnp.mean(x, axis=-1, keepdims=True)
            scale = jnp.sqrt(jnp.mean(x * x, axis=-1, keepdims=True) + LN_EPS)
            return x / scale * w + b
        key = jax.random.key(seed)
        ks = jax.random.split(key, 6)
        B, S, D, H, Dh = (2, 256, 128, 16, D_HEAD)
        std = 0.02
        return {'resid_pre': jax.random.normal(ks[0], (B, S, D), dtype=jnp.float32), 'W_Q': jax.random.normal(ks[1], (H, D, Dh), dtype=jnp.float32) * std, 'b_Q': jnp.zeros((H, Dh), dtype=jnp.float32), 'W_K': jax.random.normal(ks[2], (H, D, Dh), dtype=jnp.float32) * std, 'b_K': jnp.zeros((H, Dh), dtype=jnp.float32), 'W_V': jax.random.normal(ks[3], (H, D, Dh), dtype=jnp.float32) * std, 'b_V': jnp.zeros((H, Dh), dtype=jnp.float32), 'W_O': jax.random.normal(ks[4], (H, Dh, D), dtype=jnp.float32) * std, 'b_O': jnp.zeros((D,), dtype=jnp.float32), 'ln1_w': jnp.ones((D,), dtype=jnp.float32), 'ln1_b': jnp.zeros((D,), dtype=jnp.float32), 'ln2_w': jnp.ones((D,), dtype=jnp.float32), 'ln2_b': jnp.zeros((D,), dtype=jnp.float32)}
    _L0_attn_all = _L0_attn_setup()
    _L0_attn_in = {k: v for k, v in _L0_attn_all.items() if k in ('W_Q', 'b_Q', 'W_K', 'b_K', 'W_V', 'b_V', 'W_O', 'b_O', 'ln1_w', 'ln1_b', 'ln2_w', 'ln2_b')}
    del _L0_attn_all

    def _L0_xattn_setup():
        import jax, jax.numpy as jnp
        import numpy as np
        N_HEADS = 16

        def _split(x, n_heads):
            b, s, d = x.shape
            return x.reshape(b, s, n_heads, d // n_heads).transpose(0, 2, 1, 3)
        key = jax.random.key(seed)
        k1, k2, k3, k4, k5 = jax.random.split(key, 5)
        B, S, D = (4, 256, 128)
        q = jax.random.normal(k1, (B, S, D), dtype=jnp.float32)
        k = jax.random.normal(k2, (B, S, D), dtype=jnp.float32)
        v = jax.random.normal(k3, (B, S, D), dtype=jnp.float32)
        Wq = jax.random.normal(k4, (D, D), dtype=jnp.float32) * D ** (-0.5)
        Wo = jax.random.normal(k5, (D, D), dtype=jnp.float32) * D ** (-0.5)
        return {'q': q, 'k': k, 'v': v, 'Wq': Wq, 'Wo': Wo}
    _L0_xattn_all = _L0_xattn_setup()
    _L0_xattn_in = {k: v for k, v in _L0_xattn_all.items() if k in ('Wq', 'Wo')}
    del _L0_xattn_all

    def _L0_ffn_setup():
        import jax, jax.numpy as jnp
        import numpy as np
        TOPK = 2
        key = jax.random.key(seed)
        k0, k1, k2, k3 = jax.random.split(key, 4)
        B, S, H, I, E = (4, 256, 128, 256, 8)
        return {'hidden_states': jax.random.normal(k0, (B, S, H), dtype=jnp.float32), 'w1': jax.random.normal(k1, (E, 2 * I, H), dtype=jnp.float32) * 0.02, 'w2': jax.random.normal(k2, (E, H, I), dtype=jnp.float32) * 0.02, 'router_w': jax.random.normal(k3, (E, H), dtype=jnp.float32) * 0.02}
    _L0_ffn_all = _L0_ffn_setup()
    _L0_ffn_in = {k: v for k, v in _L0_ffn_all.items() if k in ('w1', 'w2', 'router_w')}
    del _L0_ffn_all

    def _L1_attn_setup():
        import jax, jax.numpy as jnp
        import numpy as np
        from functools import partial
        B, S, D = (8, 256, 128)
        HEADS, DIM_HEAD = (16, 64)
        MAX_ALLOWABLE = 128 * 128 * 8

        def _max_pow2_divides(n):
            i = 1
            while n % 2 == 0:
                i *= 2
                n //= 2
            return i

        def _n_splits(bh, sq, sk):
            dimprod = bh * sq * sk
            true_divisor = dimprod / MAX_ALLOWABLE
            if true_divisor < 1:
                return 1
            if true_divisor >= bh:
                return bh
            nearest_pow2 = 2 ** np.round(np.log2(true_divisor))
            return int(min(_max_pow2_divides(bh), nearest_pow2))

        def _sdp_attention(q, k, v, scale):
            scores = jnp.einsum('bid,bjd->bij', q, k) * scale
            probs = jax.nn.softmax(scores, axis=2)
            return jnp.einsum('bij,bjd->bid', probs, v)

        def _scan_attention(q, k, v, scale, n_splits):
            bh = q.shape[0]
            nq, nk, nv = [h.reshape(n_splits, bh // n_splits, h.shape[-2], h.shape[-1]) for h in (q, k, v)]

            def body(carry, args):
                cq, ck, cv = args
                return (None, _sdp_attention(cq, ck, cv, scale))
            outs = jax.lax.scan(body, None, (nq, nk, nv))[1]
            return outs.reshape(-1, outs.shape[-2], outs.shape[-1])

        def _heads_to_batch(t, heads):
            b, s, d = t.shape
            return t.reshape(b, s, heads, d // heads).transpose(0, 2, 1, 3).reshape(b * heads, s, d // heads)

        def _batch_to_heads(t, heads):
            bh, s, d = t.shape
            return t.reshape(bh // heads, heads, s, d).transpose(0, 2, 1, 3).reshape(bh // heads, s, d * heads)
        key = jax.random.key(seed)
        k1, k2, k3, k4 = jax.random.split(key, 4)
        inner = HEADS * DIM_HEAD
        return {'hidden_states': jax.random.normal(k1, (B, S, D), jnp.float32), 'Wq': jax.random.normal(k2, (D, inner), jnp.float32) * D ** (-0.5), 'Wkv': jax.random.normal(k3, (D, 2 * inner), jnp.float32) * D ** (-0.5), 'Wo': jax.random.normal(k4, (inner, D), jnp.float32) * inner ** (-0.5), 'bo': jnp.zeros((D,), jnp.float32)}
    _L1_attn_all = _L1_attn_setup()
    _L1_attn_in = {k: v for k, v in _L1_attn_all.items() if k in ('Wq', 'Wkv', 'Wo', 'bo')}
    del _L1_attn_all

    def _L1_xattn_setup():
        import jax, jax.numpy as jnp
        import numpy as np
        B, S, D, H = (4, 256, 128, 16)
        HD = D // H
        key = jax.random.key(seed)
        ks = jax.random.split(key, 12)
        scale = 1.0 / np.sqrt(D)
        inp = {'queries': jax.random.normal(ks[0], (B, S, D), jnp.float32), 'keys': jax.random.normal(ks[1], (B, S, D), jnp.float32), 'values': jax.random.normal(ks[2], (B, S, D), jnp.float32), 'mask': jax.random.randint(ks[3], (B, 1, S, S), 0, 2).astype(bool), 'Wq': jax.random.normal(ks[4], (D, D), jnp.float32) * scale, 'bq': jnp.zeros((D,), jnp.float32), 'Wk': jax.random.normal(ks[5], (D, D), jnp.float32) * scale, 'bk': jnp.zeros((D,), jnp.float32), 'Wv': jax.random.normal(ks[6], (D, D), jnp.float32) * scale, 'bv': jnp.zeros((D,), jnp.float32), 'Wo': jax.random.normal(ks[7], (D, D), jnp.float32) * scale, 'bo': jnp.zeros((D,), jnp.float32)}
        return inp
    _L1_xattn_all = _L1_xattn_setup()
    _L1_xattn_in = {k: v for k, v in _L1_xattn_all.items() if k in ('Wq', 'bq', 'Wk', 'bk', 'Wv', 'bv', 'Wo', 'bo')}
    del _L1_xattn_all

    def _L1_ffn_setup():
        import jax, jax.numpy as jnp
        import numpy as np
        D_MODEL = 128
        D_FF = 512
        N_EXPERTS = 8
        TOP_K = 2

        def _ffn(x, w1, b1, w2, b2):
            h = jax.nn.gelu(x @ w1.T + b1)
            return h @ w2.T + b2
        key = jax.random.key(seed)
        ks = jax.random.split(key, 12)
        s = 0.02
        x = jax.random.normal(ks[0], (4, 256, D_MODEL), dtype=jnp.float32)
        shared_w1 = jax.random.normal(ks[1], (D_FF, D_MODEL), dtype=jnp.float32) * s
        shared_b1 = jnp.zeros((D_FF,), dtype=jnp.float32)
        shared_w2 = jax.random.normal(ks[2], (D_MODEL, D_FF), dtype=jnp.float32) * s
        shared_b2 = jnp.zeros((D_MODEL,), dtype=jnp.float32)
        router_w = jax.random.normal(ks[3], (N_EXPERTS, D_MODEL), dtype=jnp.float32) * s
        router_b = jnp.zeros((N_EXPERTS,), dtype=jnp.float32)
        spec_w1 = jax.random.normal(ks[4], (N_EXPERTS, D_FF, D_MODEL), dtype=jnp.float32) * s
        spec_b1 = jnp.zeros((N_EXPERTS, D_FF), dtype=jnp.float32)
        spec_w2 = jax.random.normal(ks[5], (N_EXPERTS, D_MODEL, D_FF), dtype=jnp.float32) * s
        spec_b2 = jnp.zeros((N_EXPERTS, D_MODEL), dtype=jnp.float32)
        return dict(x=x, shared_w1=shared_w1, shared_b1=shared_b1, shared_w2=shared_w2, shared_b2=shared_b2, router_w=router_w, router_b=router_b, spec_w1=spec_w1, spec_b1=spec_b1, spec_w2=spec_w2, spec_b2=spec_b2)
    _L1_ffn_all = _L1_ffn_setup()
    _L1_ffn_in = {k: v for k, v in _L1_ffn_all.items() if k in ('shared_w1', 'shared_b1', 'shared_w2', 'shared_b2', 'router_w', 'router_b', 'spec_w1', 'spec_b1', 'spec_w2', 'spec_b2')}
    del _L1_ffn_all

    def _L2_attn_setup():
        import jax, jax.numpy as jnp
        import numpy as np
        NUM_HEADS = 16
        N_EMBD = 128

        def alibi_bias(num_heads: int, seq_len: int) -> jnp.ndarray:
            pos = jnp.arange(seq_len, dtype=jnp.float32)
            dgrid = pos[None, :] - pos[:, None]
            slopes = 2.0 ** (-8.0 / num_heads * (jnp.arange(num_heads, dtype=jnp.float32) + 1.0))
            bias = slopes[:, None, None] * dgrid[None, :, :]
            return jnp.where(dgrid[None, :, :] > 0, -jnp.inf, bias)
        key = jax.random.key(seed)
        k1, k2, k3 = jax.random.split(key, 3)
        B, L, E = (2, 256, N_EMBD)
        x = jax.random.normal(k1, (B, L, E), dtype=jnp.float32)
        w_in = jax.random.normal(k2, (3 * E, E), dtype=jnp.float32) * 0.02
        w_out = jax.random.normal(k3, (E, E), dtype=jnp.float32) * 0.02
        return {'x': x, 'w_in': w_in, 'w_out': w_out}
    _L2_attn_all = _L2_attn_setup()
    _L2_attn_in = {k: v for k, v in _L2_attn_all.items() if k in ('w_in', 'w_out')}
    del _L2_attn_all

    def _L2_xattn_setup():
        import jax, jax.numpy as jnp
        import numpy as np
        B, C_LEN, Q_LEN, D = (8, 256, 64, 128)
        key = jax.random.key(seed)
        ks = jax.random.split(key, 10)
        scale = 1.0 / np.sqrt(D)
        return {'c': jax.random.normal(ks[0], (B, C_LEN, D), dtype=jnp.float32), 'q': jax.random.normal(ks[1], (B, Q_LEN, D), dtype=jnp.float32), 'w_cq': jax.random.normal(ks[2], (D,), dtype=jnp.float32) * scale, 'b_cq': jax.random.normal(ks[3], (), dtype=jnp.float32) * scale, 'w_c': jax.random.normal(ks[4], (D,), dtype=jnp.float32) * scale, 'b_c': jax.random.normal(ks[5], (), dtype=jnp.float32) * scale, 'w_q': jax.random.normal(ks[6], (D,), dtype=jnp.float32) * scale, 'b_q': jax.random.normal(ks[7], (), dtype=jnp.float32) * scale, 'W_l': jax.random.normal(ks[8], (D, 4 * D), dtype=jnp.float32) * (1.0 / np.sqrt(4 * D)), 'b_l': jax.random.normal(ks[9], (D,), dtype=jnp.float32) * (1.0 / np.sqrt(4 * D))}
    _L2_xattn_all = _L2_xattn_setup()
    _L2_xattn_in = {k: v for k, v in _L2_xattn_all.items() if k in ('w_cq', 'b_cq', 'w_c', 'b_c', 'w_q', 'b_q', 'W_l', 'b_l')}
    del _L2_xattn_all

    def _L2_ffn_setup():
        import jax, jax.numpy as jnp
        import numpy as np
        N_HEAD, N_ACTIVE, D_MODEL, D_ATTN = (16, 4, 128, 64)
        key = jax.random.key(seed)
        ks = jax.random.split(key, 12)
        s = 0.02
        B, S = (2, 512)
        return {'x': jax.random.normal(ks[0], (B, S, D_MODEL), dtype=jnp.float32), 'Wq': jax.random.normal(ks[1], (D_MODEL, N_HEAD * D_ATTN), dtype=jnp.float32) * s, 'bq': jnp.zeros((N_HEAD * D_ATTN,), dtype=jnp.float32), 'Wk': jax.random.normal(ks[2], (D_MODEL, N_HEAD * D_ATTN), dtype=jnp.float32) * s, 'bk': jnp.zeros((N_HEAD * D_ATTN,), dtype=jnp.float32), 'Wv': jax.random.normal(ks[3], (D_MODEL, N_HEAD * D_ATTN), dtype=jnp.float32) * s, 'bv': jnp.zeros((N_HEAD * D_ATTN,), dtype=jnp.float32), 'Wr': jax.random.normal(ks[4], (D_MODEL, N_HEAD), dtype=jnp.float32) * s, 'br': jnp.zeros((N_HEAD,), dtype=jnp.float32), 'Wo': jax.random.normal(ks[5], (N_ACTIVE * D_ATTN, D_MODEL), dtype=jnp.float32) * s, 'bo': jnp.zeros((D_MODEL,), dtype=jnp.float32)}
    _L2_ffn_all = _L2_ffn_setup()
    _L2_ffn_in = {k: v for k, v in _L2_ffn_all.items() if k in ('Wq', 'bq', 'Wk', 'bk', 'Wv', 'bv', 'Wr', 'br', 'Wo', 'bo')}
    del _L2_ffn_all

    def _L3_attn_setup():
        import jax, jax.numpy as jnp
        import numpy as np
        N_HEADS = 16
        HEAD_DIM = 64
        HIDDEN = 128
        key = jax.random.key(seed)
        kx, kq, kk, kv, ko = jax.random.split(key, 5)
        B, S = (1, 512)
        lim = float(np.sqrt(6.0 / (HIDDEN + N_HEADS * HEAD_DIM)))
        x = jax.random.normal(kx, (B, S, HIDDEN), dtype=jnp.float32)
        wq = jax.random.uniform(kq, (N_HEADS * HEAD_DIM, HIDDEN), jnp.float32, -lim, lim)
        wk = jax.random.uniform(kk, (N_HEADS * HEAD_DIM, HIDDEN), jnp.float32, -lim, lim)
        wv = jax.random.uniform(kv, (N_HEADS * HEAD_DIM, HIDDEN), jnp.float32, -lim, lim)
        wo = jax.random.uniform(ko, (HIDDEN, N_HEADS * HEAD_DIM), jnp.float32, -lim, lim)
        return {'x': x, 'wq': wq, 'wk': wk, 'wv': wv, 'wo': wo}
    _L3_attn_all = _L3_attn_setup()
    _L3_attn_in = {k: v for k, v in _L3_attn_all.items() if k in ('wq', 'wk', 'wv', 'wo')}
    del _L3_attn_all

    def _L3_xattn_setup():
        import jax, jax.numpy as jnp
        import numpy as np
        B, NT, NM, C, H, FF = (8, 128, 256, 128, 8, 512)

        def _ln(x, g, b):
            m = x.mean(-1, keepdims=True)
            v = jnp.mean((x - m) ** 2, axis=-1, keepdims=True)
            return (x - m) / jnp.sqrt(v + 1e-05) * g + b
        key = jax.random.key(seed)
        ks = jax.random.split(key, 8)
        w = lambda k, shape, s=0.02: jax.random.normal(k, shape, dtype=jnp.float32) * s
        return {'tgt': jax.random.normal(ks[0], (B, NT, C), dtype=jnp.float32), 'memory': jax.random.normal(ks[1], (B, NM, C), dtype=jnp.float32), 'qkv_w': w(ks[2], (3 * C, C)), 'qkv_b': jnp.zeros((3 * C,), jnp.float32), 'sa_out_w': w(ks[3], (C, C)), 'sa_out_b': jnp.zeros((C,), jnp.float32), 'in_proj_w': w(ks[4], (3 * C, C)), 'in_proj_b': jnp.zeros((3 * C,), jnp.float32), 'mha_out_w': w(ks[5], (C, C)), 'mha_out_b': jnp.zeros((C,), jnp.float32), 'lin1_w': w(ks[6], (FF, C)), 'lin1_b': jnp.zeros((FF,), jnp.float32), 'lin2_w': w(ks[7], (C, FF)), 'lin2_b': jnp.zeros((C,), jnp.float32), 'ln1_g': jnp.ones((C,), jnp.float32), 'ln1_b': jnp.zeros((C,), jnp.float32), 'ln2_g': jnp.ones((C,), jnp.float32), 'ln2_b': jnp.zeros((C,), jnp.float32), 'ln3_g': jnp.ones((C,), jnp.float32), 'ln3_b': jnp.zeros((C,), jnp.float32)}
    _L3_xattn_all = _L3_xattn_setup()
    _L3_xattn_in = {k: v for k, v in _L3_xattn_all.items() if k in ('qkv_w', 'qkv_b', 'sa_out_w', 'sa_out_b', 'in_proj_w', 'in_proj_b', 'mha_out_w', 'mha_out_b', 'lin1_w', 'lin1_b', 'lin2_w', 'lin2_b', 'ln1_g', 'ln1_b', 'ln2_g', 'ln2_b', 'ln3_g', 'ln3_b')}
    del _L3_xattn_all

    def _L3_ffn_setup():
        import jax, jax.numpy as jnp
        import numpy as np

        def _bitlinear(x, w_latent):
            scale = jax.lax.stop_gradient(jnp.clip(jnp.mean(jnp.abs(w_latent), axis=1, keepdims=True), 1e-05, None))
            tern = jnp.clip(jnp.round(w_latent / scale), -1.0, 1.0)
            w = w_latent + jax.lax.stop_gradient(tern - w_latent)
            return x @ (w * scale).T
        key = jax.random.key(seed)
        ks = jax.random.split(key, 6)
        dim, hidden, rank = (128, 512, 16)
        B, S = (4, 512)
        x = jax.random.normal(ks[0], (B, S, dim), dtype=jnp.float32)
        w_fc = 0.02 * jax.random.normal(ks[1], (hidden, dim), dtype=jnp.float32)
        w_proj = 0.02 * jax.random.normal(ks[2], (dim, hidden), dtype=jnp.float32)
        u = 0.02 * jax.random.normal(ks[3], (hidden, rank), dtype=jnp.float32)
        v = 0.02 * jax.random.normal(ks[4], (rank, dim), dtype=jnp.float32)
        fast_b = jax.random.normal(ks[5], (rank, rank), dtype=jnp.float32)
        gate = jnp.float32(0.05)
        return {'x': x, 'fast_b': fast_b, 'w_fc': w_fc, 'w_proj': w_proj, 'u': u, 'v': v, 'gate': gate}
    _L3_ffn_all = _L3_ffn_setup()
    _L3_ffn_in = {k: v for k, v in _L3_ffn_all.items() if k in ('fast_b', 'w_fc', 'w_proj', 'u', 'v', 'gate')}
    del _L3_ffn_all
    return {'x': x, 'ctx_1024': ctx_1024, 'mask_Bx1xSxS2_bk1': mask_Bx1xSxS2_bk1, 'L0_attn_W_Q': _L0_attn_in['W_Q'], 'L0_attn_b_Q': _L0_attn_in['b_Q'], 'L0_attn_W_K': _L0_attn_in['W_K'], 'L0_attn_b_K': _L0_attn_in['b_K'], 'L0_attn_W_V': _L0_attn_in['W_V'], 'L0_attn_b_V': _L0_attn_in['b_V'], 'L0_attn_W_O': _L0_attn_in['W_O'], 'L0_attn_b_O': _L0_attn_in['b_O'], 'L0_attn_ln1_w': _L0_attn_in['ln1_w'], 'L0_attn_ln1_b': _L0_attn_in['ln1_b'], 'L0_attn_ln2_w': _L0_attn_in['ln2_w'], 'L0_attn_ln2_b': _L0_attn_in['ln2_b'], 'L0_xattn_Wq': _L0_xattn_in['Wq'], 'L0_xattn_Wo': _L0_xattn_in['Wo'], 'L0_ffn_w1': _L0_ffn_in['w1'], 'L0_ffn_w2': _L0_ffn_in['w2'], 'L0_ffn_router_w': _L0_ffn_in['router_w'], 'L1_attn_Wq': _L1_attn_in['Wq'], 'L1_attn_Wkv': _L1_attn_in['Wkv'], 'L1_attn_Wo': _L1_attn_in['Wo'], 'L1_attn_bo': _L1_attn_in['bo'], 'L1_xattn_Wq': _L1_xattn_in['Wq'], 'L1_xattn_bq': _L1_xattn_in['bq'], 'L1_xattn_Wk': _L1_xattn_in['Wk'], 'L1_xattn_bk': _L1_xattn_in['bk'], 'L1_xattn_Wv': _L1_xattn_in['Wv'], 'L1_xattn_bv': _L1_xattn_in['bv'], 'L1_xattn_Wo': _L1_xattn_in['Wo'], 'L1_xattn_bo': _L1_xattn_in['bo'], 'L1_ffn_shared_w1': _L1_ffn_in['shared_w1'], 'L1_ffn_shared_b1': _L1_ffn_in['shared_b1'], 'L1_ffn_shared_w2': _L1_ffn_in['shared_w2'], 'L1_ffn_shared_b2': _L1_ffn_in['shared_b2'], 'L1_ffn_router_w': _L1_ffn_in['router_w'], 'L1_ffn_router_b': _L1_ffn_in['router_b'], 'L1_ffn_spec_w1': _L1_ffn_in['spec_w1'], 'L1_ffn_spec_b1': _L1_ffn_in['spec_b1'], 'L1_ffn_spec_w2': _L1_ffn_in['spec_w2'], 'L1_ffn_spec_b2': _L1_ffn_in['spec_b2'], 'L2_attn_w_in': _L2_attn_in['w_in'], 'L2_attn_w_out': _L2_attn_in['w_out'], 'L2_xattn_w_cq': _L2_xattn_in['w_cq'], 'L2_xattn_b_cq': _L2_xattn_in['b_cq'], 'L2_xattn_w_c': _L2_xattn_in['w_c'], 'L2_xattn_b_c': _L2_xattn_in['b_c'], 'L2_xattn_w_q': _L2_xattn_in['w_q'], 'L2_xattn_b_q': _L2_xattn_in['b_q'], 'L2_xattn_W_l': _L2_xattn_in['W_l'], 'L2_xattn_b_l': _L2_xattn_in['b_l'], 'L2_ffn_Wq': _L2_ffn_in['Wq'], 'L2_ffn_bq': _L2_ffn_in['bq'], 'L2_ffn_Wk': _L2_ffn_in['Wk'], 'L2_ffn_bk': _L2_ffn_in['bk'], 'L2_ffn_Wv': _L2_ffn_in['Wv'], 'L2_ffn_bv': _L2_ffn_in['bv'], 'L2_ffn_Wr': _L2_ffn_in['Wr'], 'L2_ffn_br': _L2_ffn_in['br'], 'L2_ffn_Wo': _L2_ffn_in['Wo'], 'L2_ffn_bo': _L2_ffn_in['bo'], 'L3_attn_wq': _L3_attn_in['wq'], 'L3_attn_wk': _L3_attn_in['wk'], 'L3_attn_wv': _L3_attn_in['wv'], 'L3_attn_wo': _L3_attn_in['wo'], 'L3_xattn_qkv_w': _L3_xattn_in['qkv_w'], 'L3_xattn_qkv_b': _L3_xattn_in['qkv_b'], 'L3_xattn_sa_out_w': _L3_xattn_in['sa_out_w'], 'L3_xattn_sa_out_b': _L3_xattn_in['sa_out_b'], 'L3_xattn_in_proj_w': _L3_xattn_in['in_proj_w'], 'L3_xattn_in_proj_b': _L3_xattn_in['in_proj_b'], 'L3_xattn_mha_out_w': _L3_xattn_in['mha_out_w'], 'L3_xattn_mha_out_b': _L3_xattn_in['mha_out_b'], 'L3_xattn_lin1_w': _L3_xattn_in['lin1_w'], 'L3_xattn_lin1_b': _L3_xattn_in['lin1_b'], 'L3_xattn_lin2_w': _L3_xattn_in['lin2_w'], 'L3_xattn_lin2_b': _L3_xattn_in['lin2_b'], 'L3_xattn_ln1_g': _L3_xattn_in['ln1_g'], 'L3_xattn_ln1_b': _L3_xattn_in['ln1_b'], 'L3_xattn_ln2_g': _L3_xattn_in['ln2_g'], 'L3_xattn_ln2_b': _L3_xattn_in['ln2_b'], 'L3_xattn_ln3_g': _L3_xattn_in['ln3_g'], 'L3_xattn_ln3_b': _L3_xattn_in['ln3_b'], 'L3_ffn_fast_b': _L3_ffn_in['fast_b'], 'L3_ffn_w_fc': _L3_ffn_in['w_fc'], 'L3_ffn_w_proj': _L3_ffn_in['w_proj'], 'L3_ffn_u': _L3_ffn_in['u'], 'L3_ffn_v': _L3_ffn_in['v'], 'L3_ffn_gate': _L3_ffn_in['gate']}

def reference(x, ctx_1024, mask_Bx1xSxS2_bk1, L0_attn_W_Q, L0_attn_b_Q, L0_attn_W_K, L0_attn_b_K, L0_attn_W_V, L0_attn_b_V, L0_attn_W_O, L0_attn_b_O, L0_attn_ln1_w, L0_attn_ln1_b, L0_attn_ln2_w, L0_attn_ln2_b, L0_xattn_Wq, L0_xattn_Wo, L0_ffn_w1, L0_ffn_w2, L0_ffn_router_w, L1_attn_Wq, L1_attn_Wkv, L1_attn_Wo, L1_attn_bo, L1_xattn_Wq, L1_xattn_bq, L1_xattn_Wk, L1_xattn_bk, L1_xattn_Wv, L1_xattn_bv, L1_xattn_Wo, L1_xattn_bo, L1_ffn_shared_w1, L1_ffn_shared_b1, L1_ffn_shared_w2, L1_ffn_shared_b2, L1_ffn_router_w, L1_ffn_router_b, L1_ffn_spec_w1, L1_ffn_spec_b1, L1_ffn_spec_w2, L1_ffn_spec_b2, L2_attn_w_in, L2_attn_w_out, L2_xattn_w_cq, L2_xattn_b_cq, L2_xattn_w_c, L2_xattn_b_c, L2_xattn_w_q, L2_xattn_b_q, L2_xattn_W_l, L2_xattn_b_l, L2_ffn_Wq, L2_ffn_bq, L2_ffn_Wk, L2_ffn_bk, L2_ffn_Wv, L2_ffn_bv, L2_ffn_Wr, L2_ffn_br, L2_ffn_Wo, L2_ffn_bo, L3_attn_wq, L3_attn_wk, L3_attn_wv, L3_attn_wo, L3_xattn_qkv_w, L3_xattn_qkv_b, L3_xattn_sa_out_w, L3_xattn_sa_out_b, L3_xattn_in_proj_w, L3_xattn_in_proj_b, L3_xattn_mha_out_w, L3_xattn_mha_out_b, L3_xattn_lin1_w, L3_xattn_lin1_b, L3_xattn_lin2_w, L3_xattn_lin2_b, L3_xattn_ln1_g, L3_xattn_ln1_b, L3_xattn_ln2_g, L3_xattn_ln2_b, L3_xattn_ln3_g, L3_xattn_ln3_b, L3_ffn_fast_b, L3_ffn_w_fc, L3_ffn_w_proj, L3_ffn_u, L3_ffn_v, L3_ffn_gate):
    import jax
    import jax.numpy as jnp

    def _L0_attn_ref(resid_pre, W_Q, b_Q, W_K, b_K, W_V, b_V, W_O, b_O, ln1_w, ln1_b, ln2_w, ln2_b):
        import jax, jax.numpy as jnp
        import numpy as np
        LN_EPS = 1e-05
        D_HEAD = 64

        def _layernorm(x, w, b):
            x = x - jnp.mean(x, axis=-1, keepdims=True)
            scale = jnp.sqrt(jnp.mean(x * x, axis=-1, keepdims=True) + LN_EPS)
            return x / scale * w + b
        x = _layernorm(resid_pre, ln1_w, ln1_b)
        q = jnp.einsum('hdk,bsd->bshk', W_Q, x) + b_Q
        k = jnp.einsum('hdk,bsd->bshk', W_K, x) + b_K
        v = jnp.einsum('hdk,bsd->bshk', W_V, x) + b_V
        scores = jnp.einsum('bqhk,bphk->bhqp', q, k) / jnp.sqrt(jnp.asarray(D_HEAD, dtype=q.dtype))
        S = scores.shape[-1]
        causal = jnp.tril(jnp.ones((S, S), dtype=bool))
        scores = jnp.where(causal, scores, jnp.asarray(0.0, dtype=scores.dtype))
        pattern = jax.nn.softmax(scores, axis=-1)
        z = jnp.einsum('bhqp,bphk->bqhk', pattern, v)
        attn_out = jnp.einsum('bqhk,hkd->bqd', z, W_O) + b_O
        resid_mid = resid_pre + attn_out
        resid_post = resid_mid + _layernorm(resid_mid, ln2_w, ln2_b)
        return resid_post

    def _L0_xattn_ref(q, k, v, Wq, Wo):
        import jax, jax.numpy as jnp
        import numpy as np
        N_HEADS = 16

        def _split(x, n_heads):
            b, s, d = x.shape
            return x.reshape(b, s, n_heads, d // n_heads).transpose(0, 2, 1, 3)
        d_model = q.shape[-1]
        d_k = d_model // N_HEADS
        Q = _split(q @ Wq.T, N_HEADS)
        K = _split(k @ Wq.T, N_HEADS)
        V = _split(v @ Wq.T, N_HEADS)
        scores = jnp.einsum('bhqd,bhkd->bhqk', Q, K) / jnp.sqrt(jnp.asarray(d_k, Q.dtype))
        attn = jax.nn.softmax(scores, axis=-1)
        out = jnp.einsum('bhqk,bhkd->bhqd', attn, V)
        b, h, s, dk = out.shape
        out = out.transpose(0, 2, 1, 3).reshape(b, s, h * dk)
        return out @ Wo.T

    def _L0_ffn_ref(hidden_states, w1, w2, router_w):
        import jax, jax.numpy as jnp
        import numpy as np
        TOPK = 2
        orig_shape = hidden_states.shape
        H = orig_shape[-1]
        E = w1.shape[0]
        I = w2.shape[-1]
        dtype = hidden_states.dtype
        x = hidden_states.reshape(-1, H)
        gating = x @ router_w.T
        probs = jax.nn.softmax(gating.astype(jnp.float32), axis=-1)
        topk_weights, selected_experts = jax.lax.top_k(probs, TOPK)
        topk_weights = topk_weights.astype(dtype)
        out = jnp.zeros_like(x)
        for e in range(E):
            ew = jnp.sum(topk_weights * (selected_experts == e), axis=-1, keepdims=True)
            h = x @ w1[e].T
            gate = jax.nn.silu(h[:, :I])
            y = h[:, I:] * gate @ w2[e].T
            out = out + y * ew
        return out.reshape(orig_shape)

    def _L1_attn_ref(hidden_states, Wq, Wkv, Wo, bo):
        import jax, jax.numpy as jnp
        import numpy as np
        from functools import partial
        B, S, D = (8, 256, 128)
        HEADS, DIM_HEAD = (16, 64)
        MAX_ALLOWABLE = 128 * 128 * 8

        def _max_pow2_divides(n):
            i = 1
            while n % 2 == 0:
                i *= 2
                n //= 2
            return i

        def _n_splits(bh, sq, sk):
            dimprod = bh * sq * sk
            true_divisor = dimprod / MAX_ALLOWABLE
            if true_divisor < 1:
                return 1
            if true_divisor >= bh:
                return bh
            nearest_pow2 = 2 ** np.round(np.log2(true_divisor))
            return int(min(_max_pow2_divides(bh), nearest_pow2))

        def _sdp_attention(q, k, v, scale):
            scores = jnp.einsum('bid,bjd->bij', q, k) * scale
            probs = jax.nn.softmax(scores, axis=2)
            return jnp.einsum('bij,bjd->bid', probs, v)

        def _scan_attention(q, k, v, scale, n_splits):
            bh = q.shape[0]
            nq, nk, nv = [h.reshape(n_splits, bh // n_splits, h.shape[-2], h.shape[-1]) for h in (q, k, v)]

            def body(carry, args):
                cq, ck, cv = args
                return (None, _sdp_attention(cq, ck, cv, scale))
            outs = jax.lax.scan(body, None, (nq, nk, nv))[1]
            return outs.reshape(-1, outs.shape[-2], outs.shape[-1])

        def _heads_to_batch(t, heads):
            b, s, d = t.shape
            return t.reshape(b, s, heads, d // heads).transpose(0, 2, 1, 3).reshape(b * heads, s, d // heads)

        def _batch_to_heads(t, heads):
            bh, s, d = t.shape
            return t.reshape(bh // heads, heads, s, d).transpose(0, 2, 1, 3).reshape(bh // heads, s, d * heads)
        scale = DIM_HEAD ** (-0.5)
        q = hidden_states @ Wq
        kv = hidden_states @ Wkv
        k, v = jnp.split(kv, 2, axis=-1)
        q = _heads_to_batch(q, HEADS)
        k = _heads_to_batch(k, HEADS)
        v = _heads_to_batch(v, HEADS)
        n_splits = _n_splits(q.shape[0], q.shape[1], k.shape[1])
        out = _scan_attention(q, k, v, scale, n_splits)
        out = _batch_to_heads(out, HEADS)
        return out @ Wo + bo

    def _L1_xattn_ref(queries, keys, values, mask, Wq, bq, Wk, bk, Wv, bv, Wo, bo):
        import jax, jax.numpy as jnp
        import numpy as np
        B, S, D, H = (4, 256, 128, 16)
        HD = D // H
        b, sq, d = queries.shape

        def split_heads(x):
            return x.reshape(b, x.shape[1], H, HD).transpose(0, 2, 1, 3)
        q = split_heads(queries @ Wq + bq)
        k = split_heads(keys @ Wk + bk)
        v = split_heads(values @ Wv + bv)
        scores = jnp.einsum('bhqd,bhkd->bhqk', q, k) / jnp.sqrt(jnp.float32(HD))
        scores = jnp.where(mask, jnp.float32(-1000000000000000.0), scores)
        attn = jax.nn.softmax(scores, axis=-1)
        ctx = jnp.einsum('bhqk,bhkd->bhqd', attn, v)
        ctx = ctx.transpose(0, 2, 1, 3).reshape(b, sq, d)
        return ctx @ Wo + bo

    def _L1_ffn_ref(x, shared_w1, shared_b1, shared_w2, shared_b2, router_w, router_b, spec_w1, spec_b1, spec_w2, spec_b2):
        import jax, jax.numpy as jnp
        import numpy as np
        D_MODEL = 128
        D_FF = 512
        N_EXPERTS = 8
        TOP_K = 2

        def _ffn(x, w1, b1, w2, b2):
            h = jax.nn.gelu(x @ w1.T + b1)
            return h @ w2.T + b2
        B, T, D = x.shape
        xf = x.reshape(-1, D)
        U = xf.shape[0]
        logits = xf @ router_w.T + router_b
        routing = jax.nn.softmax(logits, axis=-1)
        sel_w, sel_idx = jax.lax.top_k(routing, TOP_K)
        sel_w = sel_w / sel_w.sum(axis=-1, keepdims=True)
        comb = jnp.zeros_like(routing).at[jnp.arange(U)[:, None], sel_idx].set(sel_w)
        shared_out = _ffn(xf, shared_w1, shared_b1, shared_w2, shared_b2)

        def body(acc, params):
            w1, b1, w2, b2, we = params
            return (acc + we[:, None] * _ffn(xf, w1, b1, w2, b2), None)
        acc0 = jnp.zeros_like(shared_out)
        acc, _ = jax.lax.scan(body, acc0, (spec_w1, spec_b1, spec_w2, spec_b2, comb.T))
        return (shared_out + acc).reshape(B, T, D)

    def _L2_attn_ref(x, w_in, w_out):
        import jax, jax.numpy as jnp
        import numpy as np
        NUM_HEADS = 16
        N_EMBD = 128

        def alibi_bias(num_heads: int, seq_len: int) -> jnp.ndarray:
            pos = jnp.arange(seq_len, dtype=jnp.float32)
            dgrid = pos[None, :] - pos[:, None]
            slopes = 2.0 ** (-8.0 / num_heads * (jnp.arange(num_heads, dtype=jnp.float32) + 1.0))
            bias = slopes[:, None, None] * dgrid[None, :, :]
            return jnp.where(dgrid[None, :, :] > 0, -jnp.inf, bias)
        B, L, E = x.shape
        H = NUM_HEADS
        D = E // H
        qkv = jnp.einsum('ble,fe->blf', x, w_in)
        q, k, v = jnp.split(qkv, 3, axis=-1)

        def to_heads(t):
            return t.reshape(B, L, H, D).transpose(0, 2, 1, 3)
        q, k, v = (to_heads(q), to_heads(k), to_heads(v))
        scale = 1.0 / jnp.sqrt(jnp.asarray(D, dtype=x.dtype))
        scores = jnp.einsum('bhqd,bhkd->bhqk', q, k) * scale
        scores = scores + alibi_bias(H, L)[None]
        attn = jax.nn.softmax(scores, axis=-1)
        ctx = jnp.einsum('bhqk,bhkd->bhqd', attn, v)
        ctx = ctx.transpose(0, 2, 1, 3).reshape(B, L, E)
        return jnp.einsum('ble,fe->blf', ctx, w_out)

    def _L2_xattn_ref(c, q, w_cq, b_cq, w_c, b_c, w_q, b_q, W_l, b_l):
        import jax, jax.numpy as jnp
        import numpy as np
        B, C_LEN, Q_LEN, D = (8, 256, 64, 128)
        cq = jnp.einsum('bcd,bqd,d->bcq', c, q, w_cq) + b_cq
        s = (c @ w_c + b_c)[:, :, None] + (q @ w_q + b_q)[:, None, :] + cq
        a = jax.nn.softmax(s, axis=2)
        c2q_att = jnp.einsum('bcq,bqd->bcd', a, q)
        b_att = jax.nn.softmax(jnp.max(s, axis=2), axis=1)
        q2c_att = jnp.einsum('bc,bcd->bd', b_att, c)[:, None, :]
        x = jnp.concatenate([c, c2q_att, c * c2q_att, c * q2c_att], axis=-1)
        z = x @ W_l.T + b_l
        return z

    def _L2_ffn_ref(x, Wq, bq, Wk, bk, Wv, bv, Wr, br, Wo, bo):
        import jax, jax.numpy as jnp
        import numpy as np
        N_HEAD, N_ACTIVE, D_MODEL, D_ATTN = (16, 4, 128, 64)
        B, S, D = x.shape
        H, K, dh = (N_HEAD, N_ACTIVE, D_ATTN)
        dist = jax.nn.softmax(jnp.mean(x @ Wr + br, axis=1), axis=-1)
        top_vals, top_idx = jax.lax.top_k(dist, K)
        sparse = jnp.zeros_like(dist).at[jnp.arange(B)[:, None], top_idx].set(top_vals)
        gates_all = jax.nn.softmax(sparse, axis=1)
        g = jnp.take_along_axis(gates_all, top_idx, axis=1)[:, :, None, None]

        def proj(W, b):
            return (x @ W + b).reshape(B, S, H, dh).transpose(0, 2, 1, 3)
        Q, Kt, V = (proj(Wq, bq), proj(Wk, bk), proj(Wv, bv))
        idx = top_idx[:, :, None, None]
        Qk = jnp.take_along_axis(Q, idx, axis=1) * g
        Kk = jnp.take_along_axis(Kt, idx, axis=1) * g
        Vk = jnp.take_along_axis(V, idx, axis=1) * g
        scores = jnp.einsum('bksd,bktd->bkst', Qk, Kk) / jnp.sqrt(jnp.float32(dh))
        attn = jax.nn.softmax(scores, axis=-1)
        out = jnp.einsum('bkst,bktd->bksd', attn, Vk)
        out = out.transpose(0, 2, 1, 3).reshape(B, S, K * dh)
        return out @ Wo + bo

    def _L3_attn_ref(x, wq, wk, wv, wo):
        import jax, jax.numpy as jnp
        import numpy as np
        N_HEADS = 16
        HEAD_DIM = 64
        HIDDEN = 128
        B, S, _ = x.shape
        scale = HEAD_DIM ** (-0.5)

        def proj(w):
            return jnp.einsum('bsh,eh->bse', x, w).reshape(B, S, N_HEADS, HEAD_DIM).transpose(0, 2, 1, 3)
        q, k, v = (proj(wq), proj(wk), proj(wv))
        scores = jnp.einsum('bhqd,bhkd->bhqk', q, k) * scale
        causal = jnp.tril(jnp.ones((S, S), dtype=bool))
        scores = jnp.where(causal, scores, -jnp.inf)
        probs = jax.nn.softmax(scores, axis=-1)
        out = jnp.einsum('bhqk,bhkd->bhqd', probs, v)
        out = out.transpose(0, 2, 1, 3).reshape(B, S, N_HEADS * HEAD_DIM)
        return jnp.einsum('bse,he->bsh', out, wo)

    def _L3_xattn_ref(tgt, memory, qkv_w, qkv_b, sa_out_w, sa_out_b, in_proj_w, in_proj_b, mha_out_w, mha_out_b, lin1_w, lin1_b, lin2_w, lin2_b, ln1_g, ln1_b, ln2_g, ln2_b, ln3_g, ln3_b):
        import jax, jax.numpy as jnp
        import numpy as np
        B, NT, NM, C, H, FF = (8, 128, 256, 128, 8, 512)

        def _ln(x, g, b):
            m = x.mean(-1, keepdims=True)
            v = jnp.mean((x - m) ** 2, axis=-1, keepdims=True)
            return (x - m) / jnp.sqrt(v + 1e-05) * g + b
        Bx, N, Cx = tgt.shape
        qkv = tgt @ qkv_w.T + qkv_b
        q, k, v = jnp.split(qkv, 3, axis=-1)
        scores = jnp.einsum('bnc,bmc->bnm', q, k) * jnp.sqrt(jnp.float32(Cx))
        diag = jnp.eye(N, dtype=bool)
        scores = jnp.where(diag[None, :, :], scores, -jnp.inf)
        attn = jax.nn.softmax(scores, axis=-1)
        sa = jnp.einsum('bnm,bmc->bnc', attn, v) @ sa_out_w.T + sa_out_b
        x = _ln(tgt + sa, ln1_g, ln1_b)
        d = Cx // H
        wq, wk, wv = jnp.split(in_proj_w, 3, axis=0)
        bq, bk, bv = jnp.split(in_proj_b, 3, axis=0)
        qh = (x @ wq.T + bq).reshape(Bx, N, H, d).transpose(0, 2, 1, 3)
        kh = (memory @ wk.T + bk).reshape(Bx, -1, H, d).transpose(0, 2, 1, 3)
        vh = (memory @ wv.T + bv).reshape(Bx, -1, H, d).transpose(0, 2, 1, 3)
        a = jax.nn.softmax(jnp.einsum('bhnd,bhmd->bhnm', qh, kh) / jnp.sqrt(jnp.float32(d)), axis=-1)
        ca = jnp.einsum('bhnm,bhmd->bhnd', a, vh).transpose(0, 2, 1, 3).reshape(Bx, N, Cx)
        ca = ca @ mha_out_w.T + mha_out_b
        x = _ln(x + ca, ln2_g, ln2_b)
        ff = jax.nn.relu(x @ lin1_w.T + lin1_b) @ lin2_w.T + lin2_b
        return _ln(x + ff, ln3_g, ln3_b)

    def _L3_ffn_ref(x, fast_b, w_fc, w_proj, u, v, gate):
        import jax, jax.numpy as jnp
        import numpy as np

        def _bitlinear(x, w_latent):
            scale = jax.lax.stop_gradient(jnp.clip(jnp.mean(jnp.abs(w_latent), axis=1, keepdims=True), 1e-05, None))
            tern = jnp.clip(jnp.round(w_latent / scale), -1.0, 1.0)
            w = w_latent + jax.lax.stop_gradient(tern - w_latent)
            return x @ (w * scale).T
        h = _bitlinear(x, w_fc) + gate * (x @ v.T @ fast_b.T @ u.T)
        r = jnp.maximum(h, 0.0)
        return _bitlinear(r * r, w_proj)
    x = x + _L0_attn_ref(_layernorm(x, axis=-1), L0_attn_W_Q, L0_attn_b_Q, L0_attn_W_K, L0_attn_b_K, L0_attn_W_V, L0_attn_b_V, L0_attn_W_O, L0_attn_b_O, L0_attn_ln1_w, L0_attn_ln1_b, L0_attn_ln2_w, L0_attn_ln2_b)
    x = x + _L0_xattn_ref(_layernorm(x, axis=-1), ctx_1024, ctx_1024, L0_xattn_Wq, L0_xattn_Wo)
    x = x + _L0_ffn_ref(_layernorm(x, axis=-1), L0_ffn_w1, L0_ffn_w2, L0_ffn_router_w)
    x = x + _L1_attn_ref(_layernorm(x, axis=-1), L1_attn_Wq, L1_attn_Wkv, L1_attn_Wo, L1_attn_bo)
    x = x + _L1_xattn_ref(_layernorm(x, axis=-1), ctx_1024, ctx_1024, mask_Bx1xSxS2_bk1, L1_xattn_Wq, L1_xattn_bq, L1_xattn_Wk, L1_xattn_bk, L1_xattn_Wv, L1_xattn_bv, L1_xattn_Wo, L1_xattn_bo)
    x = x + _L1_ffn_ref(_layernorm(x, axis=-1), L1_ffn_shared_w1, L1_ffn_shared_b1, L1_ffn_shared_w2, L1_ffn_shared_b2, L1_ffn_router_w, L1_ffn_router_b, L1_ffn_spec_w1, L1_ffn_spec_b1, L1_ffn_spec_w2, L1_ffn_spec_b2)
    x = x + _L2_attn_ref(_layernorm(x, axis=-1), L2_attn_w_in, L2_attn_w_out)
    x = x + _L2_xattn_ref(_layernorm(x, axis=-1), ctx_1024, L2_xattn_w_cq, L2_xattn_b_cq, L2_xattn_w_c, L2_xattn_b_c, L2_xattn_w_q, L2_xattn_b_q, L2_xattn_W_l, L2_xattn_b_l)
    x = x + _L2_ffn_ref(_layernorm(x, axis=-1), L2_ffn_Wq, L2_ffn_bq, L2_ffn_Wk, L2_ffn_bk, L2_ffn_Wv, L2_ffn_bv, L2_ffn_Wr, L2_ffn_br, L2_ffn_Wo, L2_ffn_bo)
    x = x + _L3_attn_ref(_layernorm(x, axis=-1), L3_attn_wq, L3_attn_wk, L3_attn_wv, L3_attn_wo)
    x = x + _L3_xattn_ref(_layernorm(x, axis=-1), ctx_1024, L3_xattn_qkv_w, L3_xattn_qkv_b, L3_xattn_sa_out_w, L3_xattn_sa_out_b, L3_xattn_in_proj_w, L3_xattn_in_proj_b, L3_xattn_mha_out_w, L3_xattn_mha_out_b, L3_xattn_lin1_w, L3_xattn_lin1_b, L3_xattn_lin2_w, L3_xattn_lin2_b, L3_xattn_ln1_g, L3_xattn_ln1_b, L3_xattn_ln2_g, L3_xattn_ln2_b, L3_xattn_ln3_g, L3_xattn_ln3_b)
    x = x + _L3_ffn_ref(_layernorm(x, axis=-1), L3_ffn_fast_b, L3_ffn_w_fc, L3_ffn_w_proj, L3_ffn_u, L3_ffn_v, L3_ffn_gate)
    return x

_drawn_inputs = setup_inputs


def setup_inputs(seed=0):
    import zlib

    import numpy as np

    out = dict(_drawn_inputs(seed))
    spreads = {'L0_attn_b_Q': (0.0, 0.8),
     'L0_attn_b_K': (0.0, 0.8),
     'L0_attn_b_V': (0.0, 0.1),
     'L0_attn_b_O': (0.0, 0.1),
     'L0_attn_ln1_w': (1.0, 0.6),
     'L0_attn_ln1_b': (0.0, 0.8),
     'L0_attn_ln2_w': (1.0, 0.2),
     'L0_attn_ln2_b': (0.0, 0.1),
     'L1_attn_bo': (0.0, 0.267),
     'L1_xattn_bq': (0.0, 0.8),
     'L1_xattn_bk': (0.0, 2.0),
     'L1_xattn_bv': (0.0, 0.1),
     'L1_xattn_bo': (0.0, 0.1),
     'L1_ffn_shared_b1': (0.0, 0.8),
     'L1_ffn_shared_b2': (0.0, 0.1),
     'L1_ffn_router_b': (0.0, 0.442),
     'L1_ffn_spec_b1': (0.0, 0.8),
     'L1_ffn_spec_b2': (0.0, 0.356),
     'L2_ffn_bq': (0.0, 2.0),
     'L2_ffn_bk': (0.0, 2.0),
     'L2_ffn_bv': (0.0, 2.0),
     'L2_ffn_br': (0.0, 0.8),
     'L2_ffn_bo': (0.0, 0.27),
     'L3_xattn_qkv_b': (0.0, 0.8),
     'L3_xattn_sa_out_b': (0.0, 0.362),
     'L3_xattn_in_proj_b': (0.0, 0.8),
     'L3_xattn_mha_out_b': (0.0, 1.71),
     'L3_xattn_lin1_b': (0.0, 0.8),
     'L3_xattn_lin2_b': (0.0, 0.358),
     'L3_xattn_ln1_g': (1.0, 0.2),
     'L3_xattn_ln1_b': (0.0, 0.345),
     'L3_xattn_ln2_g': (1.0, 0.538),
     'L3_xattn_ln2_b': (0.0, 0.301),
     'L3_xattn_ln3_g': (1.0, 0.2),
     'L3_xattn_ln3_b': (0.0, 0.333)}
    factors = {'L0_attn_W_Q': 8.0,
     'L0_attn_W_K': 8.0,
     'L0_attn_W_V': 4.218,
     'L0_ffn_w1': 8.0,
     'L0_ffn_w2': 8.0,
     'L0_ffn_router_w': 8.0,
     'L1_ffn_shared_w1': 3.296,
     'L1_ffn_shared_w2': 2.947,
     'L1_ffn_spec_w1': 4.774,
     'L1_ffn_spec_w2': 4.28,
     'L2_attn_w_in': 8.0,
     'L2_attn_w_out': 8.0,
     'L2_xattn_b_l': 3.665,
     'L2_ffn_Wq': 200.0,
     'L2_ffn_Wk': 200.0,
     'L2_ffn_Wv': 8.0,
     'L2_ffn_Wr': 8.0,
     'L2_ffn_Wo': 8.0,
     'L3_attn_wq': 6.76,
     'L3_attn_wk': 6.681,
     'L3_xattn_qkv_w': 4.594,
     'L3_xattn_sa_out_w': 4.134,
     'L3_xattn_in_proj_w': 8.0,
     'L3_xattn_mha_out_w': 7.579,
     'L3_xattn_lin1_w': 3.919,
     'L3_xattn_lin2_w': 3.105,
     'L3_ffn_fast_b': 8.0,
     'L3_ffn_w_fc': 8.0,
     'L3_ffn_w_proj': 8.0,
     'L3_ffn_u': 8.0,
     'L3_ffn_v': 8.0,
     'L2_xattn_w_c': 3.177}
    for name, (base, spread) in spreads.items():
        noise = np.random.default_rng([zlib.crc32(name.encode()), seed]).standard_normal(out[name].shape)
        drawn = base * np.exp(spread * noise) if base else spread * noise
        out[name] = jnp.asarray(drawn.astype(out[name].dtype))
    for name, factor in factors.items():
        out[name] = (out[name] * factor).astype(out[name].dtype)
    return out
```

```python
from contextlib import ExitStack

import numpy as np
import concourse.bass as bass
from concourse import mybir
from concourse.alu_op_type import AluOpType as ALU

ACT = mybir.ActivationFunctionType
F32 = mybir.dt.float32
BF16 = mybir.dt.bfloat16
U8 = mybir.dt.uint8
AX = mybir.AxisListType

STAGES = range(0, 12)

B, S, D = 32, 100, 128
TOK = B * S
GB = 4
GT = GB * S
NG = B // GB
S2 = 1444
EPS = 1e-5
BANK = 512


class Stage:

    def __init__(self, nc, name):
        self.nc, self.name, self.ctx, self.sems = nc, name, ExitStack(), []

    def __enter__(self):
        return self

    def __exit__(self, *a):
        self.ctx.__exit__(*a)
        if self.sems and a[0] is None:
            self.nc.clear_and_free_semaphores(self.sems)
            self.nc.all_engine_barrier()
        return False

    def sb(self, name, shape, dt=F32):
        return self.ctx.enter_context(self.nc.sbuf_tensor(f"{self.name}_{name}", list(shape), dt))

    def ps(self, name, shape, dt=F32):
        return self.ctx.enter_context(self.nc.psum_tensor(f"{self.name}_ps_{name}", list(shape), dt))

    def sem(self, name):
        self.sems.append(self.nc.alloc_semaphore(f"{self.name}_{name}"))
        return self.sems[-1]


class Link:

    def __init__(self, eng, sem, per, i):
        self.eng, self.sem, self.per, self.i, self.c = eng, sem, per, i, 0

    def __call__(self, ins):
        self.c += 1
        ins.then_inc(self.sem, 1)
        self.eng.wait_ge(self.sem, self.i * self.per + self.c)

    def end(self):
        assert self.c == self.per, (self.c, self.per)


def after(eng, sem, n):
    if not (isinstance(n, int) and n <= 0):
        eng.wait_ge(sem, n)


def layer_norm(nc, name, G, src, dst, gain=None, shift=None, add_to=None):
    with Stage(nc, name) as st:
        mean = [st.ps(f"mean{j}", [128, BANK]) for j in range(2)]
        var = [st.ps(f"var{j}", [128, BANK]) for j in range(2)]
        square = [st.sb(f"square{j}", [128, GT]) for j in range(2)]
        std = [st.sb(f"std{j}", [128, GT]) for j in range(2)]
        mean_ready, centred, squared, var_ready, std_ready, inverted, normed = (
            st.sem(n) for n in ("mean_ready", "centred", "squared", "var_ready", "std_ready", "inverted", "normed"))
        n_out = 2 if gain is not None else 1
        block = st.ctx.enter_context(nc.Block())

        @block.tensor
        def _(pe):
            def pair(i):
                for j in range(2):
                    after(pe, centred, 2 * i + j)
                    nc.tensor.matmul(mean[j][:, 0:GT], G["mean_mat"][:, :], src[:, bass.ds((2 * i + j) * GT, GT)],
                                     start=True, stop=True).then_inc(mean_ready, 1)
                for j in range(2):
                    pe.wait_ge(squared, 2 * i + j + 1)
                    after(pe, std_ready, 2 * i + j)
                    nc.tensor.matmul(var[j][:, 0:GT], G["mean_mat"][:, :], square[j][:, :],
                                     start=True, stop=True).then_inc(var_ready, 1)

            pair(0)
            with pe.Fori(1, NG // 2) as i:
                pair(i)

        @block.scalar
        def _(act):
            def pair(i):
                for j in range(2):
                    act.wait_ge(centred, 2 * i + j + 1)
                    after(act, var_ready, 2 * i + j)
                    nc.scalar.activation(square[j][:, :], dst[:, bass.ds((2 * i + j) * GT, GT)],
                                         ACT.Square).then_inc(squared, 1)
                for j in range(2):
                    act.wait_ge(var_ready, 2 * i + j + 1)
                    after(act, normed, (2 * i + j) * n_out)
                    nc.scalar.activation(std[j][:, :], var[j][:, 0:GT], ACT.Sqrt, bias=G["eps"][:, :]).then_inc(std_ready, 1)

            pair(0)
            with act.Fori(1, NG // 2) as i:
                pair(i)

        @block.vector
        def _(dve):
            def pair(i):
                for j in range(2):
                    dve.wait_ge(mean_ready, 2 * i + j + 1)
                    nc.vector.tensor_tensor(dst[:, bass.ds((2 * i + j) * GT, GT)], src[:, bass.ds((2 * i + j) * GT, GT)],
                                            mean[j][:, 0:GT], ALU.subtract).then_inc(centred, 1)
                for j in range(2):
                    part = bass.ds((2 * i + j) * GT, GT)
                    dve.wait_ge(std_ready, 2 * i + j + 1)
                    nc.vector.reciprocal(std[j][:, :], std[j][:, :]).then_inc(inverted, 1)
                    dve.wait_ge(inverted, 2 * i + j + 1)
                    nc.vector.tensor_tensor(dst[:, part], dst[:, part], std[j][:, :], ALU.mult).then_inc(normed, 1)
                    if gain is not None:
                        dve.wait_ge(normed, (2 * i + j) * 2 + 1)
                        nc.vector.tensor_scalar(dst[:, part], dst[:, part], gain, shift, ALU.mult, ALU.add).then_inc(normed, 1)

            pair(0)
            with dve.Fori(1, NG // 2) as i:
                pair(i)


def top2_weights(nc, name, G, xn, router, router_b, n_shared, normalise, combT):
    E = 8
    EW = E + n_shared
    with Stage(nc, name) as st:
        w_sb = st.sb("router", [128, E])
        rb = st.sb("router_b", [S, E])
        logit_ps = st.ps("logit", [S, BANK])
        turn = [st.ps(f"turn{j}", [EW, BANK]) for j in range(2)]
        logit = st.sb("logits", [S, B, E])
        mx = st.sb("mx", [S, B])
        prob = st.sb("prob", [S, B, E])
        tot = st.sb("tot", [S, B])
        pair = st.sb("pair", [S, B, E, E])
        tie = st.sb("tie", [S, B, E, E])
        rank = st.sb("rank", [S, B, E])
        comb = st.sb("comb", [S, B, EW])
        earlier = st.sb("earlier", [S, E, E])
        loaded, logits_ready, dve_chain, shifted, exp_done, comb_ready, turned, stored = (
            st.sem(n) for n in ("loaded", "logits_ready", "dve_chain", "shifted", "exp_done", "comb_ready", "turned", "stored"))
        block = st.ctx.enter_context(nc.Block())

        @block.sync
        def _(sp):
            sp.dma_start(w_sb[:, :], router).then_inc(loaded, 16)
            sp.dma_start(earlier[:, :, :], G["earlier_dram"]).then_inc(loaded, 16)
            if router_b is not None:
                sp.dma_start(rb[:, :], router_b.partition_broadcast(S)).then_inc(loaded, 16)

        @block.tensor
        def _(pe):
            pe.wait_ge(loaded, 48 if router_b is not None else 32)
            for b in range(B):
                last = nc.tensor.matmul(logit_ps[:, b * E:(b + 1) * E], xn[:, b * S:(b + 1) * S], w_sb[:, :],
                                        start=True, stop=True)
            last.then_inc(logits_ready, 1)
            pe.wait_ge(comb_ready, 1)
            for g in range(NG):
                if g >= 2:
                    pe.wait_ge(stored, g - 1)
                for k in range(GB):
                    last = nc.tensor.transpose(turn[g % 2][:, k * S:(k + 1) * S], comb[:, g * GB + k, :],
                                               G["ident"][0:S, 0:S])
                last.then_inc(turned, 1)

        @block.scalar
        def _(act):
            act.wait_ge(shifted, 1)
            nc.scalar.activation(prob[:, :, :], logit[:, :, :], ACT.Exp).then_inc(exp_done, 1)
            for g in range(NG):
                act.wait_ge(turned, g + 1)
                nc.scalar.activation(combT[0:EW, g * GT:(g + 1) * GT], turn[g % 2][:, 0:GT], ACT.Copy).then_inc(stored, 1)

        @block.vector
        def _(dve):
            link = Link(dve, dve_chain, 11 + 1 + (router_b is not None) + n_shared + 2 * normalise, 0)
            link(nc.vector.memset(combT[:, :], 0.0))
            lp = logit_ps[:, 0:B * E].rearrange("p (b e) -> p b e", e=E)
            dve.wait_ge(logits_ready, 1)
            src = lp
            if router_b is not None:
                link(nc.vector.tensor_tensor(logit[:, :, :], lp, rb[:, :].unsqueeze(1).to_broadcast([S, B, E]), ALU.add))
                src = logit[:, :, :]
            link(nc.vector.tensor_reduce(mx[:, :], src, AX.X, ALU.max))
            nc.vector.tensor_tensor(logit[:, :, :], src, mx[:, :].unsqueeze(2).to_broadcast([S, B, E]),
                                    ALU.subtract).then_inc(shifted, 1)
            dve.wait_ge(exp_done, 1)
            link(nc.vector.tensor_reduce(tot[:, :], prob[:, :, :], AX.X, ALU.add))
            link(nc.vector.reciprocal(mx[:, :], tot[:, :]))
            link(nc.vector.tensor_tensor(prob[:, :, :], prob[:, :, :], mx[:, :].unsqueeze(2).to_broadcast([S, B, E]), ALU.mult))

            def other(b):
                return prob[:, b, :].unsqueeze(1).to_broadcast([S, E, E])

            def own(b):
                return prob[:, b, :].unsqueeze(2).to_broadcast([S, E, E])

            for b in range(B):
                a = nc.vector.tensor_tensor(pair[:, b, :, :], other(b), own(b), ALU.is_gt)
                c = nc.vector.tensor_tensor(tie[:, b, :, :], other(b), own(b), ALU.is_equal)
            link(c)
            link(nc.vector.tensor_tensor(tie[:, :, :, :].rearrange("p b e f -> p b (e f)"),
                                         tie[:, :, :, :].rearrange("p b e f -> p b (e f)"),
                                         earlier[:, :, :].rearrange("p e f -> p (e f)").unsqueeze(1).to_broadcast([S, B, E * E]),
                                         ALU.mult))
            link(nc.vector.tensor_tensor(pair[:, :, :, :], pair[:, :, :, :], tie[:, :, :, :], ALU.add))
            link(nc.vector.tensor_reduce(rank[:, :, :], pair[:, :, :, :], AX.X, ALU.add))
            link(nc.vector.tensor_scalar(rank[:, :, :], rank[:, :, :], 1.5, None, ALU.is_lt))
            link(nc.vector.tensor_tensor(comb[:, :, 0:E], rank[:, :, :], prob[:, :, :], ALU.mult))
            if normalise:
                link(nc.vector.tensor_reduce(tot[:, :], comb[:, :, 0:E], AX.X, ALU.add))
                link(nc.vector.reciprocal(mx[:, :], tot[:, :]))
                link(nc.vector.tensor_tensor(comb[:, :, 0:E], comb[:, :, 0:E], mx[:, :].unsqueeze(2).to_broadcast([S, B, E]), ALU.mult))
            else:
                link(nc.vector.tensor_copy(tot[:, :], mx[:, :]))
            if n_shared:
                link(nc.vector.memset(comb[:, :, E:EW], 1.0))
            nc.vector.tensor_copy(mx[:, :], tot[:, :]).then_inc(comb_ready, 1)
            link.end()


def experts_ffn(nc, name, G, xT, xn, combT, w1, w2, n_exp, n_hidden, gated, b1, b2):
    HC = n_hidden // 128
    UNITS = n_exp * HC
    cols = 2 * n_hidden if gated else n_hidden
    with Stage(nc, name) as st:
        w1_sb = st.sb("w1", [128, n_exp, cols])
        w2_sb = st.sb("w2", [128, n_exp, HC, D])
        b1_sb = st.sb("b1", [128, n_exp * HC])
        b2_sb = st.sb("b2", [128, D])
        pick = st.sb("pick", [128, n_exp, 128])
        gate_ps = [st.ps(f"gate{j}", [128, BANK]) for j in range(2)]
        up_ps = [st.ps(f"up{j}", [128, BANK]) for j in range(2)] if gated else None
        wt_ps = [st.ps(f"wt{j}", [128, BANK]) for j in range(2)]
        out_ps = st.ps("out", [128, BANK])
        acted = [st.sb(f"acted{j}", [128, GT]) for j in range(2)]
        prod = [st.sb(f"prod{j}", [128, GT]) for j in range(2)]
        hid = [st.sb(f"hid{j}", [128, GT]) for j in range(2)]
        loaded, hid_in, wt_ready, act_done, prod_done, hid_ready, hid_used, out_ready, out_added = (
            st.sem(n) for n in ("loaded", "hid_in", "wt_ready", "act_done", "prod_done", "hid_ready", "hid_used",
                                "out_ready", "out_added"))
        loads = [(w1_sb[:, :, :], w1), (w2_sb[:, :, :, :], w2), (pick[:, :, :], G["pick_dram"][:, 0:n_exp, :])]
        if b1 is not None:
            loads += [(b1_sb[:, :], b1), (b2_sb[0:n_exp, :], b2)]
        cleared = st.sem("cleared")
        block = st.ctx.enter_context(nc.Block())

        @block.sync
        def _(sp):
            sp.wait_ge(cleared, 1)
            for dst, src in loads:
                sp.dma_start(dst, src).then_inc(loaded, 16)

        @block.tensor
        def _(pe):
            pe.wait_ge(loaded, 16 * len(loads))
            def group(g):
                x = xn[:, bass.ds(g * GT, GT)]

                def project(u):
                    e, c = u // HC, u % HC
                    j = u % 2
                    if c == 0:
                        after(pe, hid_ready, g * UNITS + (e - 1) * HC if e >= 2 else g * UNITS)
                        nc.tensor.matmul(wt_ps[e % 2][:, 0:GT], pick[:, e, :], combT[:, bass.ds(g * GT, GT)],
                                         start=True, stop=True).then_inc(wt_ready, 1)
                    after(pe, act_done, g * UNITS + max(u - 1, 0))
                    m = nc.tensor.matmul(gate_ps[j][:, 0:GT], w1_sb[:, e, c * 128:(c + 1) * 128], x, start=True, stop=True)
                    if gated:
                        after(pe, prod_done, g * UNITS + max(u - 1, 0))
                        m = nc.tensor.matmul(up_ps[j][:, 0:GT], w1_sb[:, e, n_hidden + c * 128:n_hidden + (c + 1) * 128],
                                             x, start=True, stop=True)
                    m.then_inc(hid_in, 1)

                def reduce(u):
                    e, c = u // HC, u % HC
                    if u == 0:
                        after(pe, out_added, g)
                        if b2 is not None:
                            nc.tensor.matmul(out_ps[:, 0:GT], b2_sb[:, :], combT[:, bass.ds(g * GT, GT)], start=True, stop=False)
                    pe.wait_ge(hid_ready, g * UNITS + u + 1)
                    m = nc.tensor.matmul(out_ps[:, 0:GT], w2_sb[:, e, c, :], hid[u % 2][:, :],
                                         start=(u == 0 and b2 is None), stop=(u == UNITS - 1))
                    m.then_inc(hid_used, 1)

                project(0)
                for u in range(1, UNITS):
                    project(u)
                    reduce(u - 1)
                reduce(UNITS - 1)

            group(0)
            with pe.Fori(1, NG) as g:
                group(g)

        @block.scalar
        def _(act):
            act.wait_ge(loaded, 16 * len(loads))
            def group(g):
                for u in range(UNITS):
                    act.wait_ge(hid_in, g * UNITS + u + 1)
                    after(act, prod_done if gated else hid_ready, g * UNITS + max(u - 1, 0))
                    if gated:
                        i = nc.scalar.activation(acted[u % 2][:, :], gate_ps[u % 2][:, 0:GT], ACT.Silu)
                    else:
                        i = nc.scalar.activation(acted[u % 2][:, :], gate_ps[u % 2][:, 0:GT], ACT.Gelu_apprx_tanh,
                                                 bias=b1_sb[:, u:u + 1])
                    i.then_inc(act_done, 1)

            group(0)
            with act.Fori(1, NG) as g:
                group(g)

        @block.vector
        def _(dve):
            nc.vector.memset(b2_sb[:, :], 0.0).then_inc(cleared, 1)
            def group(g):
                for u in range(UNITS):
                    j, e = u % 2, u // HC
                    dve.wait_ge(act_done, g * UNITS + u + 1)
                    src = acted[j]
                    if gated:
                        after(dve, hid_ready, g * UNITS + max(u - 1, 0))
                        nc.vector.tensor_tensor(prod[j][:, :], acted[j][:, :], up_ps[j][:, 0:GT], ALU.mult).then_inc(prod_done, 1)
                        dve.wait_ge(prod_done, g * UNITS + u + 1)
                        src = prod[j]
                    dve.wait_ge(wt_ready, g * n_exp + e + 1)
                    after(dve, hid_used, g * UNITS + max(u - 1, 0))
                    nc.vector.tensor_tensor(hid[j][:, :], src[:, :], wt_ps[e % 2][:, 0:GT], ALU.mult).then_inc(hid_ready, 1)
                dve.wait_ge(hid_used, (g + 1) * UNITS)
                part = bass.ds(g * GT, GT)
                nc.vector.tensor_tensor(xT[:, part], xT[:, part], out_ps[:, 0:GT], ALU.add).then_inc(out_added, 1)
                dve.wait_ge(out_added, g + 1)

            group(0)
            with dve.Fori(1, NG) as g:
                group(g)


def stage_ffn0(nc, G, I):
    layer_norm(nc, "s2ln", G, G["xT"], G["xn"])
    with nc.sbuf_tensor("s2_comb", [128, TOK], F32) as combT:
        top2_weights(nc, "s2r", G, G["xn"], I["L0_ffn_router_w"], None, 0, 0, combT)
        experts_ffn(nc, "s2f", G, G["xT"], G["xn"], combT, I["L0_ffn_w1"], I["L0_ffn_w2"], 8, 256, True, None, None)


def stage_ffn1(nc, G, I):
    layer_norm(nc, "s5ln", G, G["xT"], G["xn"])
    with nc.sbuf_tensor("s5_comb", [128, TOK], F32) as combT:
        top2_weights(nc, "s5r", G, G["xn"], I["L1_ffn_router_w"], I["L1_ffn_router_b"], 1, 1, combT)
        experts_ffn(nc, "s5f", G, G["xT"], G["xn"], combT, I["L1_ffn_w1"], I["L1_ffn_w2"], 9, 512, False,
                    I["L1_ffn_b1"], I["L1_ffn_b2"])


KC = 128
NCH = -(-S2 // KC)
LAST = S2 - (NCH - 1) * KC
SEG = 482
SEGS = [(n * SEG, min(SEG, S2 - n * SEG)) for n in range(3)]
TERMS = [(0, 0), (0, 1), (1, 0), (1, 1), (0, 2), (2, 0)]
NEVER = -1e30
MASKED = -float(2 ** 51)


def cross_attention(nc, name, G, I, acc, src, H, wq, bq, wk, bk, wv, bv, wo, bo, masked):
    d = D // H
    RQ = len(TERMS) * d
    SR = 96
    RS = SR + 3
    NE = H * NCH // 8
    NQ = H // 4
    RU = 6 + 3 * H
    KU = 3
    TAIL = 3
    FULL = S2 if len(TERMS) * d == SR else 0
    CLEARS = 17
    scale = 1.0 / float(np.sqrt(d))
    with Stage(nc, name) as st:
        wk_sb, wv_sb, wo_sb = (st.sb(n, [128, D]) for n in ("wk", "wv", "wo"))
        bias = st.sb("bias", [128, 4])
        bv_sb = st.sb("bv", [128, D])
        with Stage(nc, name + "q") as sq:
            wq_sb = sq.sb("wq", [128, D])
            q_ps = [sq.ps(f"ps{j}", [128, BANK]) for j in range(2)]
            q = sq.sb("q", [128, TOK])
            qpart = [sq.sb(f"q{n}", [128, TOK], BF16) for n in range(3)]
            q_out = sq.sem("q_out")
            loaded, q_ready, q_copied, part_done = (sq.sem(n) for n in ("loaded", "q_ready", "q_copied", "part_done"))
            loads = [(wq_sb[:, :], wq), (wk_sb[:, :], wk), (wv_sb[:, :], wv), (wo_sb[:, :], wo)]
            if bq is not None:
                loads += [(bias[:, 0:1], bq), (bias[:, 1:2], bk), (bias[:, 2:3], bo), (bv_sb[:, :], bv.partition_broadcast(128))]
            block = sq.ctx.enter_context(nc.Block())

            @block.sync
            def _(sp):
                for dst, s in loads:
                    sp.dma_start(dst, s).then_inc(loaded, 16)
                sp.wait_ge(loaded, 16 * len(loads))
                sp.wait_ge(part_done, 5 * NG)
                for n in range(3):
                    sp.dma_start(G["q_dram"][n], qpart[n][:, :]).then_inc(q_out, 16)
                sp.wait_ge(q_out, 48)

            @block.tensor
            def _(pe):
                pe.wait_ge(loaded, 16 * len(loads))
                for g in range(NG):
                    after(pe, q_copied, g - 1)
                    nc.tensor.matmul(q_ps[g % 2][:, 0:GT], wq_sb[:, :], src[:, g * GT:(g + 1) * GT],
                                     start=True, stop=True).then_inc(q_ready, 1)

            @block.vector
            def _(dve):
                dve.wait_ge(loaded, 16 * len(loads))
                for g in range(NG):
                    part = slice(g * GT, (g + 1) * GT)
                    dve.wait_ge(q_ready, g + 1)
                    if bq is not None:
                        nc.vector.tensor_scalar(q[:, part], q_ps[g % 2][:, 0:GT], bias[:, 0:1], None, ALU.add).then_inc(q_copied, 1)
                    else:
                        nc.vector.tensor_copy(q[:, part], q_ps[g % 2][:, 0:GT]).then_inc(q_copied, 1)
                    dve.wait_ge(q_copied, g + 1)
                    nc.vector.tensor_copy(qpart[0][:, part], q[:, part]).then_inc(part_done, 1)
                    dve.wait_ge(part_done, 5 * g + 1)
                    nc.vector.tensor_tensor(q[:, part], q[:, part], qpart[0][:, part], ALU.subtract).then_inc(part_done, 1)
                    dve.wait_ge(part_done, 5 * g + 2)
                    nc.vector.tensor_copy(qpart[1][:, part], q[:, part]).then_inc(part_done, 1)
                    dve.wait_ge(part_done, 5 * g + 3)
                    nc.vector.tensor_tensor(q[:, part], q[:, part], qpart[1][:, part], ALU.subtract).then_inc(part_done, 1)
                    dve.wait_ge(part_done, 5 * g + 4)
                    nc.vector.tensor_copy(qpart[2][:, part], q[:, part]).then_inc(part_done, 1)

        kst = [st.sb(f"kst{j}", [RS, H, NCH * KC], BF16) for j in range(2)]
        qst = [st.sb(f"qst{j}", [RS, H, S], BF16) for j in range(2)]
        ctx = [st.sb(f"ctx{j}", [128, S2]) for j in range(2)]
        k = st.sb("k", [128, S2])
        krest = st.sb("krest", [128, S2])
        kpart = [st.sb(f"k{n}", [128, S2], BF16) for n in range(3)]
        v1_all = [st.sb(f"v{j}", [KC, NCH * H * (d + 1) + 32]) for j in range(2)]
        v1 = [v[:, 0:NCH * H * (d + 1)].rearrange("p (c h f) -> p c h f", c=NCH, h=H) for v in v1_all]
        p = [st.sb(f"p{j}", [KC, 2, 4 * S]) for j in range(3)]
        seg_max = st.sb("seg_max", [S, H, 3])
        shift = st.sb("shift", [S, H])
        srest = st.sb("srest", [S, H])
        spart_all = st.sb("spart", [S, 128], BF16)
        spart = spart_all[:, 0:3 * H].rearrange("p (a h) -> p a h", a=3)
        shiftT = st.sb("shiftT", [3 * H, S], BF16)
        inv = st.sb("inv", [S, H])
        z = st.sb("z", [S, D])
        zT = st.sb("zT", [128, S])
        zraw = st.sb("zraw", [128, 4 * S])
        if masked:
            mask8 = st.sb("mask8", [S, S2], U8)
            mask8T = st.sb("mask8T", [KC, NCH, S], U8)
            maskb = st.sb("maskb", [S, S2], BF16)
            maskbT = [st.sb(f"maskbT{j}", [KC, NCH, S], BF16) for j in range(2)]
            junk = [st.sb(f"junk{j}", [S, SEG]) for j in range(2)]
        ring = [st.ps(f"ring{j}", [128, BANK]) for j in range(2)]
        sc = [st.ps(f"sc{j}", [128, 2, BANK]) for j in range(2)]
        zps = st.ps("zps", [128, BANK])
        misc = st.ps("misc", [128, BANK])
        shiftT_ps = misc[:, 0:S // 2].bitcast(BF16)
        zT_ps, o_ps = misc[:, 128:128 + S], misc[:, 256:256 + S]
        (cleared, ring_full, ring_read, k_used, part_ready, qst_in, shift_step, shift_turned, shiftT_done,
         shift_in, sc_full, exp_done, pv_done, z_step, z_turned, zT_done, o_full, o_added, mask_done, kpart_out, zraw_done, zraw_turned) = (
            st.sem(n) for n in ("cleared", "ring_full", "ring_read", "k_used", "part_ready", "qst_in",
                                "shift_step", "shift_turned", "shiftT_done", "shift_in", "sc_full", "exp_done", "pv_done",
                                "z_step", "z_turned", "zT_done", "o_full", "o_added", "mask_done", "kpart_out", "zraw_done", "zraw_turned"))
        block = st.ctx.enter_context(nc.Block())

        ctx_in = [st.sem(f"ctx_in{j}") for j in range(2)]
        kst_in = [st.sem(f"kst_in{n}") for n in range(NQ)]
        mask_in = st.sem("mask_in")

        passed = [st.sem(f"passed{n}") for n in range(3)]

        def ctx_loads(b, j):
            return 8 * (b - j) + 16

        def is_last(t):
            return isinstance(t, int) and t == B - 1

        def ring_no(t, u):
            return 3 + t * RU + u - (KU if is_last(t) else 0)

        def bank_of(t, u):
            return ring[(u + 3 - (KU if is_last(t) else 0)) % 2]

        def slot_units(t, g):
            first = KU if is_last(t) else 0
            n, slots = RU - first, NE - TAIL
            return [first + x for x in range(g * n // slots, (g + 1) * n // slots)] if g < slots else []

        def batches(eng, body):
            body(0, 0, True, False)
            with eng.Fori(0, (B - 4) // 2) as i:
                body(2 * i + 1, 1, True, True)
                body(2 * i + 2, 0, True, True)
            body(B - 3, 1, True, True)
            body(B - 2, 0, True, True)
            body(B - 1, 1, False, True)

        @block.sync
        def _(sp):
            def load_ctx(b, j):
                if b is not 0 and b is not 1:
                    sp.wait_ge(ring_full, ring_no(b - 2, 6))
                    sp.sem_inc(passed[2], 1)
                sp.dma_start(ctx[j][:, :], I["ctxT"][bass.ds(b, 1), :, :].rearrange("a p n -> p (a n)")).then_inc(ctx_in[j], 16)

            def load_masks(b):
                if masked:
                    after(sp, mask_done, 2 * b)
                    sp.sem_inc(passed[2], 1)
                    sp.dma_start(mask8[:, :], I["mask"][bass.ds(b, 1), :, :].rearrange("a p n -> p (a n)")).then_inc(mask_in, 16)
                    sp.dma_start(mask8T[:, :, :], I["maskT"][bass.ds(b, 1), :, :, :].rearrange("a p c n -> p (a c) n")).then_inc(mask_in, 16)

            def put_parts(b, j):
                for n in range(3):
                    sp.wait_ge(part_ready, 3 * b + n + 1)
                    sp.dma_start(G["k_dram"][j, n], kpart[n][:, :]).then_inc(kpart_out, 16)
                sp.wait_ge(kpart_out, 48 * b + 48)
                sp.sem_inc(passed[2], 1)

            def stack_keys(b, j, quad):
                after(sp, kst_in[quad], 16 * len(TERMS) * b)
                sp.sem_inc(passed[2], 1)
                after(sp, sc_full, (b - 2) * NE + 6 * (quad + 1))
                for t, (_, pk) in enumerate(TERMS):
                    sp.dma_start(kst[j][t * d:(t + 1) * d, 4 * quad:4 * quad + 4, 0:S2],
                                 G["k_dram"][j, pk, 4 * d * quad:4 * d * (quad + 1), :].rearrange("(h f) n -> f h n", f=d)).then_inc(kst_in[quad], 16)

            def stack_queries(b, j):
                after(sp, sc_full, (b - 1) * NE)
                sp.sem_inc(passed[2], 1)
                for t, (pq, _) in enumerate(TERMS):
                    sp.dma_start(qst[j][t * d:(t + 1) * d, :, :],
                                 G["q_dram"][pq, :, bass.ds(b * S, S)].rearrange("(h f) n -> f h n", f=d)).then_inc(qst_in, 16)

            def put_shift(b, j):
                sp.wait_ge(shiftT_done, b + 1)
                for n in range(3):
                    sp.dma_start(qst[j][SR + n:SR + n + 1, :, :], shiftT[n * H:(n + 1) * H, :]).then_inc(shift_in, 16)

            def around(t, j, load=True, prepare=True):
                if load:
                    load_ctx(t + 2, j)
                if prepare:
                    load_masks(t + 1)
                    put_parts(t + 1, 1 - j)
                    for quad in range(NQ - 1):
                        stack_keys(t + 1, 1 - j, quad)
                put_shift(t, j)
                if prepare:
                    stack_queries(t + 1, 1 - j)
                    stack_keys(t + 1, 1 - j, NQ - 1)

            load_ctx(0, 0)
            load_ctx(1, 1)
            load_masks(0)
            sp.wait_ge(cleared, CLEARS)
            stack_queries(0, 0)
            put_parts(0, 0)
            for quad in range(NQ):
                stack_keys(0, 0, quad)
            around(0, 0)
            around(1, 1)
            with sp.Fori(0, (B - 4) // 2) as i:
                around(2 * i + 2, 0)
                around(2 * i + 3, 1)
            around(B - 2, 0, load=False)
            around(B - 1, 1, load=False, prepare=False)

        @block.tensor
        def _(pe):
            def project_keys(b, j, u, no, bank):
                if u == 0:
                    pe.wait_ge(ctx_in[j], ctx_loads(b, j))
                after(pe, ring_read, no - 1)
                at, n = SEGS[u]
                nc.tensor.matmul(bank[:, 0:n], wk_sb[:, :], ctx[j][:, at:at + n], start=True, stop=True).then_inc(ring_full, 1)

            def ring_unit(t, j, u):
                no, bank = ring_no(t, u), bank_of(t, u)
                if u < KU:
                    project_keys(t + 1, 1 - j, u, no, bank)
                    return
                after(pe, ring_read, no - 1)
                if u < 6:
                    for c in range(4):
                        cc = (u - 3) * 4 + c
                        n = KC if cc < NCH - 1 else LAST
                        m = nc.tensor.matmul(bank[0:n, c * D:(c + 1) * D], ctx[j][:, cc * KC:cc * KC + n], wv_sb[:, :],
                                             start=True, stop=True)
                else:
                    h, (at, n) = (u - 6) // 3, SEGS[(u - 6) % 3]
                    if u == 6:
                        pe.wait_ge(qst_in, 16 * len(TERMS) * (t + 1))
                    if (u - 6) % 12 == 0:
                        pe.wait_ge(kst_in[h // 4], 16 * len(TERMS) * (t + 1))
                    m = nc.tensor.matmul(bank[0:S, 0:n], qst[j][0:SR, h, :], kst[j][0:SR, h, at:at + n], start=True, stop=True)
                m.then_inc(ring_full, 1)

            def turn_shift(b, j):
                pe.wait_ge(shift_step, 6 * (b + 1))
                nc.tensor.transpose(shiftT_ps, spart_all[:, :], G["ident_bf"][0:S, 0:S]).then_inc(shift_turned, 1)

            def scores(b, j, g):
                if g == 0:
                    pe.wait_ge(shift_in, 48 * (b + 1))
                    if masked:
                        pe.wait_ge(mask_done, 2 * (b + 1))
                after(pe, exp_done, b * NE + g - 1)
                for k2 in range(2):
                    quad, c = g // 6, 2 * (g % 6) + k2
                    if masked:
                        nc.tensor.matmul(sc[g % 2][:, k2, 0:4 * S].rearrange("p (h n) -> p h n", n=S), G["ident_bf"][:, :],
                                         maskbT[j][:, c:c + 1, :].to_broadcast([KC, 4, S]), start=True, stop=False,
                                         skip_group_check=True)
                    for n in range(4):
                        h = 4 * quad + n
                        m = nc.tensor.matmul(sc[g % 2][:, k2, n * S:(n + 1) * S], kst[j][:, h, c * KC:(c + 1) * KC],
                                             qst[j][:, h, :], start=not masked, stop=True, skip_group_check=masked)
                m.then_inc(sc_full, 1)

            def values(b, j, g):
                pe.wait_ge(exp_done, b * NE + g + 1)
                if g == 0:
                    after(pe, z_step, 2 * b)
                    pe.wait_ge(ring_read, ring_no(b, 6))
                for k2 in range(2):
                    quad, c = g // 6, 2 * (g % 6) + k2
                    for n in range(4):
                        at = (c * H + 4 * quad + n) * (d + 1)
                        m = nc.tensor.matmul(zps[32 * n:32 * n + 32, quad * S:(quad + 1) * S], v1_all[j][:, at:at + 32],
                                             p[g % 3][:, k2, n * S:(n + 1) * S], start=(c == 0), stop=(c == NCH - 1))
                m.then_inc(pv_done, 1)

            def turn_sums(b):
                pe.wait_ge(zraw_done, b + 1)
                for quad in range(H // 4):
                    m = nc.tensor.transpose(zps[0:S, quad * 128:(quad + 1) * 128], zraw[:, quad * S:(quad + 1) * S], G["ident"][:, :])
                m.then_inc(zraw_turned, 1)

            def turn_z(b):
                pe.wait_ge(z_step, 2 * (b + 1))
                nc.tensor.transpose(zT_ps, z[:, :], G["ident"][0:S, 0:S]).then_inc(z_turned, 1)

            def project_out(b):
                pe.wait_ge(zT_done, b + 1)
                nc.tensor.matmul(o_ps, wo_sb[:, :], zT[:, :], start=True, stop=True).then_inc(o_full, 1)

            for u in range(3):
                project_keys(0, 0, u, u, ring[u % 2])
            for u in range(RU):
                ring_unit(0, 0, u)
            turn_shift(0, 0)

            def body(b, j, has_next, has_prev):
                for g in range(NE):
                    scores(b, j, g)
                    if has_prev and g == 0:
                        turn_sums(b - 1)
                    if has_next:
                        for u in slot_units(b + 1, g):
                            ring_unit(b + 1, 1 - j, u)
                        if g == NE - TAIL + 1:
                            turn_shift(b + 1, 1 - j)
                    if g:
                        values(b, j, g - 1)
                    if has_prev and g == 2:
                        turn_z(b - 1)
                    if has_prev and g == 3:
                        project_out(b - 1)
                values(b, j, NE - 1)

            batches(pe, body)
            turn_sums(B - 1)
            turn_z(B - 1)
            project_out(B - 1)

        @block.scalar
        def _(act):
            def part(b, n):
                after(act, kpart_out, 48 * b)
                if n == 0:
                    act.wait_ge(ring_read, 3 if b is 0 else ring_no(b - 1, KU))
                    nc.scalar.activation(kpart[0][:, :], k[:, :], ACT.Copy).then_inc(part_ready, 1)
                else:
                    act.wait_ge(k_used, 2 * b + 1)
                    nc.scalar.activation(kpart[1][:, :], krest[:, :], ACT.Copy).then_inc(part_ready, 1)

            def copy_shift(b):
                act.wait_ge(shift_turned, b + 1)
                after(act, shift_in, 48 * b)
                nc.scalar.activation(shiftT[:, :], shiftT_ps[0:3 * H, :], ACT.Copy).then_inc(shiftT_done, 1)

            def copy_z(b):
                act.wait_ge(z_turned, b + 1)
                nc.scalar.activation(zT[:, :], zT_ps, ACT.Copy).then_inc(zT_done, 1)

            for b in range(2):
                part(b, 0)
                part(b, 1)
            copy_shift(0)

            def copy_sums(b):
                act.wait_ge(pv_done, (b + 1) * NE)
                n = H // 4 * S
                nc.scalar.activation(zraw[:, 0:n], zps[:, 0:n], ACT.Copy).then_inc(zraw_done, 1)

            def body(b, j, has_next, has_prev):
                if has_prev:
                    copy_sums(b - 1)
                for g in range(NE):
                    act.wait_ge(sc_full, b * NE + g + 1)
                    after(act, pv_done, b * NE + g - 2)
                    nc.scalar.activation(p[g % 3][:, :, :], sc[g % 2][:, :, 0:4 * S], ACT.Exp, scale=scale).then_inc(exp_done, 1)
                    if has_prev and g == 2:
                        copy_z(b - 1)
                    if has_next and not is_last(b + 1) and g == 3:
                        part(b + 2, 0)
                    if has_next and not is_last(b + 1) and g == 6:
                        part(b + 2, 1)
                    if has_next and g == NE - TAIL + 1:
                        copy_shift(b + 1)

            batches(act, body)
            copy_sums(B - 1)
            copy_z(B - 1)

        @block.gpsimd
        def _(pool):
            def rest(b):
                pool.wait_ge(part_ready, 3 * b + 1)
                nc.gpsimd.tensor_tensor(krest[:, :], k[:, :], kpart[0][:, :], ALU.subtract).then_inc(k_used, 1)
                pool.wait_ge(part_ready, 3 * b + 2)
                pool.wait_ge(k_used, 2 * b + 1)
                after(pool, kpart_out, 48 * b)
                nc.gpsimd.tensor_tensor(kpart[2][:, :], krest[:, :], kpart[1][:, :], ALU.subtract).then_inc(part_ready, 1)
                pool.wait_ge(part_ready, 3 * b + 3)
                pool.sem_inc(k_used, 1)

            def masks(b, j):
                pool.wait_ge(mask_in, 32 * (b + 1))
                if b is not 0:
                    pool.wait_ge(ring_read, ring_no(b - 1, RU))
                pool.sem_inc(passed[1], 1)
                nc.gpsimd.tensor_scalar(maskb[:, :], mask8[:, :], MASKED, None, ALU.mult).then_inc(mask_done, 1)
                after(pool, sc_full, (b - 1) * NE)
                pool.sem_inc(passed[1], 1)
                nc.gpsimd.tensor_scalar(maskbT[j][:, :, :], mask8T[:, :, :], MASKED, None, ALU.mult).then_inc(mask_done, 1)

            rest(0)
            if masked:
                masks(0, 0)
            rest(1)

            def body(b, j, has_next, has_prev):
                if has_next:
                    if masked:
                        masks(b + 1, 1 - j)
                    if not is_last(b + 1):
                        rest(b + 2)

            batches(pool, body)

        @block.vector
        def _(dve):
            def copy_keys(b, u, no, bank):
                dve.wait_ge(ring_full, no + 1)
                at, n = SEGS[u]
                after(dve, k_used, 2 * b)
                if bk is not None:
                    nc.vector.tensor_scalar(k[:, at:at + n], bank[:, 0:n], bias[:, 1:2], None, ALU.add).then_inc(ring_read, 1)
                else:
                    nc.vector.tensor_copy(k[:, at:at + n], bank[:, 0:n]).then_inc(ring_read, 1)

            def ring_unit(b, j, u):
                no, bank = ring_no(b, u), bank_of(b, u)
                if u < KU:
                    copy_keys(b + 1, u, no, bank)
                    return
                dve.wait_ge(ring_full, no + 1)
                if u < 6:
                    if u == 3:
                        after(dve, pv_done, (b - 1) * NE)
                    c0 = (u - 3) * 4
                    for n, c1, c2 in ((KC, 0, 3), (LAST, 3, 4)) if u == 5 else ((KC, 0, 4),):
                        dst = v1[j][0:n, c0 + c1:c0 + c2, :, 0:d].rearrange("p c h f -> p (c h) f")
                        s = bank[0:n, c1 * D:c2 * D].rearrange("p (x f) -> p x f", f=d)
                        if bv is not None:
                            for c in range(c1, c2):
                                m = nc.vector.tensor_tensor(v1[j][0:n, c0 + c, :, 0:d], bank[0:n, c * D:(c + 1) * D].rearrange("p (h f) -> p h f", f=d),
                                                            bv_sb[0:n, :].rearrange("p (h f) -> p h f", f=d), ALU.add)
                        else:
                            m = nc.vector.tensor_copy(dst, s)
                else:
                    h, sg = (u - 6) // 3, (u - 6) % 3
                    at, n = SEGS[sg]
                    if u == 6:
                        after(dve, shift_step, 6 * b)
                    if masked:
                        if u == 6:
                            dve.wait_ge(mask_done, 2 * b + 1)
                        dve.wait_ge(ring_read, no - 1)
                        dve.sem_inc(passed[0], 1)
                        m = nc.vector.tensor_tensor_reduce(junk[u % 2][:, 0:n], bank[0:S, 0:n], maskb[:, at:at + n], 1.0, -3.0e38,
                                                           ALU.add, ALU.max, seg_max[:, h, sg:sg + 1])
                    else:
                        m = nc.vector.tensor_reduce(seg_max[:, h, sg:sg + 1], bank[0:S, 0:n], AX.X, ALU.max)
                m.then_inc(ring_read, 1)

            def make_shift(b):
                dve.wait_ge(ring_read, ring_no(b, RU))
                after(dve, shift_turned, b)
                nc.vector.tensor_reduce(shift[:, :], seg_max[:, :, :], AX.X, ALU.max, negate=True).then_inc(shift_step, 1)
                dve.wait_ge(shift_step, 6 * b + 1)
                nc.vector.tensor_copy(spart[:, 0, :], shift[:, :]).then_inc(shift_step, 1)
                dve.wait_ge(shift_step, 6 * b + 2)
                nc.vector.tensor_tensor(srest[:, :], shift[:, :], spart[:, 0, :], ALU.subtract).then_inc(shift_step, 1)
                dve.wait_ge(shift_step, 6 * b + 3)
                nc.vector.tensor_copy(spart[:, 1, :], srest[:, :]).then_inc(shift_step, 1)
                dve.wait_ge(shift_step, 6 * b + 4)
                nc.vector.tensor_tensor(shift[:, :], srest[:, :], spart[:, 1, :], ALU.subtract).then_inc(shift_step, 1)
                dve.wait_ge(shift_step, 6 * b + 5)
                nc.vector.tensor_copy(spart[:, 2, :], shift[:, :]).then_inc(shift_step, 1)

            def normalise(b):
                dve.wait_ge(zraw_turned, b + 1)
                zv = zps[0:S, 0:H * 32].rearrange("p (h f) -> p h f", f=32)
                nc.vector.reciprocal(inv[:, :].unsqueeze(2), zv[:, :, d:d + 1]).then_inc(z_step, 1)
                dve.wait_ge(z_step, 2 * b + 1)
                nc.vector.tensor_tensor(z[:, :].rearrange("p (h f) -> p h f", f=d), zv[:, :, 0:d],
                                        inv[:, :].unsqueeze(2).to_broadcast([S, H, d]), ALU.mult).then_inc(z_step, 1)

            def add_out(b):
                dve.wait_ge(o_full, b + 1)
                part = acc[:, bass.ds(b * S, S)]
                if bo is not None:
                    nc.vector.scalar_tensor_tensor(out=part, in0=o_ps, scalar=bias[:, 2:3], in1=part,
                                                   op0=ALU.add, op1=ALU.add).then_inc(o_added, 1)
                else:
                    nc.vector.tensor_tensor(part, part, o_ps, ALU.add).then_inc(o_added, 1)

            link = Link(dve, cleared, CLEARS, 0)
            for j in range(2):
                link(nc.vector.memset(kst[j][0:SR, :, FULL:NCH * KC], 0.0))
                link(nc.vector.memset(kst[j][SR:RS, :, 0:S2], 1.0))
                link(nc.vector.memset(kst[j][SR:RS, :, S2:NCH * KC], 0.0))
                link(nc.vector.memset(qst[j][0:SR, :, :], 0.0))
                link(nc.vector.memset(v1_all[j][:, :], 1.0))
                link(nc.vector.memset(v1[j][:, NCH - 1, :, :], 0.0))
                link(nc.vector.memset(v1[j][0:32, NCH - 1, :, d:d + 1], 1.0))
                link(nc.vector.memset(v1[j][32:LAST, NCH - 1, :, d:d + 1], 1.0))
            link(nc.vector.memset(spart_all[:, :], 0.0))
            link.end()
            for u in range(3):
                copy_keys(0, u, u, ring[u % 2])
            for u in range(RU):
                ring_unit(0, 0, u)
            make_shift(0)

            def body(b, j, has_next, has_prev):
                for g in range(NE):
                    if has_next:
                        for u in slot_units(b + 1, g):
                            ring_unit(b + 1, 1 - j, u)
                    if has_prev and g == 0:
                        normalise(b - 1)
                    if has_prev and g == 3:
                        add_out(b - 1)
                    if has_next and g == NE - TAIL:
                        make_shift(b + 1)

            batches(dve, body)
            normalise(B - 1)
            add_out(B - 1)


def stage_cross0(nc, G, I):
    layer_norm(nc, "s1ln", G, G["xT"], G["xn"])
    wq = I["L0_xattn_Wq"]
    cross_attention(nc, "s1x", G, I, G["xT"], G["xn"], 16, wq, None, wq, None, wq, None, I["L0_xattn_Wo"], None, False)


def stage_cross1(nc, G, I):
    layer_norm(nc, "s4ln", G, G["xT"], G["xn"])
    w = {n: I["L1_xattn_" + n] for n in ("Wq", "bq", "Wk", "bk", "Wv", "bv", "Wo", "bo")}
    cross_attention(nc, "s4x", G, I, G["xT"], G["xn"], 16, w["Wq"], w["bq"], w["Wk"], w["bk"], w["Wv"], w["bv"],
                    w["Wo"], w["bo"], True)


class HeadPlan:

    def __init__(self, d):
        self.d = d
        self.inner = 16 * d
        self.pairs = max(1, self.inner // 128)
        self.per_bank = min(4, self.pairs)
        n = self.pairs // self.per_bank
        nv = max(1, self.inner // BANK)
        self.proj = [("q", c) for c in range(n)] + [("k", c) for c in range(n)] + [("v", c) for c in range(nv)]
        self.n_qk, self.nv, self.nt = 2 * n, nv, n
        self.vw = min(BANK, self.inner)
        self.last_use = []
        for u in range(len(self.proj)):
            m = [x for x in range(u) if x % 2 == u % 2]
            if m:
                self.last_use.append((0, m[-1]))
            else:
                m = [x for x in range(len(self.proj)) if x % 2 == u % 2]
                self.last_use.append((1, m[-1]))


def self_attention(nc, name, G, acc, src, d, wq, wk, wv, wo, bq, bk, bv, bo, mode, table):
    H, NB4 = 16, 4
    plan = HeadPlan(d)
    NU, PAIRS, PB, NT, NV, VW = len(plan.proj), plan.pairs, plan.per_bank, plan.nt, plan.nv, plan.vw
    inner = plan.inner
    scale = 1.0 / float(np.sqrt(d))
    tabled = mode is not None
    with Stage(nc, name) as st:
        wq_sb, wk_sb, wv_sb = (st.sb(n, [128, inner]) for n in ("wq", "wk", "wv"))
        wo_sb = st.sb("wo", [128, PAIRS, D])
        bqk = st.sb("bqk", [128, 2, PAIRS])
        bv_sb = st.sb("bv", [S, inner])
        bo_sb = st.sb("bo", [128, 1])
        tab = st.sb("tab", [S, table[1], S]) if tabled else None
        block_mask = st.sb("block_mask", [128, H]) if d == 8 else None
        loads = [(wq_sb[:, :], wq), (wk_sb[:, :], wk), (wv_sb[:, :], wv), (wo_sb[:, :, :], wo)]
        if bq is not None:
            loads += [(bqk[:, 0, :], bq), (bqk[:, 1, :], bk), (bv_sb[:, :], bv.partition_broadcast(S))]
        if bo is not None:
            loads += [(bo_sb[:, :], bo)]
        if tabled:
            loads += [(tab[:, :, :], table[0])]
        if d == 8:
            loads += [(block_mask[:, :], G["block_mask_dram"])]
        xs = st.sb("xs", [128, S])
        qT = st.sb("qT", [128, PAIRS, S])
        kT = st.sb("kT", [128, H, S] if d == 8 else [128, PAIRS, S])
        v = st.sb("v", [S, inner])
        t = st.sb("t", [S, H, S]) if tabled else None
        pr = st.sb("pr", [S, H, S])
        prT = st.sb("prT", [S, H, S])
        low = st.sb("low", [S, H])
        tot = st.sb("tot", [S, H])
        inv = st.sb("inv", [S, H])
        z = st.sb("z", [S, inner])
        zT = st.sb("zT", [128, PAIRS, S])
        aps = [st.ps(f"a{j}", [128, BANK]) for j in range(2)]
        bps = [st.ps(f"b{j}", [128, BANK]) for j in range(NB4)]
        cps = [st.ps(f"c{j}", [128, BANK]) for j in range(2)]
        (loaded, xs_ready, proj_full, proj_read, s_full, t_ready, low_ready, exp_done, turned, prT_ready, z_full, z_step,
         z_turned, zT_ready, o_full, o_added) = (
            st.sem(n) for n in ("loaded", "xs_ready", "proj_full", "proj_read", "s_full", "t_ready", "low_ready", "exp_done",
                                "turned", "prT_ready", "z_full", "z_step", "z_turned", "zT_ready", "o_full", "o_added"))
        LOWS = 1 if tabled else 2
        block = st.ctx.enter_context(nc.Block())

        def batches(eng, body):
            body(0, True, False)
            with eng.Fori(1, B - 1) as b:
                body(b, True, True)
            body(B - 1, False, True)

        @block.sync
        def _(sp):
            for dst, s in loads:
                sp.dma_start(dst, s).then_inc(loaded, 16)
            sp.wait_ge(loaded, 16 * len(loads))

        @block.tensor
        def _(pe):
            pe.wait_ge(loaded, 16 * len(loads))

            def project(b, u):
                kind, c = plan.proj[u]
                back, lu = plan.last_use[u]
                after(pe, proj_read, (b - back) * NU + lu + 1)
                bank = aps[u % 2]
                if kind == "v":
                    if c == 0:
                        pe.wait_ge(xs_ready, b + 1)
                    m = nc.tensor.matmul(bank[0:S, 0:VW], xs[:, :], wv_sb[:, c * VW:(c + 1) * VW], start=True, stop=True)
                else:
                    w = wq_sb if kind == "q" else wk_sb
                    for n in range(PB):
                        p = c * PB + n
                        m = nc.tensor.matmul(bank[:, n * S:(n + 1) * S], w[:, p * 128:(p + 1) * 128], src[:, bass.ds(b * S, S)],
                                             start=True, stop=True)
                m.then_inc(proj_full, 1)

            def scores(b, g):
                if g == 0:
                    pe.wait_ge(proj_read, b * NU + plan.n_qk)
                after(pe, prT_ready, (b - 1) * NB4 + g + 1)
                if d == 8:
                    m = nc.tensor.matmul(bps[g][0:S, 0:4 * S], qT[:, 0, :], kT[:, 4 * g:4 * g + 4, :].rearrange("p h n -> p (h n)"),
                                         start=True, stop=True)
                else:
                    for n in range(4):
                        rows, p = slice(64 * (g % 2), 64 * (g % 2) + 64), 4 * (g // 2) + n
                        m = nc.tensor.matmul(bps[g][0:S, n * S:(n + 1) * S], qT[rows, p, :], kT[rows, p, :],
                                             start=True, stop=True)
                m.then_inc(s_full, 1)

            def turn(b, g):
                pe.wait_ge(exp_done, b * H + 4 * (g + 1))
                for n in range(4):
                    m = nc.tensor.transpose(bps[g][0:S, n * S:(n + 1) * S], pr[:, 4 * g + n, :], G["ident"][0:S, 0:S])
                m.then_inc(turned, 1)

            def values(b, c):
                if c == 0:
                    pe.wait_ge(proj_read, (b + 1) * NU)
                    after(pe, o_added, b)
                hb = H // NV
                for h in range(c * hb, (c + 1) * hb):
                    if h % 4 == 0:
                        pe.wait_ge(prT_ready, b * NB4 + h // 4 + 1)
                    m = nc.tensor.matmul(cps[c][0:S, (h - c * hb) * d:(h - c * hb + 1) * d], prT[:, h, :], v[:, h * d:(h + 1) * d],
                                         start=True, stop=True)
                m.then_inc(z_full, 1)

            def turn_z(b):
                for c in range(NT):
                    if c == 0:
                        pe.wait_ge(z_step, (b + 1) * (1 + NV))
                    for n in range(PB):
                        p = c * PB + n
                        m = nc.tensor.transpose(cps[c][:, n * S:(n + 1) * S], z[:, p * 128:(p + 1) * 128], G["ident"][0:S, 0:S])
                    m.then_inc(z_turned, 1)

            def project_out(b):
                pe.wait_ge(zT_ready, (b + 1) * NT)
                for p in range(PAIRS):
                    m = nc.tensor.matmul(cps[0][:, 0:S], wo_sb[:, p, :], zT[:, p, :], start=(p == 0), stop=(p == PAIRS - 1))
                m.then_inc(o_full, 1)

            for u in range(NU):
                project(0, u)

            def body(b, has_next, has_prev):
                for g in range(NB4):
                    scores(b, g)
                if has_prev:
                    turn_z(b - 1)
                if has_next:
                    for u in range(plan.n_qk // 2):
                        project(b + 1, u)
                if has_prev:
                    project_out(b - 1)
                if has_next:
                    for u in range(plan.n_qk // 2, plan.n_qk):
                        project(b + 1, u)
                for g in range(NB4):
                    turn(b, g)
                for c in range(NV):
                    values(b, c)
                if has_next:
                    for u in range(plan.n_qk, NU):
                        project(b + 1, u)

            batches(pe, body)
            turn_z(B - 1)
            project_out(B - 1)

        @block.gpsimd
        def _(pool):
            def copy_x(b):
                after(pool, proj_full, b * NU)
                nc.gpsimd.tensor_copy(xs[:, :], src[:, bass.ds(b * S, S)]).then_inc(xs_ready, 1)

            copy_x(0)
            with pool.Fori(1, B) as b:
                copy_x(b)

        @block.scalar
        def _(act):
            def softmax(b, g):
                act.wait_ge(low_ready, (b * NB4 + g + 1) * LOWS)
                after(act, turned, (b - 1) * NB4 + g + 1)
                for n in range(4):
                    h = 4 * g + n
                    if tabled:
                        e = nc.scalar.activation(pr[:, h, :], t[:, h, :], ACT.Exp, bias=low[:, h:h + 1], accum_out=tot[:, h:h + 1])
                    else:
                        e = nc.scalar.activation(pr[:, h, :], bps[g][0:S, n * S:(n + 1) * S], ACT.Exp, bias=low[:, h:h + 1],
                                                 scale=scale, accum_out=tot[:, h:h + 1])
                    e.then_inc(exp_done, 1)

            def copy_turned(b, g):
                act.wait_ge(turned, b * NB4 + g + 1)
                after(act, z_full, b * NV)
                nc.scalar.activation(prT[:, 4 * g:4 * g + 4, :], bps[g][0:S, 0:4 * S].rearrange("p (h n) -> p h n", n=S),
                                     ACT.Copy).then_inc(prT_ready, 1)

            def copy_z(b):
                for c in range(NT):
                    act.wait_ge(z_turned, b * NT + c + 1)
                    nc.scalar.activation(zT[:, c * PB:(c + 1) * PB, :], cps[c][:, 0:PB * S].rearrange("p (h n) -> p h n", n=S),
                                         ACT.Copy).then_inc(zT_ready, 1)

            def body(b, has_next, has_prev):
                softmax(b, 0)
                if has_prev:
                    copy_z(b - 1)
                softmax(b, 1)
                softmax(b, 2)
                softmax(b, 3)
                for g in range(NB4):
                    copy_turned(b, g)

            batches(act, body)
            copy_z(B - 1)

        @block.vector
        def _(dve):
            dve.wait_ge(loaded, 16 * len(loads))

            def read_proj(b, u):
                kind, c = plan.proj[u]
                bank = aps[u % 2]
                dve.wait_ge(proj_full, b * NU + u + 1)
                if kind == "v":
                    after(dve, z_full, b * NV)
                    part = slice(c * VW, (c + 1) * VW)
                    if bv is not None:
                        m = nc.vector.tensor_tensor(v[:, part], bank[0:S, 0:VW], bv_sb[:, part], ALU.add)
                    else:
                        m = nc.vector.tensor_copy(v[:, part], bank[0:S, 0:VW])
                else:
                    after(dve, s_full, b * NB4)
                    ps = bank[:, 0:PB * S].rearrange("p (h n) -> p h n", n=S)
                    if kind == "k" and d == 8:
                        m = nc.vector.tensor_tensor(kT[:, :, :], bank[:, 0:S].unsqueeze(1).to_broadcast([128, H, S]),
                                                    block_mask[:, :].unsqueeze(2).to_broadcast([128, H, S]), ALU.mult)
                    else:
                        dst = (qT if kind == "q" else kT)[:, c * PB:(c + 1) * PB, :]
                        if bq is not None:
                            bias = bqk[:, 0 if kind == "q" else 1, c * PB:(c + 1) * PB]
                            m = nc.vector.tensor_tensor(dst, ps, bias.unsqueeze(2).to_broadcast([128, PB, S]), ALU.add)
                        else:
                            m = nc.vector.tensor_copy(dst, ps)
                m.then_inc(proj_read, 1)

            def lowest(b, g):
                dve.wait_ge(s_full, b * NB4 + g + 1)
                after(dve, exp_done, (b - 1) * H + 4 * (g + 1))
                ps = bps[g][0:S, 0:4 * S].rearrange("p (h n) -> p h n", n=S)
                heads = slice(4 * g, 4 * g + 4)
                if tabled:
                    tb = tab[:, heads, :] if table[1] == H else tab[:, 0:1, :].to_broadcast([S, 4, S])
                    nc.vector.scalar_tensor_tensor(out=t[:, heads, :], in0=ps, scalar=scale, in1=tb, op0=ALU.mult,
                                                   op1=ALU.mult if mode == "mul" else ALU.add).then_inc(t_ready, 1)
                    dve.wait_ge(t_ready, b * NB4 + g + 1)
                    nc.vector.tensor_reduce(low[:, heads], t[:, heads, :], AX.X, ALU.max, negate=True).then_inc(low_ready, 1)
                else:
                    nc.vector.tensor_reduce(low[:, heads], ps, AX.X, ALU.max, negate=True).then_inc(low_ready, 1)
                    dve.wait_ge(low_ready, 2 * (b * NB4 + g) + 1)
                    nc.vector.tensor_scalar(low[:, heads], low[:, heads], scale, None, ALU.mult).then_inc(low_ready, 1)

            def normalise(b):
                dve.wait_ge(exp_done, (b + 1) * H)
                nc.vector.reciprocal(inv[:, :], tot[:, :]).then_inc(z_step, 1)
                dve.wait_ge(z_step, b * (1 + NV) + 1)
                after(dve, z_turned, b * NT)
                hb = H // NV
                for c in range(NV):
                    dve.wait_ge(z_full, b * NV + c + 1)
                    nc.vector.tensor_tensor(z[:, c * VW:(c + 1) * VW].rearrange("p (h f) -> p h f", f=d),
                                            cps[c][0:S, 0:VW].rearrange("p (h f) -> p h f", f=d),
                                            inv[:, c * hb:(c + 1) * hb].unsqueeze(2).to_broadcast([S, hb, d]), ALU.mult).then_inc(z_step, 1)

            def add_out(b):
                dve.wait_ge(o_full, b + 1)
                part = acc[:, bass.ds(b * S, S)]
                if bo is not None:
                    nc.vector.scalar_tensor_tensor(out=part, in0=cps[0][:, 0:S], scalar=bo_sb[:, :], in1=part,
                                                   op0=ALU.add, op1=ALU.add).then_inc(o_added, 1)
                else:
                    nc.vector.tensor_tensor(part, part, cps[0][:, 0:S], ALU.add).then_inc(o_added, 1)

            for u in range(NU):
                read_proj(0, u)

            def body(b, has_next, has_prev):
                for g in range(NB4):
                    lowest(b, g)
                if has_next:
                    for u in range(plan.n_qk // 2):
                        read_proj(b + 1, u)
                if has_prev:
                    add_out(b - 1)
                if has_next:
                    for u in range(plan.n_qk // 2, plan.n_qk):
                        read_proj(b + 1, u)
                normalise(b)
                if has_next:
                    for u in range(plan.n_qk, NU):
                        read_proj(b + 1, u)

            batches(dve, body)
            add_out(B - 1)


def load_columns(nc, name, pairs):
    with Stage(nc, name) as st:
        loaded = st.sem("loaded")
        block = st.ctx.enter_context(nc.Block())

        @block.sync
        def _(sp):
            for dst, src in pairs:
                sp.dma_start(dst, src).then_inc(loaded, 16)
            sp.wait_ge(loaded, 16 * len(pairs))


def add_to(nc, name, dst, src):
    with Stage(nc, name) as st:
        added = st.sem("added")
        block = st.ctx.enter_context(nc.Block())

        @block.vector
        def _(dve):
            nc.vector.tensor_tensor(dst[:, :], dst[:, :], src[:, :], ALU.add).then_inc(added, 1)
            dve.wait_ge(added, 1)


def stage_self0(nc, G, I):
    with Stage(nc, "s0") as st:
        xa = st.sb("xa", [128, TOK])
        cols = st.sb("cols", [128, 4])
        load_columns(nc, "s0c", [(cols[:, :], I["L0_ln"])])
        layer_norm(nc, "s0ln", G, G["xT"], G["xn"])
        layer_norm(nc, "s0ln1", G, G["xn"], xa, cols[:, 0:1], cols[:, 1:2])
        w = {n: I["L0_attn_" + n] for n in ("W_Q", "W_K", "W_V", "W_O", "b_Q", "b_K", "b_V", "b_O")}
        self_attention(nc, "s0a", G, G["xn"], xa, 64, w["W_Q"], w["W_K"], w["W_V"], w["W_O"], w["b_Q"], w["b_K"], w["b_V"],
                       w["b_O"], "mul", (I["c_causal01"], 1))
        layer_norm(nc, "s0ln2", G, G["xn"], xa, cols[:, 2:3], cols[:, 3:4])
        add_to(nc, "s0p", G["xT"], G["xn"])
        add_to(nc, "s0r", G["xT"], xa)


def stage_self1(nc, G, I):
    layer_norm(nc, "s3ln", G, G["xT"], G["xn"])
    self_attention(nc, "s3a", G, G["xT"], G["xn"], 64, I["L1_attn_Wq"], I["L1_attn_Wk"], I["L1_attn_Wv"], I["L1_attn_Wo"],
                   None, None, None, I["L1_attn_bo"], None, None)


def stage_self2(nc, G, I):
    layer_norm(nc, "s6ln", G, G["xT"], G["xn"])
    self_attention(nc, "s6a", G, G["xT"], G["xn"], 8, I["L2_attn_wq"], I["L2_attn_wk"], I["L2_attn_wv"], I["L2_attn_wo"],
                   None, None, None, None, "add", (I["c_alibi"], 16))


def stage_self3(nc, G, I):
    layer_norm(nc, "s9ln", G, G["xT"], G["xn"])
    self_attention(nc, "s9a", G, G["xT"], G["xn"], 64, I["L3_attn_wq"], I["L3_attn_wk"], I["L3_attn_wv"], I["L3_attn_wo"],
                   None, None, None, None, "add", (I["c_causal"], 1))


def expert_heads(nc, name, G, I, acc, src):
    H, R, d = 16, 4, 64
    WC = 258
    Q0, K0, V0, BV0 = 0, 65, 130, 194
    idx_dram = nc.dram_tensor(name + "_idx", (B, 8), mybir.dt.uint32, kind="Internal").ap()
    with Stage(nc, name) as st:
        g2 = st.sb("g2", [128, B, R])
        g1 = st.sb("g1", [128, B, R])
        with Stage(nc, name + "r") as sr:
            wr = sr.sb("wr", [128, H])
            br = sr.sb("br", [B, H])
            xm = sr.sb("xm", [128, B])
            dist = sr.sb("dist", [B, H])
            top = sr.sb("top", [B, 8])
            idx = sr.sb("idx", [B, 8], mybir.dt.uint32)
            col = sr.sb("col", [B, 8])
            spread = sr.sb("spread", [B, 2, B, R])
            ones = sr.sb("ones", [B, 128])
            ps = sr.ps("ps", [128, BANK])
            ps2 = sr.ps("ps2", [128, BANK])
            loaded, mean_ready, logits_ready, chain, shifted, exp_done, shifted2, exp2_done, spread_ready, bcast, kept = (
                sr.sem(n) for n in ("loaded", "mean_ready", "logits_ready", "chain", "shifted", "exp_done", "shifted2",
                                    "exp2_done", "spread_ready", "bcast", "kept"))
            block = sr.ctx.enter_context(nc.Block())

            @block.sync
            def _(sp):
                sp.dma_start(wr[:, :], I["L2_ffn_Wr"]).then_inc(loaded, 16)
                sp.dma_start(br[:, :], I["L2_ffn_br"].partition_broadcast(B)).then_inc(loaded, 16)
                sp.wait_ge(spread_ready, 1)
                sp.dma_start(idx_dram, idx[:, :]).then_inc(kept, 16)
                sp.wait_ge(kept, 16)

            @block.tensor
            def _(pe):
                pe.wait_ge(loaded, 32)
                pe.wait_ge(mean_ready, 1)
                nc.tensor.matmul(ps[0:B, 0:H], xm[:, :], wr[:, :], start=True, stop=True).then_inc(logits_ready, 1)
                pe.wait_ge(spread_ready, 1)
                nc.tensor.matmul(ps2[:, 0:2 * B * R], ones[:, :], spread[:, :, :, :].rearrange("p a b k -> p (a b k)"),
                                 start=True, stop=True).then_inc(bcast, 1)

            @block.scalar
            def _(act):
                act.wait_ge(shifted, 1)
                nc.scalar.activation(dist[:, :], dist[:, :], ACT.Exp).then_inc(exp_done, 1)
                act.wait_ge(shifted2, 1)
                nc.scalar.activation(col[:, 0:5], col[:, 0:5], ACT.Exp).then_inc(exp2_done, 1)

            @block.vector
            def _(dve):
                link = Link(dve, chain, 18, 0)
                link(nc.vector.memset(ones[:, :], 1.0))
                link(nc.vector.tensor_reduce(xm[:, :], src[:, :].rearrange("p (b n) -> p b n", n=S), AX.X, ALU.add))
                nc.vector.tensor_scalar(xm[:, :], xm[:, :], 1.0 / S, None, ALU.mult).then_inc(mean_ready, 1)
                dve.wait_ge(loaded, 32)
                dve.wait_ge(logits_ready, 1)
                link(nc.vector.tensor_tensor(dist[:, :], ps[0:B, 0:H], br[:, :], ALU.add))
                link(nc.vector.tensor_reduce(col[:, 7:8], dist[:, :], AX.X, ALU.max))
                nc.vector.tensor_scalar(dist[:, :], dist[:, :], col[:, 7:8], None, ALU.subtract).then_inc(shifted, 1)
                dve.wait_ge(exp_done, 1)
                link(nc.vector.tensor_reduce(col[:, 7:8], dist[:, :], AX.X, ALU.add))
                link(nc.vector.reciprocal(col[:, 6:7], col[:, 7:8]))
                link(nc.vector.tensor_scalar(dist[:, :], dist[:, :], col[:, 6:7], None, ALU.mult))
                link(nc.vector.max(top[:, :], dist[:, :]))
                link(nc.vector.max_index(idx[:, :], top[:, :], dist[:, :]))
                link(nc.vector.memset(col[:, 0:5], 0.0))
                link(nc.vector.tensor_copy(col[:, 0:4], top[:, 0:4]))
                nc.vector.tensor_scalar(col[:, 0:5], col[:, 0:5], top[:, 0:1], None, ALU.subtract).then_inc(shifted2, 1)
                dve.wait_ge(exp2_done, 1)
                link(nc.vector.tensor_reduce(col[:, 7:8], col[:, 0:4], AX.X, ALU.add))
                link(nc.vector.scalar_tensor_tensor(out=col[:, 6:7], in0=col[:, 4:5], scalar=12.0, in1=col[:, 7:8],
                                                    op0=ALU.mult, op1=ALU.add))
                link(nc.vector.reciprocal(col[:, 5:6], col[:, 6:7]))
                link(nc.vector.tensor_scalar(col[:, 0:4], col[:, 0:4], col[:, 5:6], None, ALU.mult))
                diag = G["ident"][0:B, 0:B].unsqueeze(2).to_broadcast([B, B, R])
                gates = col[:, 0:4].unsqueeze(1).to_broadcast([B, B, R])
                link(nc.vector.tensor_tensor(spread[:, 0, :, :], diag, gates, ALU.mult))
                link(nc.vector.tensor_tensor(spread[:, 1, :, :], spread[:, 0, :, :], gates, ALU.mult))
                nc.vector.tensor_scalar(spread[:, 1, :, :], spread[:, 1, :, :], 1.0 / 8.0, None, ALU.mult).then_inc(spread_ready, 1)
                dve.wait_ge(bcast, 1)
                half = ps2[:, 0:2 * B * R].rearrange("p (a b k) -> p a b k", a=2, b=B)
                link(nc.vector.tensor_copy(g1[:, :, :], half[:, 0, :, :]))
                nc.vector.tensor_copy(g2[:, :, :], half[:, 1, :, :])
                link.end()

        w = [st.sb(f"w{j}", [128, R, WC]) for j in range(2)]
        wo_sb = st.sb("wo", [128, 2, D])
        bo_sb = st.sb("bo", [128, 1])
        xs = [st.sb(f"xs{j}", [128, S]) for j in range(2)]
        qT = st.sb("qT", [128, 2, S])
        kT = st.sb("kT", [128, 2, S])
        v = st.sb("v", [S, R, d])
        pr = st.sb("pr", [S, R, S])
        prT = st.sb("prT", [S, R, S])
        low, tot, inv = (st.sb(n, [S, R]) for n in ("low", "tot", "inv"))
        z = st.sb("z", [S, R * d])
        zT = st.sb("zT", [128, 2, S])
        qk_ps, v_ps, turn_ps, z_ps, zT_ps, o_ps = (st.ps(n, [128, BANK]) for n in ("qk", "v", "turn", "z", "zT", "o"))
        s_ps = [st.ps(f"s{j}", [128, BANK]) for j in range(2)]
        passed = st.sem("passed")
        w_in = [st.sem(f"w_in{j}") for j in range(2)]
        (loaded, xs_ready, qk_full, v_full, q_copied, k_copied, v_copied, s_full, low_step, exp_done, turned, prT_ready, z_full,
         z_step, z_turned, zT_ready, o_full, o_added) = (
            st.sem(n) for n in ("loaded", "xs_ready", "qk_full", "v_full", "q_copied", "k_copied", "v_copied", "s_full", "low_step",
                                "exp_done", "turned", "prT_ready", "z_full", "z_step", "z_turned", "zT_ready", "o_full", "o_added"))
        block = st.ctx.enter_context(nc.Block())

        def weights_by(b, j):
            return 8 * R * (b - j) + 16 * R

        def batches(eng, body):
            body(0, 0, True, False)
            with eng.Fori(0, (B - 2) // 2) as i:
                body(2 * i + 1, 1, True, True)
                body(2 * i + 2, 0, True, True)
            body(B - 1, 1, False, True)

        @block.sync
        def _(sp):
            sp.dma_start(wo_sb[:, :, :], I["L2_ffn_Wo"]).then_inc(loaded, 16)
            sp.dma_start(bo_sb[:, :], I["L2_ffn_bo"]).then_inc(loaded, 16)

            def load(b, j):
                for r in range(R):
                    head = sp.value_load(idx_dram[bass.ds(b, 1), r:r + 1], min_val=0, max_val=H - 1)
                    sp.dma_start(w[j][:, r, :], I["L2_ffn_heads"][bass.ds(head, 1), :, :].rearrange("a p n -> p (a n)")).then_inc(w_in[j], 16)

            load(0, 0)
            load(1, 1)

            def next_load(b, j):
                sp.wait_ge(v_copied, b - 1)
                sp.sem_inc(passed, 1)
                load(b, j)

            with sp.Fori(0, (B - 2) // 2) as i:
                next_load(2 * i + 2, 0)
                next_load(2 * i + 3, 1)

        @block.gpsimd
        def _(pool):
            def copy_x(b, j):
                after(pool, v_full, b - 1)
                nc.gpsimd.tensor_copy(xs[j][:, :], src[:, bass.ds(b * S, S)]).then_inc(xs_ready, 1)

            copy_x(0, 0)
            copy_x(1, 1)
            with pool.Fori(0, (B - 2) // 2) as i:
                copy_x(2 * i + 2, 0)
                copy_x(2 * i + 3, 1)

        @block.tensor
        def _(pe):
            pe.wait_ge(loaded, 32)

            def project_qk(b, j):
                pe.wait_ge(w_in[j], weights_by(b, j))
                after(pe, k_copied, 4 * b)
                pe.wait_ge(xs_ready, b + 1)
                for n, c0 in enumerate((Q0, K0)):
                    for r in range(R):
                        rows, at = slice(64 * (r % 2), 64 * (r % 2) + 64), (2 * n + r // 2) * S
                        m = nc.tensor.matmul(qk_ps[rows, at:at + S], w[j][:, r, c0:c0 + d], xs[j][:, :], start=True, stop=True)
                m.then_inc(qk_full, 1)

            def project_v(b, j):
                after(pe, v_copied, b)
                nc.tensor.matmul(v_ps[0:S, 0:R * d], xs[j][:, :], w[j][:, :, V0:V0 + d], start=True, stop=True).then_inc(v_full, 1)

            def scores(b):
                pe.wait_ge(k_copied, 4 * (b + 1))
                pe.wait_ge(q_copied, 4 * (b + 1))
                after(pe, exp_done, R * b)
                for r in range(R):
                    rows = slice(64 * (r % 2), 64 * (r % 2) + 64)
                    m = nc.tensor.matmul(s_ps[r % 2][0:S, (r // 2) * S:(r // 2 + 1) * S], qT[rows, r // 2, :], kT[rows, r // 2, :],
                                         start=True, stop=True)
                m.then_inc(s_full, 1)

            def turn(b):
                after(pe, prT_ready, b)
                for r in range(R):
                    pe.wait_ge(exp_done, R * b + r + 1)
                    m = nc.tensor.transpose(turn_ps[0:S, r * S:(r + 1) * S], pr[:, r, :], G["ident"][0:S, 0:S])
                m.then_inc(turned, 1)

            def values(b):
                pe.wait_ge(prT_ready, b + 1)
                pe.wait_ge(v_copied, b + 1)
                after(pe, z_step, 3 * b)
                for r in range(R):
                    m = nc.tensor.matmul(z_ps[0:S, r * d:(r + 1) * d], prT[:, r, :], v[:, r, :], start=True, stop=True)
                m.then_inc(z_full, 1)

            def turn_z(b):
                pe.wait_ge(z_step, 3 * (b + 1))
                for p in range(2):
                    m = nc.tensor.transpose(zT_ps[:, p * S:(p + 1) * S], z[:, p * 128:(p + 1) * 128], G["ident"][0:S, 0:S])
                m.then_inc(z_turned, 1)

            def project_out(b):
                pe.wait_ge(zT_ready, b + 1)
                for p in range(2):
                    m = nc.tensor.matmul(o_ps[:, 0:S], wo_sb[:, p, :], zT[:, p, :], start=(p == 0), stop=(p == 1))
                m.then_inc(o_full, 1)

            project_qk(0, 0)
            project_v(0, 0)

            def body(b, j, has_next, has_prev):
                scores(b)
                if has_prev:
                    turn_z(b - 1)
                if has_next:
                    project_qk(b + 1, 1 - j)
                if has_prev:
                    project_out(b - 1)
                turn(b)
                values(b)
                if has_next:
                    project_v(b + 1, 1 - j)

            batches(pe, body)
            turn_z(B - 1)
            project_out(B - 1)

        @block.scalar
        def _(act):
            def body(b, j, has_next, has_prev):
                act.wait_ge(low_step, 3 * (b + 1))
                after(act, turned, b)
                for r in range(R):
                    nc.scalar.activation(pr[:, r, :], s_ps[r % 2][0:S, (r // 2) * S:(r // 2 + 1) * S], ACT.Exp, bias=low[:, r:r + 1],
                                         scale=g2[0:S, bass.ds(b, 1), r:r + 1].rearrange("p a r -> p (a r)"),
                                         accum_out=tot[:, r:r + 1]).then_inc(exp_done, 1)
                if has_prev:
                    act.wait_ge(z_turned, b)
                    nc.scalar.activation(zT[:, :, :], zT_ps[:, 0:2 * S].rearrange("p (a n) -> p a n", n=S), ACT.Copy).then_inc(zT_ready, 1)
                act.wait_ge(turned, b + 1)
                after(act, z_full, b)
                nc.scalar.activation(prT[:, :, :], turn_ps[0:S, 0:R * S].rearrange("p (a n) -> p a n", n=S), ACT.Copy).then_inc(prT_ready, 1)

            batches(act, body)
            act.wait_ge(z_turned, B)
            nc.scalar.activation(zT[:, :, :], zT_ps[:, 0:2 * S].rearrange("p (a n) -> p a n", n=S), ACT.Copy).then_inc(zT_ready, 1)

        @block.vector
        def _(dve):
            dve.wait_ge(loaded, 32)

            def copy_qk(b, j):
                dve.wait_ge(qk_full, b + 1)
                dve.wait_ge(w_in[j], weights_by(b, j))
                after(dve, s_full, b)
                for n, (dst, c0, copied) in enumerate(((qT, Q0, q_copied), (kT, K0, k_copied))):
                    for r in range(R):
                        rows = slice(64 * (r % 2), 64 * (r % 2) + 64)
                        nc.vector.tensor_scalar(dst[rows, r // 2, :], qk_ps[rows, (2 * n + r // 2) * S:(2 * n + r // 2 + 1) * S],
                                                w[j][rows, r, c0 + d:c0 + d + 1], None, ALU.add).then_inc(copied, 1)

            def copy_v(b, j):
                dve.wait_ge(v_full, b + 1)
                after(dve, z_full, b)
                nc.vector.tensor_tensor(v[:, :, :], v_ps[0:S, 0:R * d].rearrange("p (r f) -> p r f", f=d), w[j][0:S, :, BV0:BV0 + d],
                                        ALU.add).then_inc(v_copied, 1)

            def lowest(b):
                dve.wait_ge(s_full, b + 1)
                after(dve, exp_done, R * b)
                for half in range(2):
                    nc.vector.tensor_reduce(low[:, half::2], s_ps[half][0:S, 0:2 * S].rearrange("p (r n) -> p r n", n=S), AX.X, ALU.max,
                                            negate=True).then_inc(low_step, 1)
                dve.wait_ge(low_step, 3 * b + 2)
                nc.vector.tensor_tensor(low[:, :], low[:, :], g2[0:S, bass.ds(b, 1), :].rearrange("p a r -> p (a r)"),
                                        ALU.mult).then_inc(low_step, 1)

            def normalise(b):
                dve.wait_ge(exp_done, R * (b + 1))
                nc.vector.reciprocal(inv[:, :], tot[:, :]).then_inc(z_step, 1)
                dve.wait_ge(z_step, 3 * b + 1)
                nc.vector.tensor_tensor(inv[:, :], inv[:, :], g1[0:S, bass.ds(b, 1), :].rearrange("p a r -> p (a r)"),
                                        ALU.mult).then_inc(z_step, 1)
                dve.wait_ge(z_step, 3 * b + 2)
                dve.wait_ge(z_full, b + 1)
                after(dve, z_turned, b)
                nc.vector.tensor_tensor(z[:, :].rearrange("p (r f) -> p r f", f=d), z_ps[0:S, 0:R * d].rearrange("p (r f) -> p r f", f=d),
                                        inv[:, :].unsqueeze(2).to_broadcast([S, R, d]), ALU.mult).then_inc(z_step, 1)

            def add_out(b):
                dve.wait_ge(o_full, b + 1)
                part = acc[:, bass.ds(b * S, S)]
                nc.vector.scalar_tensor_tensor(out=part, in0=o_ps[:, 0:S], scalar=bo_sb[:, :], in1=part,
                                               op0=ALU.add, op1=ALU.add).then_inc(o_added, 1)

            copy_qk(0, 0)
            copy_v(0, 0)

            def body(b, j, has_next, has_prev):
                lowest(b)
                if has_next:
                    copy_qk(b + 1, 1 - j)
                if has_prev:
                    add_out(b - 1)
                normalise(b)
                if has_next:
                    copy_v(b + 1, 1 - j)

            batches(dve, body)
            add_out(B - 1)


def stage_ffn2(nc, G, I):
    layer_norm(nc, "s8ln", G, G["xT"], G["xn"])
    expert_heads(nc, "s8a", G, I, G["xT"], G["xn"])


def dense_ffn(nc, name, acc, src, w1, w2, b1, b2, low_rank):
    HC = 4
    with Stage(nc, name) as st:
        h_ps = [st.ps(f"h{j}", [128, BANK]) for j in range(2)]
        o_ps = st.ps("o", [128, BANK])
        lr_ps = st.ps("lr", [128, BANK])
        t1, t2 = st.sb("t1", [16, GT]), st.sb("t2", [16, GT])
        hid = [st.sb(f"hid{j}", [128, GT]) for j in range(2)]
        rel = [st.sb(f"rel{j}", [128, GT]) for j in range(2)]
        h_full, h_read, hid_ready, hid_used, o_added, lr_full, lr_read = (
            st.sem(n) for n in ("h_full", "h_read", "hid_ready", "hid_used", "o_added", "lr_full", "lr_read"))
        block = st.ctx.enter_context(nc.Block())

        @block.tensor
        def _(pe):
            def group(g):
                x = src[:, bass.ds(g * GT, GT)]
                if low_rank:
                    vT, fbT, uT, _ = low_rank
                    after(pe, lr_read, 2 * g)
                    nc.tensor.matmul(lr_ps[:, 0:GT], vT, x, start=True, stop=True).then_inc(lr_full, 1)
                    pe.wait_ge(lr_read, 2 * g + 1)
                    nc.tensor.matmul(lr_ps[:, 0:GT], fbT, t1[:, :], start=True, stop=True).then_inc(lr_full, 1)
                    pe.wait_ge(lr_read, 2 * g + 2)
                for c in range(HC + 1):
                    if c < HC:
                        after(pe, h_read, g * HC + c - 1)
                        m = nc.tensor.matmul(h_ps[c % 2][:, 0:GT], w1[:, c, :], x, start=True, stop=not low_rank)
                        if low_rank:
                            m = nc.tensor.matmul(h_ps[c % 2][:, 0:GT], uT[:, c * 128:(c + 1) * 128], t2[:, :], start=False, stop=True)
                        m.then_inc(h_full, 1)
                    if c:
                        if c == 1:
                            after(pe, o_added, g)
                        pe.wait_ge(hid_ready, g * HC + c)
                        nc.tensor.matmul(o_ps[:, 0:GT], w2[:, c - 1, :], hid[(c - 1) % 2][:, :], start=(c == 1), stop=(c == HC)).then_inc(hid_used, 1)

            group(0)
            with pe.Fori(1, NG) as g:
                group(g)

        @block.scalar
        def _(act):
            def group(g):
                if low_rank:
                    act.wait_ge(lr_full, 2 * g + 1)
                    nc.scalar.activation(t1[:, :], lr_ps[0:16, 0:GT], ACT.Copy).then_inc(lr_read, 1)
                    act.wait_ge(lr_full, 2 * g + 2)
                    after(act, h_full, g * HC)
                    nc.scalar.activation(t2[:, :], lr_ps[0:16, 0:GT], ACT.Identity, scale=low_rank[3]).then_inc(lr_read, 1)
                for c in range(HC):
                    act.wait_ge(h_full, g * HC + c + 1)
                    if low_rank:
                        after(act, hid_ready, g * HC + c - 1)
                        nc.scalar.activation(rel[c % 2][:, :], h_ps[c % 2][:, 0:GT], ACT.Relu).then_inc(h_read, 1)
                    else:
                        after(act, hid_used, g * HC + c - 1)
                        nc.scalar.activation(hid[c % 2][:, :], h_ps[c % 2][:, 0:GT], ACT.Relu, bias=b1[:, c:c + 1]).then_inc(h_read, 1)
                        act.wait_ge(h_read, g * HC + c + 1)
                        act.sem_inc(hid_ready, 1)

            group(0)
            with act.Fori(1, NG) as g:
                group(g)

        @block.vector
        def _(dve):
            def group(g):
                if low_rank:
                    for c in range(HC):
                        dve.wait_ge(h_read, g * HC + c + 1)
                        after(dve, hid_used, g * HC + c - 1)
                        nc.vector.tensor_tensor(hid[c % 2][:, :], rel[c % 2][:, :], rel[c % 2][:, :], ALU.mult).then_inc(hid_ready, 1)
                dve.wait_ge(hid_used, (g + 1) * HC)
                part = acc[:, bass.ds(g * GT, GT)]
                if b2 is None:
                    nc.vector.tensor_tensor(part, part, o_ps[:, 0:GT], ALU.add).then_inc(o_added, 1)
                else:
                    nc.vector.scalar_tensor_tensor(out=part, in0=o_ps[:, 0:GT], scalar=b2, in1=part, op0=ALU.add, op1=ALU.add).then_inc(o_added, 1)

            group(0)
            with dve.Fori(1, NG) as g:
                group(g)


def diagonal_attention(nc, name, G, I, acc, src):
    scale = float(np.sqrt(D))
    with Stage(nc, name) as st:
        w = st.sb("w", [128, 4, D])
        cols = st.sb("cols", [128, 3])
        bv = st.sb("bv", [S, D])
        mask = st.sb("mask", [S, 1, S])
        xs = st.sb("xs", [128, GT])
        qT, kT, zT = (st.sb(n, [128, GT]) for n in ("qT", "kT", "zT"))
        v = st.sb("v", [S, GB, D])
        t, pr, prT = (st.sb(n, [S, GB, S]) for n in ("t", "pr", "prT"))
        low, tot, inv = (st.sb(n, [S, GB]) for n in ("low", "tot", "inv"))
        q_ps, k_ps, v_ps, s_ps, t_ps, z_ps, o_ps = (st.ps(n, [128, BANK]) for n in ("q", "k", "v", "s", "t", "z", "o"))
        loaded, xs_ready, proj_full, proj_copied, s_full, soft, exp_done, turned, prT_ready, z_full, zT_ready, o_full, o_added = (
            st.sem(n) for n in ("loaded", "xs_ready", "proj_full", "proj_copied", "s_full", "soft", "exp_done", "turned",
                                "prT_ready", "z_full", "zT_ready", "o_full", "o_added"))
        block = st.ctx.enter_context(nc.Block())

        def groups(eng, body):
            body(0)
            with eng.Fori(1, NG) as g:
                body(g)

        @block.sync
        def _(sp):
            for dst, s in ((w[:, :, :], I["L3_sa_w"]), (cols[:, :], I["L3_sa_cols"]), (bv[:, :], I["L3_sa_bv"].partition_broadcast(S)),
                           (mask[:, :, :], I["c_diagonal"])):
                sp.dma_start(dst, s).then_inc(loaded, 16)

        @block.gpsimd
        def _(pool):
            def body(g):
                after(pool, proj_full, 3 * g)
                nc.gpsimd.tensor_copy(xs[:, :], src[:, bass.ds(g * GT, GT)]).then_inc(xs_ready, 1)

            groups(pool, body)

        @block.tensor
        def _(pe):
            pe.wait_ge(loaded, 64)

            def body(g):
                pe.wait_ge(xs_ready, g + 1)
                after(pe, proj_copied, 3 * g)
                nc.tensor.matmul(q_ps[:, 0:GT], w[:, 0, :], xs[:, :], start=True, stop=True).then_inc(proj_full, 1)
                nc.tensor.matmul(k_ps[:, 0:GT], w[:, 1, :], xs[:, :], start=True, stop=True).then_inc(proj_full, 1)
                for n in range(GB):
                    m = nc.tensor.matmul(v_ps[0:S, n * D:(n + 1) * D], xs[:, n * S:(n + 1) * S], w[:, 2, :], start=True, stop=True)
                m.then_inc(proj_full, 1)
                pe.wait_ge(proj_copied, 3 * g + 2)
                after(pe, soft, 4 * g)
                for n in range(GB):
                    part = slice(n * S, (n + 1) * S)
                    m = nc.tensor.matmul(s_ps[0:S, part], qT[:, part], kT[:, part], start=True, stop=True)
                m.then_inc(s_full, 1)
                pe.wait_ge(soft, 4 * g + 4)
                for n in range(GB):
                    m = nc.tensor.transpose(t_ps[0:S, n * S:(n + 1) * S], pr[:, n, :], G["ident"][0:S, 0:S])
                m.then_inc(turned, 1)
                pe.wait_ge(prT_ready, g + 1)
                pe.wait_ge(proj_copied, 3 * g + 3)
                for n in range(GB):
                    m = nc.tensor.matmul(z_ps[:, n * S:(n + 1) * S], v[:, n, :], prT[:, n, :], start=True, stop=True)
                m.then_inc(z_full, 1)
                pe.wait_ge(zT_ready, g + 1)
                after(pe, o_added, g)
                nc.tensor.matmul(o_ps[:, 0:GT], w[:, 3, :], zT[:, :], start=True, stop=True).then_inc(o_full, 1)

            groups(pe, body)

        @block.scalar
        def _(act):
            def body(g):
                act.wait_ge(soft, 4 * g + 2)
                for n in range(GB):
                    nc.scalar.activation(pr[:, n, :], t[:, n, :], ACT.Exp, bias=low[:, n:n + 1], accum_out=tot[:, n:n + 1]).then_inc(exp_done, 1)
                act.wait_ge(turned, g + 1)
                nc.scalar.activation(prT[:, :, :], t_ps[0:S, 0:GT].rearrange("p (a n) -> p a n", n=S), ACT.Copy).then_inc(prT_ready, 1)
                act.wait_ge(z_full, g + 1)
                nc.scalar.activation(zT[:, :], z_ps[:, 0:GT], ACT.Copy).then_inc(zT_ready, 1)

            groups(act, body)

        @block.vector
        def _(dve):
            dve.wait_ge(loaded, 64)

            def body(g):
                dve.wait_ge(proj_full, 3 * g + 1)
                nc.vector.tensor_scalar(qT[:, :], q_ps[:, 0:GT], cols[:, 0:1], None, ALU.add).then_inc(proj_copied, 1)
                dve.wait_ge(proj_full, 3 * g + 2)
                nc.vector.tensor_scalar(kT[:, :], k_ps[:, 0:GT], cols[:, 1:2], None, ALU.add).then_inc(proj_copied, 1)
                dve.wait_ge(proj_full, 3 * g + 3)
                nc.vector.tensor_tensor(v[:, :, :], v_ps[0:S, :].rearrange("p (a n) -> p a n", n=D),
                                        bv[:, :].unsqueeze(1).to_broadcast([S, GB, D]), ALU.add).then_inc(proj_copied, 1)
                dve.wait_ge(s_full, g + 1)
                nc.vector.scalar_tensor_tensor(out=t[:, :, :], in0=s_ps[0:S, 0:GT].rearrange("p (a n) -> p a n", n=S), scalar=scale,
                                               in1=mask[:, 0:1, :].to_broadcast([S, GB, S]), op0=ALU.mult, op1=ALU.add).then_inc(soft, 1)
                dve.wait_ge(soft, 4 * g + 1)
                nc.vector.tensor_reduce(low[:, :], t[:, :, :], AX.X, ALU.max, negate=True).then_inc(soft, 1)
                dve.wait_ge(exp_done, GB * (g + 1))
                nc.vector.reciprocal(inv[:, :], tot[:, :]).then_inc(soft, 1)
                dve.wait_ge(soft, 4 * g + 3)
                nc.vector.tensor_tensor(pr[:, :, :], pr[:, :, :], inv[:, :].unsqueeze(2).to_broadcast([S, GB, S]), ALU.mult).then_inc(soft, 1)
                dve.wait_ge(o_full, g + 1)
                part = acc[:, bass.ds(g * GT, GT)]
                nc.vector.scalar_tensor_tensor(out=part, in0=o_ps[:, 0:GT], scalar=cols[:, 2:3], in1=part, op0=ALU.add, op1=ALU.add).then_inc(o_added, 1)

            groups(dve, body)


def stage_cross3(nc, G, I):
    with Stage(nc, "s10") as st:
        cols = st.sb("cols", [128, 11])
        load_columns(nc, "s10c", [(cols[:, :], I["L3_cols"])])
        layer_norm(nc, "s10ln", G, G["xT"], G["xn"])
        diagonal_attention(nc, "s10s", G, I, G["xn"], G["xn"])
        layer_norm(nc, "s10ln1", G, G["xn"], G["xn"], cols[:, 0:1], cols[:, 1:2])
        w = {n: I["L3_x_" + n] for n in ("wq", "bq", "wk", "bk", "wv", "bv", "wo", "bo")}
        cross_attention(nc, "s10x", G, I, G["xn"], G["xn"], 8, w["wq"], w["bq"], w["wk"], w["bk"], w["wv"], w["bv"],
                        w["wo"], w["bo"], False)
        layer_norm(nc, "s10ln2", G, G["xn"], G["xn"], cols[:, 2:3], cols[:, 3:4])
        w1, w2 = st.sb("w1", [128, 4, 128]), st.sb("w2", [128, 4, 128])
        load_columns(nc, "s10w", [(w1[:, :, :], I["L3_lin1_w"]), (w2[:, :, :], I["L3_lin2_w"])])
        dense_ffn(nc, "s10f", G["xn"], G["xn"], w1, w2, cols[:, 6:10], cols[:, 10:11], None)
        layer_norm(nc, "s10ln3", G, G["xn"], G["xn"], cols[:, 4:5], cols[:, 5:6])
        add_to(nc, "s10p", G["xT"], G["xn"])


def ternary_weights(nc, name, G, natural, n_blocks, n_scales, turned):
    BIG = float(3 << 22)
    row = n_blocks * 128 // n_scales
    with Stage(nc, name) as st:
        mean, inv = st.sb("mean", [128, n_scales]), st.sb("inv", [128, n_scales])
        w = natural[:, :, :].rearrange("p c n -> p (c n)").rearrange("p (s n) -> p s n", s=n_scales)
        shape = [128, n_scales, row]
        tern = st.sb("tern", shape)
        ps = st.ps("ps", [128, BANK])
        chain, ready, turned_ps = st.sem("chain"), st.sem("ready"), st.sem("turned")
        block = st.ctx.enter_context(nc.Block())

        @block.vector
        def _(dve):
            link = Link(dve, chain, 9, 0)
            link(nc.vector.tensor_reduce(mean[:, :], w, AX.X, ALU.add, apply_absolute_value=True))
            link(nc.vector.tensor_scalar(mean[:, :], mean[:, :], 1.0 / row, 1e-5, ALU.mult, ALU.max))
            link(nc.vector.reciprocal(inv[:, :], mean[:, :]))
            link(nc.vector.tensor_tensor(tern[:, :, :], w, inv[:, :].unsqueeze(2).to_broadcast(shape), ALU.mult))
            link(nc.vector.tensor_scalar(tern[:, :, :], tern[:, :, :], BIG, BIG, ALU.add, ALU.subtract))
            link(nc.vector.tensor_scalar(tern[:, :, :], tern[:, :, :], 1.0, -1.0, ALU.min, ALU.max))
            link(nc.vector.tensor_tensor(tern[:, :, :], tern[:, :, :], w, ALU.subtract))
            link(nc.vector.tensor_tensor(tern[:, :, :], tern[:, :, :], w, ALU.add))
            nc.vector.tensor_tensor(tern[:, :, :], tern[:, :, :], mean[:, :].unsqueeze(2).to_broadcast(shape), ALU.mult).then_inc(ready, 1)
            dve.wait_ge(turned_ps, 1)
            link(nc.vector.tensor_copy(turned[:, :, :], ps[:, :].rearrange("p (c n) -> p c n", c=n_blocks)))
            link.end()

        @block.tensor
        def _(pe):
            pe.wait_ge(ready, 1)
            flat = tern[:, :, :].rearrange("p s n -> p (s n)")
            for c in range(n_blocks):
                m = nc.tensor.transpose(ps[:, c * 128:(c + 1) * 128], flat[:, c * 128:(c + 1) * 128], G["ident"][:, :])
            m.then_inc(turned_ps, 1)


def stage_ffn3(nc, G, I):
    layer_norm(nc, "s11ln", G, G["xT"], G["xn"])
    with Stage(nc, "s11") as st:
        fc, proj, fcT, projT = (st.sb(n, [128, 4, 128]) for n in ("fc", "proj", "fcT", "projT"))
        vT = st.sb("vT", [128, 128])
        fbT = st.sb("fbT", [16, 128])
        uT = st.sb("uT", [16, 512])
        gate = st.sb("gate", [16, 1])
        load_columns(nc, "s11w", [(fc[:, :, :], I["L3_ffn_w_fc"]), (proj[:, :, :], I["L3_ffn_w_proj"]), (vT[:, :], I["L3_ffn_v"]),
                                  (fbT[:, :], I["L3_ffn_fast_b"]), (uT[:, :], I["L3_ffn_u"]),
                                  (gate[:, :], I["L3_ffn_gate"].partition_broadcast(16))])
        ternary_weights(nc, "s11a", G, fc, 4, 4, fcT)
        ternary_weights(nc, "s11b", G, proj, 4, 1, projT)
        dense_ffn(nc, "s11f", G["xT"], G["xn"], fcT, projT, None, None, (vT[:, :], fbT[:, :], uT, gate[:, :]))


def bidirectional_attention(nc, name, G, I, acc, src):
    NL = 2
    with Stage(nc, name) as st:
        cols = st.sb("cols", [128, 4])
        consts = st.sb("consts", [S, 3])
        wl = st.sb("wl", [128, 4, D])
        a_all = st.sb("a_all", [128, TOK])
        peak = st.sb("peak", [S, B])
        with Stage(nc, name + "a") as sa:
            ctxT = [sa.sb(f"ctxT{j}", [128, S2]) for j in range(2)]
            ctx = [sa.sb(f"ctx{j}", [KC, NCH, D]) for j in range(2)]
            cs = sa.sb("cs", [128, S])
            xs = sa.sb("xs", [128, S])
            pr = sa.sb("pr", [S, NCH * KC])
            prT = sa.sb("prT", [KC, NCH, S])
            m3, t3 = sa.sb("m3", [S, 4]), sa.sb("t3", [S, 3])
            low, tot, inv = (sa.sb(n, [S, 1]) for n in ("low", "tot", "inv"))
            z = sa.sb("z", [S, D])
            s_ps = [sa.ps(f"s{n}", [128, BANK]) for n in range(3)]
            t_ps = [sa.ps(f"t{n}", [128, BANK]) for n in range(2)]
            z_ps, zT_ps, r_ps = sa.ps("z", [128, BANK]), sa.ps("zT", [128, BANK]), sa.ps("r", [128, BANK])
            ctx_in = [sa.sem(f"ctx_in{j}") for j in range(2)]
            (loaded, cs_ready, xs_ready, s_full, r_full, max_step, exp_done, turned, prT_ready, z_full, z_step, z_turned, a_ready,
             padded) = (
                sa.sem(n) for n in ("loaded", "cs_ready", "xs_ready", "s_full", "r_full", "max_step", "exp_done", "turned", "prT_ready",
                                    "z_full", "z_step", "z_turned", "a_ready", "padded"))
            tot_step = sa.sem("tot_step")
            block = sa.ctx.enter_context(nc.Block())

            def loaded_by(b, j):
                return 8 * NL * (b - j) + 16 * NL

            def batches(eng, body):
                body(0, 0, True, False)
                with eng.Fori(0, (B - 2) // 2) as i:
                    body(2 * i + 1, 1, True, True)
                    body(2 * i + 2, 0, True, True)
                body(B - 1, 1, False, True)

            @block.sync
            def _(sp):
                for dst, s in ((cols[:, :], I["L2_x_cols"]), (consts[:, :], I["L2_x_consts"].partition_broadcast(S)), (wl[:, :, :], I["L2_x_wl"])):
                    sp.dma_start(dst, s).then_inc(loaded, 16)

                def load(b, j):
                    after(sp, z_full, b - 1)
                    sp.dma_start(ctxT[j][:, :], I["ctxT"][bass.ds(b, 1), :, :].rearrange("a p n -> p (a n)")).then_inc(ctx_in[j], 16)
                    sp.dma_start(ctx[j][:, :, :], I["ctx"][bass.ds(b, 1), :, :, :].rearrange("a p c n -> p (a c) n")).then_inc(ctx_in[j], 16)

                load(0, 0)
                load(1, 1)
                with sp.Fori(0, (B - 2) // 2) as i:
                    load(2 * i + 2, 0)
                    load(2 * i + 3, 1)

            @block.gpsimd
            def _(pool):
                def copy_x(b):
                    after(pool, r_full, b)
                    nc.gpsimd.tensor_copy(xs[:, :], src[:, bass.ds(b * S, S)]).then_inc(xs_ready, 1)

                copy_x(0)
                with pool.Fori(1, B) as b:
                    copy_x(b)

            @block.tensor
            def _(pe):
                pe.wait_ge(loaded, 48)
                pe.wait_ge(padded, 1)

                def scores(b, j):
                    pe.wait_ge(ctx_in[j], loaded_by(b, j))
                    pe.wait_ge(cs_ready, b + 1)
                    for n, (at, w) in enumerate(SEGS):
                        after(pe, exp_done, 3 * (b - 1) + n + 1)
                        nc.tensor.matmul(s_ps[n][0:S, 0:w], cs[:, :], ctxT[j][:, at:at + w], start=True, stop=True).then_inc(s_full, 1)
                    pe.wait_ge(xs_ready, b + 1)
                    after(pe, max_step, 4 * b)
                    nc.tensor.matmul(r_ps[0:S, 0:1], xs[:, :], cols[:, 2:3], start=True, stop=True).then_inc(r_full, 1)

                def body(b, j, has_next, has_prev):
                    if has_next:
                        scores(b + 1, 1 - j)
                    pe.wait_ge(exp_done, 3 * (b + 1))
                    for g in range(3):
                        after(pe, prT_ready, 3 * b + g - 1)
                        for c in range(4):
                            at = (4 * g + c) * KC
                            m = nc.tensor.transpose(t_ps[g % 2][0:KC, c * S:(c + 1) * S],
                                                    pr[:, at:at + KC], G["ident"][0:S, 0:S])
                        m.then_inc(turned, 1)
                    after(pe, z_step, 2 * b)
                    for c in range(NCH):
                        if c % 4 == 0:
                            pe.wait_ge(prT_ready, 3 * b + c // 4 + 1)
                        n = KC if c < NCH - 1 else LAST
                        m = nc.tensor.matmul(z_ps[0:S, 0:D], prT[0:n, c, :], ctx[j][0:n, c, :], start=(c == 0), stop=(c == NCH - 1))
                    m.then_inc(z_full, 1)
                    pe.wait_ge(z_step, 2 * (b + 1))
                    after(pe, a_ready, b)
                    nc.tensor.transpose(zT_ps[:, 0:S], z[:, :], G["ident"][0:S, 0:S]).then_inc(z_turned, 1)

                scores(0, 0)
                batches(pe, body)

            @block.scalar
            def _(act):
                def body(b, j, has_next, has_prev):
                    act.wait_ge(max_step, 4 * b + 3)
                    after(act, turned, 3 * b)
                    for n, (at, w) in enumerate(SEGS):
                        nc.scalar.activation(pr[:, at:at + w], s_ps[n][0:S, 0:w], ACT.Exp, bias=low[:, :], accum_out=t3[:, n:n + 1]).then_inc(exp_done, 1)
                    for g in range(3):
                        act.wait_ge(turned, 3 * b + g + 1)
                        after(act, z_full, b)
                        nc.scalar.activation(prT[:, 4 * g:4 * g + 4, :], t_ps[g % 2][0:KC, 0:4 * S].rearrange("p (c n) -> p c n", n=S),
                                             ACT.Copy).then_inc(prT_ready, 1)
                    act.wait_ge(z_turned, b + 1)
                    nc.scalar.activation(a_all[:, bass.ds(b * S, S)], zT_ps[:, 0:S], ACT.Copy).then_inc(a_ready, 1)

                batches(act, body)

            @block.vector
            def _(dve):
                nc.vector.memset(pr[:, S2:NCH * KC], 0.0).then_inc(padded, 1)
                dve.wait_ge(loaded, 48)

                def scale_queries(b):
                    after(dve, s_full, 3 * b)
                    nc.vector.tensor_scalar(cs[:, :], src[:, bass.ds(b * S, S)], cols[:, 0:1], cols[:, 1:2], ALU.mult, ALU.add).then_inc(cs_ready, 1)

                def maxima(b):
                    for n, (at, w) in enumerate(SEGS):
                        dve.wait_ge(s_full, 3 * b + n + 1)
                        m = nc.vector.tensor_reduce(m3[:, n:n + 1], s_ps[n][0:S, 0:w], AX.X, ALU.max)
                    m.then_inc(max_step, 1)
                    dve.wait_ge(max_step, 4 * b + 1)
                    nc.vector.tensor_reduce(m3[:, 3:4], m3[:, 0:3], AX.X, ALU.max).then_inc(max_step, 1)
                    dve.wait_ge(max_step, 4 * b + 2)
                    after(dve, exp_done, 3 * b)
                    nc.vector.tensor_scalar(low[:, :], m3[:, 3:4], -1.0, None, ALU.mult).then_inc(max_step, 1)
                    dve.wait_ge(r_full, b + 1)
                    nc.vector.tensor_tensor(peak[:, bass.ds(b, 1)], m3[:, 3:4], r_ps[0:S, 0:1], ALU.add).then_inc(max_step, 1)
                    dve.wait_ge(max_step, 4 * b + 4)

                def normalise(b):
                    dve.wait_ge(z_full, b + 1)
                    after(dve, z_turned, b)
                    nc.vector.tensor_reduce(tot[:, :], t3[:, :], AX.X, ALU.add).then_inc(tot_step, 1)
                    dve.wait_ge(tot_step, b + 1)
                    nc.vector.reciprocal(inv[:, :], tot[:, :]).then_inc(z_step, 1)
                    dve.wait_ge(z_step, 2 * b + 1)
                    nc.vector.tensor_scalar(z[:, :], z_ps[0:S, 0:D], inv[:, :], None, ALU.mult).then_inc(z_step, 1)

                def body(b, j, has_next, has_prev):
                    if has_next:
                        scale_queries(b + 1)
                    normalise(b)
                    if has_next:
                        maxima(b + 1)

                scale_queries(0)
                maxima(0)
                batches(dve, body)

        with Stage(nc, name + "b") as sb:
            pc = sb.sb("pc", [S, B])
            rowT = sb.sb("rowT", [B, S])
            low, tot, inv = (sb.sb(n, [B, 1]) for n in ("low", "tot", "inv"))
            spread = sb.sb("spread", [B, B, S])
            ones = sb.sb("ones", [B, 128])
            q2c = sb.sb("q2c", [128, B])
            junk = [sb.sb(f"junk{j}", [128, GT]) for j in range(2)]
            ca = [sb.sb(f"ca{j}", [128, GT]) for j in range(2)]
            cq = [sb.sb(f"cq{j}", [128, GT]) for j in range(2)]
            p_ps = sb.ps("p", [128, BANK])
            b_ps = [sb.ps(f"b{j}", [128, BANK]) for j in range(2)]
            o_ps = [sb.ps(f"o{j}", [128, BANK]) for j in range(2)]
            chain, peak_ready, turned, shifted, exp_done, spread_ready, b_full, q2c_done, ca_ready, cq_ready, o_full, o_added = (
                sb.sem(n) for n in ("chain", "peak_ready", "turned", "shifted", "exp_done", "spread_ready", "b_full", "q2c_done",
                                    "ca_ready", "cq_ready", "o_full", "o_added"))
            summed = sb.sem("summed")
            block = sb.ctx.enter_context(nc.Block())

            @block.tensor
            def _(pe):
                pe.wait_ge(peak_ready, 1)
                nc.tensor.transpose(p_ps[0:B, 0:S], pc[:, :], G["ident"][0:S, 0:S]).then_inc(turned, 1)
                pe.wait_ge(spread_ready, 1)

                def group(g, j):
                    part = slice(g * GT, (g + 1) * GT)
                    after(pe, q2c_done, g - 1)
                    nc.tensor.matmul(b_ps[j][:, 0:GT], ones[:, :], spread[:, g * GB:(g + 1) * GB, :].rearrange("p b n -> p (b n)"),
                                     start=True, stop=True).then_inc(b_full, 1)
                    after(pe, o_added, g - 1)
                    nc.tensor.matmul(o_ps[j][:, 0:GT], wl[:, 0, :], src[:, part], start=True, stop=False)
                    nc.tensor.matmul(o_ps[j][:, 0:GT], wl[:, 1, :], a_all[:, part], start=False, stop=False)
                    pe.wait_ge(ca_ready, g + 1)
                    nc.tensor.matmul(o_ps[j][:, 0:GT], wl[:, 2, :], ca[j][:, :], start=False, stop=False)
                    pe.wait_ge(cq_ready, g + 1)
                    nc.tensor.matmul(o_ps[j][:, 0:GT], wl[:, 3, :], cq[j][:, :], start=False, stop=True).then_inc(o_full, 1)

                for g in range(NG):
                    group(g, g % 2)

            @block.scalar
            def _(act):
                act.wait_ge(shifted, 1)
                nc.scalar.activation(rowT[:, :], p_ps[0:B, 0:S], ACT.Exp, bias=low[:, :], accum_out=tot[:, :]).then_inc(exp_done, 1)

            @block.gpsimd
            def _(pool):
                for g in range(NG):
                    after(pool, o_full, g - 1)
                    part = slice(g * GT, (g + 1) * GT)
                    nc.gpsimd.tensor_tensor(ca[g % 2][:, :], src[:, part], a_all[:, part], ALU.mult).then_inc(ca_ready, 1)

            @block.vector
            def _(dve):
                link = Link(dve, chain, 4, 0)
                link(nc.vector.memset(ones[:, :], 1.0))
                link(nc.vector.tensor_scalar(pc[:, :], peak[:, :], consts[:, 0:1], consts[:, 1:2], ALU.add, ALU.add))
                nc.vector.tensor_scalar(pc[:, :], pc[:, :], consts[:, 2:3], None, ALU.add).then_inc(peak_ready, 1)
                dve.wait_ge(turned, 1)
                nc.vector.tensor_reduce(low[:, :], p_ps[0:B, 0:S], AX.X, ALU.max, negate=True).then_inc(shifted, 1)
                dve.wait_ge(exp_done, 1)
                link(nc.vector.reciprocal(inv[:, :], tot[:, :]))
                link(nc.vector.tensor_scalar(rowT[:, :], rowT[:, :], inv[:, :], None, ALU.mult))
                nc.vector.tensor_tensor(spread[:, :, :], rowT[:, :].unsqueeze(1).to_broadcast([B, B, S]),
                                        G["ident"][0:B, 0:B].unsqueeze(2).to_broadcast([B, B, S]), ALU.mult).then_inc(spread_ready, 1)
                for g in range(NG):
                    j, part = g % 2, slice(g * GT, (g + 1) * GT)
                    dve.wait_ge(b_full, g + 1)
                    after(dve, cq_ready, g - 1)
                    nc.vector.tensor_tensor(junk[j][:, :], src[:, part], b_ps[j][:, 0:GT], ALU.mult).then_inc(q2c_done, 1)
                    dve.wait_ge(q2c_done, g + 1)
                    nc.vector.tensor_reduce(q2c[:, g * GB:(g + 1) * GB], junk[j][:, :].rearrange("p (b n) -> p b n", n=S), AX.X,
                                            ALU.add).then_inc(summed, 1)
                    dve.wait_ge(summed, g + 1)
                    after(dve, o_full, g - 1)
                    nc.vector.tensor_tensor(cq[j][:, :].rearrange("p (b n) -> p b n", n=S), src[:, part].rearrange("p (b n) -> p b n", n=S),
                                            q2c[:, g * GB:(g + 1) * GB].unsqueeze(2).to_broadcast([128, GB, S]), ALU.mult).then_inc(cq_ready, 1)
                    dve.wait_ge(o_full, g + 1)
                    nc.vector.scalar_tensor_tensor(out=acc[:, part], in0=o_ps[j][:, 0:GT], scalar=cols[:, 3:4], in1=acc[:, part],
                                                   op0=ALU.add, op1=ALU.add).then_inc(o_added, 1)
                link.end()


def stage_cross2(nc, G, I):
    layer_norm(nc, "s7ln", G, G["xT"], G["xn"])
    bidirectional_attention(nc, "s7x", G, I, G["xT"], G["xn"])


STAGE_FUNCS = {7: stage_cross2, 8: stage_ffn2, 10: stage_cross3, 11: stage_ffn3, 0: stage_self0, 3: stage_self1, 6: stage_self2, 9: stage_self3, 1: stage_cross0, 4: stage_cross1, 2: stage_ffn0, 5: stage_ffn1}


def build(nc, I, out):
    ctx = ExitStack()
    with ctx:
        def sb(name, shape, dt=F32):
            return ctx.enter_context(nc.sbuf_tensor(name, list(shape), dt))

        G = {"xT": sb("xT", [128, TOK]), "xn": sb("xn", [128, TOK]), "ident": sb("ident", [128, 128]),
             "mean_mat": sb("mean_mat", [128, 128]), "ident_bf": sb("ident_bf", [128, 128], BF16),
             "eps": sb("eps", [128, 1])}
        G["q_dram"] = nc.dram_tensor("q_parts", (3, D, TOK), BF16, kind="Internal").ap()
        G["k_dram"] = nc.dram_tensor("k_parts", (2, 3, D, S2), BF16, kind="Internal").ap()
        for k in ("earlier", "pick", "block_mask"):
            G[k + "_dram"] = I["c_" + k]
        with Stage(nc, "init") as st:
            loaded = st.sem("loaded")
            made = st.sem("made")
            block = st.ctx.enter_context(nc.Block())

            @block.sync
            def _(sp):
                sp.dma_start(G["xT"][:, :], I["x"]).then_inc(loaded, 16)
                sp.dma_start(G["ident"][:, :], I["c_ident"]).then_inc(loaded, 16)
                sp.wait_ge(loaded, 32)

            @block.vector
            def _(dve):
                nc.vector.memset(G["mean_mat"][:, :], 1.0 / D).then_inc(made, 1)
                nc.vector.memset(G["eps"][:, :], EPS).then_inc(made, 1)
                dve.wait_ge(loaded, 32)
                nc.vector.tensor_copy(G["ident_bf"][:, :], G["ident"][:, :]).then_inc(made, 1)
                dve.wait_ge(made, 3)

        for s in STAGES:
            STAGE_FUNCS[s](nc, G, I)

        with Stage(nc, "fin") as st:
            saved = st.sem("saved")
            block = st.ctx.enter_context(nc.Block())

            @block.sync
            def _(sp):
                sp.dma_start(out, G["xT"][:, :]).then_inc(saved, 16)
                sp.wait_ge(saved, 16)


def lay_out(v):
    A = {}
    A["x"] = v["x"].transpose(2, 0, 1).reshape(D, TOK)
    A["c_ident"] = np.eye(128, dtype=np.float32)
    A["c_earlier"] = np.broadcast_to(np.tril(np.ones((8, 8), np.float32), -1), (S, 8, 8))
    A["c_pick"] = np.broadcast_to(np.eye(128, 9, dtype=np.float32)[:, :, None], (128, 9, 128))
    q, k = np.arange(S)[:, None], np.arange(S)[None, :]
    A["c_block_mask"] = (np.arange(128)[:, None] // 8 == np.arange(16)[None, :]).astype(np.float32)
    A["c_causal01"] = (k <= q).astype(np.float32)[:, None, :]
    A["c_causal"] = np.where(k <= q, 0.0, NEVER).astype(np.float32)[:, None, :]
    slope = (2.0 ** (-8.0 / 16 * (np.arange(16, dtype=np.float32) + 1.0))).astype(np.float32)
    alibi = slope[None, :, None] * (k - q).astype(np.float32)[:, None, :]
    A["c_alibi"] = np.where((k <= q)[:, None, :], alibi, NEVER).astype(np.float32)

    def rows(w):
        return w.reshape(-1, 128, w.shape[-1]).transpose(1, 0, 2)

    def columns(b):
        return b.reshape(-1, 128).T

    order = [4 * (2 * (p // 4) + half) + p % 4 for p in range(8) for half in range(2)]

    def paired(w):
        w = w.reshape(-1, 16, 64)[:, order]
        return w.reshape(-1, 1024)

    for n in "QKV":
        A["L0_attn_W_" + n] = v["L0_attn_W_" + n].transpose(1, 0, 2).reshape(D, 1024)
    for n in "QK":
        A["L0_attn_W_" + n] = paired(A["L0_attn_W_" + n])
    A["L0_attn_W_O"] = rows(v["L0_attn_W_O"].reshape(1024, D))
    A["L0_attn_b_Q"], A["L0_attn_b_K"] = columns(paired(v["L0_attn_b_Q"])), columns(paired(v["L0_attn_b_K"]))
    A["L0_attn_b_V"] = v["L0_attn_b_V"].reshape(-1)
    A["L0_attn_b_O"] = v["L0_attn_b_O"].reshape(D, 1)
    A["L0_ln"] = np.stack([v["L0_attn_" + n] for n in ("ln1_w", "ln1_b", "ln2_w", "ln2_b")], 1)
    A["L1_attn_Wq"] = paired(v["L1_attn_Wq"])
    A["L1_attn_Wk"], A["L1_attn_Wv"] = paired(v["L1_attn_Wkv"][:, :1024]), v["L1_attn_Wkv"][:, 1024:]
    A["L1_attn_Wo"] = rows(v["L1_attn_Wo"])
    A["L1_attn_bo"] = v["L1_attn_bo"].reshape(D, 1)
    for m, n in enumerate(("wq", "wk", "wv")):
        A["L2_attn_" + n] = v["L2_attn_w_in"][m * D:(m + 1) * D].T
        A["L3_attn_" + n] = v["L3_attn_" + n].T
    A["L3_attn_wq"], A["L3_attn_wk"] = paired(A["L3_attn_wq"]), paired(A["L3_attn_wk"])
    A["L2_attn_wo"] = rows(v["L2_attn_w_out"].T)
    A["L3_attn_wo"] = rows(v["L3_attn_wo"].T)
    heads = []
    for h in range(16):
        f = slice(h * 64, h * 64 + 64)
        cols = []
        for n in "qk":
            cols += [v["L2_ffn_W" + n][:, f], np.tile(v["L2_ffn_b" + n][f], 2)[:, None]]
        cols += [v["L2_ffn_Wv"][:, f], np.broadcast_to(v["L2_ffn_bv"][f], (128, 64))]
        heads.append(np.concatenate(cols, 1))
    A["L2_ffn_heads"] = np.stack(heads)
    A["L2_ffn_Wr"], A["L2_ffn_br"] = v["L2_ffn_Wr"], v["L2_ffn_br"]
    A["L2_ffn_Wo"] = rows(v["L2_ffn_Wo"])
    A["L2_ffn_bo"] = v["L2_ffn_bo"].reshape(D, 1)
    A["c_diagonal"] = np.where(k == q, 0.0, NEVER).astype(np.float32)[:, None, :]
    qkv_b = v["L3_xattn_qkv_b"].reshape(3, D)
    A["L3_sa_w"] = np.stack([w.T for w in (*v["L3_xattn_qkv_w"].reshape(3, D, D), v["L3_xattn_sa_out_w"])], 1)
    A["L3_sa_cols"] = np.stack([qkv_b[0], qkv_b[1], v["L3_xattn_sa_out_b"]], 1)
    A["L3_sa_bv"] = qkv_b[2]
    A["L3_cols"] = np.concatenate([np.stack([v["L3_xattn_" + n] for n in ("ln1_g", "ln1_b", "ln2_g", "ln2_b", "ln3_g", "ln3_b")], 1),
                                   columns(v["L3_xattn_lin1_b"]), columns(v["L3_xattn_lin2_b"])], 1)
    for m, n in enumerate("qkv"):
        A["L3_x_w" + n] = v["L3_xattn_in_proj_w"][m * D:(m + 1) * D].T
        A["L3_x_b" + n] = v["L3_xattn_in_proj_b"][m * D:(m + 1) * D].reshape((D, 1) if n != "v" else (D,))
    A["L3_x_wo"] = v["L3_xattn_mha_out_w"].T
    A["L3_x_bo"] = v["L3_xattn_mha_out_b"].reshape(D, 1)
    A["L3_lin1_w"] = v["L3_xattn_lin1_w"].T.reshape(128, 4, 128)
    A["L3_lin2_w"] = rows(v["L3_xattn_lin2_w"].T)
    A["L3_ffn_w_fc"] = rows(v["L3_ffn_w_fc"])
    A["L3_ffn_w_proj"] = v["L3_ffn_w_proj"].reshape(128, 4, 128)
    A["L3_ffn_v"] = np.pad(v["L3_ffn_v"].T, ((0, 0), (0, 112)))
    A["L3_ffn_fast_b"] = np.pad(v["L3_ffn_fast_b"].T, ((0, 0), (0, 112)))
    A["L3_ffn_u"] = v["L3_ffn_u"].T
    A["L3_ffn_gate"] = v["L3_ffn_gate"].reshape(1)
    A["ctx"] = np.pad(v["ctx_1024"], ((0, 0), (0, NCH * KC - S2), (0, 0))).reshape(B, NCH, KC, D).transpose(0, 2, 1, 3)
    A["L2_x_cols"] = np.stack([v["L2_xattn_" + n] for n in ("w_cq", "w_q", "w_c", "b_l")], 1)
    A["L2_x_consts"] = np.stack([v["L2_xattn_" + n].reshape(()) for n in ("b_c", "b_q", "b_cq")])
    A["L2_x_wl"] = v["L2_xattn_W_l"].T.reshape(4, D, D).transpose(1, 0, 2)
    A["ctxT"] = v["ctx_1024"].transpose(0, 2, 1)
    mask = v["mask_Bx1xSxS2_bk1"][:, 0]
    A["mask"] = mask
    A["maskT"] = np.pad(mask, ((0, 0), (0, 0), (0, NCH * KC - S2))).reshape(B, S, NCH, KC).transpose(0, 3, 2, 1)
    A["L0_xattn_Wq"] = v["L0_xattn_Wq"].T
    A["L0_xattn_Wo"] = v["L0_xattn_Wo"].T
    for n in ("Wq", "Wk", "Wv", "Wo"):
        A["L1_xattn_" + n] = v["L1_xattn_" + n]
    for n in ("bq", "bk", "bo"):
        A["L1_xattn_" + n] = v["L1_xattn_" + n].reshape(D, 1)
    A["L1_xattn_bv"] = v["L1_xattn_bv"]
    A["L0_ffn_router_w"] = v["L0_ffn_router_w"].T
    A["L0_ffn_w1"] = v["L0_ffn_w1"].transpose(2, 0, 1)
    A["L0_ffn_w2"] = v["L0_ffn_w2"].reshape(8, 128, 2, 128).transpose(3, 0, 2, 1)
    A["L1_ffn_router_w"] = v["L1_ffn_router_w"].T
    A["L1_ffn_router_b"] = v["L1_ffn_router_b"]
    w1 = np.concatenate([v["L1_ffn_spec_w1"], v["L1_ffn_shared_w1"][None]])
    w2 = np.concatenate([v["L1_ffn_spec_w2"], v["L1_ffn_shared_w2"][None]])
    b1 = np.concatenate([v["L1_ffn_spec_b1"], v["L1_ffn_shared_b1"][None]])
    A["L1_ffn_w1"] = w1.transpose(2, 0, 1)
    A["L1_ffn_w2"] = w2.reshape(9, 128, 4, 128).transpose(3, 0, 2, 1)
    A["L1_ffn_b1"] = b1.reshape(36, 128).T
    A["L1_ffn_b2"] = np.concatenate([v["L1_ffn_spec_b2"], v["L1_ffn_shared_b2"][None]])
    return A


def kernel(**inputs):
    import concourse.bacc as bacc
    from concourse.bass_utils import run_bass_kernel_spmd

    nc = bacc.Bacc("TRN2", target_bir_lowering=False, num_devices=1)
    laid = lay_out({k: np.asarray(a) for k, a in inputs.items()})
    arrays, I = {}, {}
    for name, a in laid.items():
        a = np.ascontiguousarray(a)
        arrays[f"in_{name}"] = a
        I[name] = nc.dram_tensor(f"in_{name}", a.shape, mybir.dt.from_np(a.dtype), kind="ExternalInput").ap()
    out = nc.dram_tensor("out_xT", (D, TOK), F32, kind="ExternalOutput").ap()
    build(nc, I, out)
    r = run_bass_kernel_spmd(nc, [arrays], core_ids=[0])
    return r.results[0]["out_xT"].reshape(D, B, S).transpose(1, 2, 0)
```

```python
from contextlib import ExitStack

import numpy as np
import concourse.bass as bass
from concourse import mybir
from concourse.alu_op_type import AluOpType as ALU

ACT = mybir.ActivationFunctionType
F32 = mybir.dt.float32
BF16 = mybir.dt.bfloat16
U8 = mybir.dt.uint8
AX = mybir.AxisListType

STAGES = range(0, 12)

B, S, D = 32, 100, 128
TOK = B * S
GB = 4
GT = GB * S
NG = B // GB
S2 = 1444
EPS = 1e-5
BANK = 512


class Stage:

    def __init__(self, nc, name):
        self.nc, self.name, self.ctx, self.sems = nc, name, ExitStack(), []

    def __enter__(self):
        return self

    def __exit__(self, *a):
        self.ctx.__exit__(*a)
        if self.sems and a[0] is None:
            self.nc.clear_and_free_semaphores(self.sems)
            self.nc.all_engine_barrier()
        return False

    def sb(self, name, shape, dt=F32):
        return self.ctx.enter_context(self.nc.sbuf_tensor(f"{self.name}_{name}", list(shape), dt))

    def ps(self, name, shape, dt=F32):
        return self.ctx.enter_context(self.nc.psum_tensor(f"{self.name}_ps_{name}", list(shape), dt))

    def sem(self, name):
        self.sems.append(self.nc.alloc_semaphore(f"{self.name}_{name}"))
        return self.sems[-1]


class Link:

    def __init__(self, eng, sem, per, i):
        self.eng, self.sem, self.per, self.i, self.c = eng, sem, per, i, 0

    def __call__(self, ins):
        self.c += 1
        ins.then_inc(self.sem, 1)
        self.eng.wait_ge(self.sem, self.i * self.per + self.c)

    def end(self):
        assert self.c == self.per, (self.c, self.per)


def after(eng, sem, n):
    if not (isinstance(n, int) and n <= 0):
        eng.wait_ge(sem, n)


def layer_norm(nc, name, G, src, dst, gain=None, shift=None):
    ROWS = 128 // NG
    with Stage(nc, name) as st:
        mean = [st.ps(f"mean{j}", [128, BANK]) for j in range(2)]
        var = st.ps("var", [128, BANK])
        back = [st.ps(f"back{j}", [128, BANK]) for j in range(2)]
        square = [st.sb(f"square{j}", [128, GT]) for j in range(2)]
        inverse = st.sb("inverse", [128, GT])
        mean_ready, centred, squared, var_ready, std_ready, inverted, spread, normed, scaled = (
            st.sem(n) for n in ("mean_ready", "centred", "squared", "var_ready", "std_ready", "inverted", "spread",
                                "normed", "scaled"))
        block = st.ctx.enter_context(nc.Block())

        def columns(g):
            return slice(g * GT, (g + 1) * GT)

        @block.tensor
        def _(pe):
            def mean_of(g):
                after(pe, centred, g - 1)
                nc.tensor.matmul(mean[g % 2][:, 0:GT], G["mean_mat"][:, :], src[:, columns(g)],
                                 start=True, stop=True).then_inc(mean_ready, 1)

            mean_of(0)
            mean_of(1)
            for g in range(NG):
                pe.wait_ge(squared, g + 1)
                nc.tensor.matmul(var[:, 0:GT], G["mean_band"][:, (NG - 1 - g) * ROWS:(NG - 1 - g) * ROWS + 128],
                                 square[g % 2][:, :], start=(g == 0), stop=(g == NG - 1)).then_inc(var_ready, 1)
                if g + 2 < NG:
                    mean_of(g + 2)
            pe.wait_ge(inverted, 1)
            for g in range(NG):
                after(pe, normed, g - 1)
                nc.tensor.matmul(back[g % 2][:, 0:GT], G["pick"][:, g, :], inverse[:, :],
                                 start=True, stop=True).then_inc(spread, 1)

        @block.scalar
        def _(act):
            for g in range(NG):
                act.wait_ge(centred, g + 1)
                after(act, var_ready, g - 1)
                nc.scalar.activation(square[g % 2][:, :], dst[:, columns(g)], ACT.Square).then_inc(squared, 1)
            act.wait_ge(var_ready, NG)
            nc.scalar.activation(inverse[:, :], var[:, 0:GT], ACT.Sqrt, bias=G["eps"][:, :]).then_inc(std_ready, 1)
            if gain is not None:
                for g in range(NG):
                    act.wait_ge(normed, g + 1)
                    nc.scalar.activation(dst[:, columns(g)], dst[:, columns(g)], ACT.Identity, bias=shift, scale=gain).then_inc(scaled, 1)

        @block.vector
        def _(dve):
            for g in range(NG):
                dve.wait_ge(mean_ready, g + 1)
                nc.vector.tensor_tensor(dst[:, columns(g)], src[:, columns(g)], mean[g % 2][:, 0:GT],
                                        ALU.subtract).then_inc(centred, 1)
            dve.wait_ge(std_ready, 1)
            nc.vector.reciprocal(inverse[:, :], inverse[:, :]).then_inc(inverted, 1)
            for g in range(NG):
                dve.wait_ge(spread, g + 1)
                nc.vector.tensor_tensor(dst[:, columns(g)], dst[:, columns(g)], back[g % 2][:, 0:GT],
                                        ALU.mult).then_inc(normed, 1)


def top2_weights(nc, name, G, xn, router, router_b, n_shared, normalise, combT):
    E = 8
    EW = E + n_shared
    with Stage(nc, name) as st:
        w_sb = st.sb("router", [128, E])
        rb = st.sb("router_b", [S, E])
        logit_ps = st.ps("logit", [S, BANK])
        turn = [st.ps(f"turn{j}", [EW, BANK]) for j in range(2)]
        logit = st.sb("logits", [S, B, E])
        mx = st.sb("mx", [S, B])
        prob = st.sb("prob", [S, B, E])
        tot = st.sb("tot", [S, B])
        pair = st.sb("pair", [S, B, E, E])
        tie = st.sb("tie", [S, B, E, E])
        rank = st.sb("rank", [S, B, E])
        comb = st.sb("comb", [S, B, EW])
        earlier = st.sb("earlier", [S, E, E])
        loaded, logits_ready, dve_chain, shifted, exp_done, comb_ready, turned, stored = (
            st.sem(n) for n in ("loaded", "logits_ready", "dve_chain", "shifted", "exp_done", "comb_ready", "turned", "stored"))
        block = st.ctx.enter_context(nc.Block())

        @block.sync
        def _(sp):
            sp.dma_start(w_sb[:, :], router).then_inc(loaded, 16)
            sp.dma_start(earlier[:, :, :], G["earlier_dram"]).then_inc(loaded, 16)
            if router_b is not None:
                sp.dma_start(rb[:, :], router_b.partition_broadcast(S)).then_inc(loaded, 16)

        @block.tensor
        def _(pe):
            pe.wait_ge(loaded, 48 if router_b is not None else 32)
            for b in range(B):
                last = nc.tensor.matmul(logit_ps[:, b * E:(b + 1) * E], xn[:, b * S:(b + 1) * S], w_sb[:, :],
                                        start=True, stop=True)
            last.then_inc(logits_ready, 1)
            pe.wait_ge(comb_ready, 1)
            for g in range(NG):
                if g >= 2:
                    pe.wait_ge(stored, g - 1)
                for k in range(GB):
                    last = nc.tensor.transpose(turn[g % 2][:, k * S:(k + 1) * S], comb[:, g * GB + k, :],
                                               G["ident"][0:S, 0:S])
                last.then_inc(turned, 1)

        @block.scalar
        def _(act):
            act.wait_ge(shifted, 1)
            nc.scalar.activation(prob[:, :, :], logit[:, :, :], ACT.Exp).then_inc(exp_done, 1)
            for g in range(NG):
                act.wait_ge(turned, g + 1)
                nc.scalar.activation(combT[0:EW, g * GT:(g + 1) * GT], turn[g % 2][:, 0:GT], ACT.Copy).then_inc(stored, 1)

        @block.vector
        def _(dve):
            link = Link(dve, dve_chain, 11 + 1 + (router_b is not None) + n_shared + 2 * normalise, 0)
            link(nc.vector.memset(combT[:, :], 0.0))
            lp = logit_ps[:, 0:B * E].rearrange("p (b e) -> p b e", e=E)
            dve.wait_ge(logits_ready, 1)
            src = lp
            if router_b is not None:
                link(nc.vector.tensor_tensor(logit[:, :, :], lp, rb[:, :].unsqueeze(1).to_broadcast([S, B, E]), ALU.add))
                src = logit[:, :, :]
            link(nc.vector.tensor_reduce(mx[:, :], src, AX.X, ALU.max))
            nc.vector.tensor_tensor(logit[:, :, :], src, mx[:, :].unsqueeze(2).to_broadcast([S, B, E]),
                                    ALU.subtract).then_inc(shifted, 1)
            dve.wait_ge(exp_done, 1)
            link(nc.vector.tensor_reduce(tot[:, :], prob[:, :, :], AX.X, ALU.add))
            link(nc.vector.reciprocal(mx[:, :], tot[:, :]))
            link(nc.vector.tensor_tensor(prob[:, :, :], prob[:, :, :], mx[:, :].unsqueeze(2).to_broadcast([S, B, E]), ALU.mult))

            def other(b):
                return prob[:, b, :].unsqueeze(1).to_broadcast([S, E, E])

            def own(b):
                return prob[:, b, :].unsqueeze(2).to_broadcast([S, E, E])

            for b in range(B):
                a = nc.vector.tensor_tensor(pair[:, b, :, :], other(b), own(b), ALU.is_gt)
                c = nc.vector.tensor_tensor(tie[:, b, :, :], other(b), own(b), ALU.is_equal)
            link(c)
            link(nc.vector.tensor_tensor(tie[:, :, :, :].rearrange("p b e f -> p b (e f)"),
                                         tie[:, :, :, :].rearrange("p b e f -> p b (e f)"),
                                         earlier[:, :, :].rearrange("p e f -> p (e f)").unsqueeze(1).to_broadcast([S, B, E * E]),
                                         ALU.mult))
            link(nc.vector.tensor_tensor(pair[:, :, :, :], pair[:, :, :, :], tie[:, :, :, :], ALU.add))
            link(nc.vector.tensor_reduce(rank[:, :, :], pair[:, :, :, :], AX.X, ALU.add))
            link(nc.vector.tensor_scalar(rank[:, :, :], rank[:, :, :], 1.5, None, ALU.is_lt))
            link(nc.vector.tensor_tensor(comb[:, :, 0:E], rank[:, :, :], prob[:, :, :], ALU.mult))
            if normalise:
                link(nc.vector.tensor_reduce(tot[:, :], comb[:, :, 0:E], AX.X, ALU.add))
                link(nc.vector.reciprocal(mx[:, :], tot[:, :]))
                link(nc.vector.tensor_tensor(comb[:, :, 0:E], comb[:, :, 0:E], mx[:, :].unsqueeze(2).to_broadcast([S, B, E]), ALU.mult))
            else:
                link(nc.vector.tensor_copy(tot[:, :], mx[:, :]))
            if n_shared:
                link(nc.vector.memset(comb[:, :, E:EW], 1.0))
            nc.vector.tensor_copy(mx[:, :], tot[:, :]).then_inc(comb_ready, 1)
            link.end()


def experts_ffn(nc, name, G, xT, xn, combT, w1, w2, n_exp, n_hidden, gated, b1, b2):
    HC = n_hidden // 128
    UNITS = n_exp * HC
    cols = 2 * n_hidden if gated else n_hidden
    with Stage(nc, name) as st:
        w1_sb = st.sb("w1", [128, n_exp, cols])
        w2_sb = st.sb("w2", [128, n_exp, HC, D])
        b1_sb = st.sb("b1", [128, n_exp * HC])
        b2_sb = st.sb("b2", [128, D])
        pick = st.sb("pick", [128, n_exp, 128])
        gate_ps = [st.ps(f"gate{j}", [128, BANK]) for j in range(2)]
        up_ps = [st.ps(f"up{j}", [128, BANK]) for j in range(2)] if gated else None
        wt_ps = [st.ps(f"wt{j}", [128, BANK]) for j in range(2)]
        out_ps = st.ps("out", [128, BANK])
        acted = [st.sb(f"acted{j}", [128, GT]) for j in range(2)]
        prod = [st.sb(f"prod{j}", [128, GT]) for j in range(2)]
        hid = [st.sb(f"hid{j}", [128, GT]) for j in range(2)]
        loaded, hid_in, wt_ready, act_done, prod_done, hid_ready, hid_used, out_ready, out_added = (
            st.sem(n) for n in ("loaded", "hid_in", "wt_ready", "act_done", "prod_done", "hid_ready", "hid_used",
                                "out_ready", "out_added"))
        loads = [(w1_sb[:, :, :], w1), (w2_sb[:, :, :, :], w2), (pick[:, :, :], G["pick_dram"][:, 0:n_exp, :])]
        if b1 is not None:
            loads += [(b1_sb[:, :], b1), (b2_sb[0:n_exp, :], b2)]
        cleared = st.sem("cleared")
        block = st.ctx.enter_context(nc.Block())

        @block.sync
        def _(sp):
            sp.wait_ge(cleared, 1)
            for dst, src in loads:
                sp.dma_start(dst, src).then_inc(loaded, 16)

        @block.tensor
        def _(pe):
            pe.wait_ge(loaded, 16 * len(loads))
            def group(g):
                x = xn[:, bass.ds(g * GT, GT)]

                def project(u):
                    e, c = u // HC, u % HC
                    j = u % 2
                    if c == 0:
                        after(pe, hid_ready, g * UNITS + (e - 1) * HC if e >= 2 else g * UNITS)
                        nc.tensor.matmul(wt_ps[e % 2][:, 0:GT], pick[:, e, :], combT[:, bass.ds(g * GT, GT)],
                                         start=True, stop=True).then_inc(wt_ready, 1)
                    after(pe, act_done, g * UNITS + max(u - 1, 0))
                    m = nc.tensor.matmul(gate_ps[j][:, 0:GT], w1_sb[:, e, c * 128:(c + 1) * 128], x, start=True, stop=True)
                    if gated:
                        after(pe, prod_done, g * UNITS + max(u - 1, 0))
                        m = nc.tensor.matmul(up_ps[j][:, 0:GT], w1_sb[:, e, n_hidden + c * 128:n_hidden + (c + 1) * 128],
                                             x, start=True, stop=True)
                    m.then_inc(hid_in, 1)

                def reduce(u):
                    e, c = u // HC, u % HC
                    if u == 0:
                        after(pe, out_added, g)
                        if b2 is not None:
                            nc.tensor.matmul(out_ps[:, 0:GT], b2_sb[:, :], combT[:, bass.ds(g * GT, GT)], start=True, stop=False)
                    pe.wait_ge(hid_ready, g * UNITS + u + 1)
                    m = nc.tensor.matmul(out_ps[:, 0:GT], w2_sb[:, e, c, :], hid[u % 2][:, :],
                                         start=(u == 0 and b2 is None), stop=(u == UNITS - 1))
                    m.then_inc(hid_used, 1)

                project(0)
                for u in range(1, UNITS):
                    project(u)
                    reduce(u - 1)
                reduce(UNITS - 1)

            group(0)
            with pe.Fori(1, NG) as g:
                group(g)

        @block.scalar
        def _(act):
            act.wait_ge(loaded, 16 * len(loads))
            def group(g):
                for u in range(UNITS):
                    act.wait_ge(hid_in, g * UNITS + u + 1)
                    after(act, prod_done if gated else hid_ready, g * UNITS + max(u - 1, 0))
                    if gated:
                        i = nc.scalar.activation(acted[u % 2][:, :], gate_ps[u % 2][:, 0:GT], ACT.Silu)
                    else:
                        i = nc.scalar.activation(acted[u % 2][:, :], gate_ps[u % 2][:, 0:GT], ACT.Gelu_apprx_tanh,
                                                 bias=b1_sb[:, u:u + 1])
                    i.then_inc(act_done, 1)

            group(0)
            with act.Fori(1, NG) as g:
                group(g)

        @block.vector
        def _(dve):
            nc.vector.memset(b2_sb[:, :], 0.0).then_inc(cleared, 1)
            def group(g):
                for u in range(UNITS):
                    j, e = u % 2, u // HC
                    dve.wait_ge(act_done, g * UNITS + u + 1)
                    src = acted[j]
                    if gated:
                        after(dve, hid_ready, g * UNITS + max(u - 1, 0))
                        nc.vector.tensor_tensor(prod[j][:, :], acted[j][:, :], up_ps[j][:, 0:GT], ALU.mult).then_inc(prod_done, 1)
                        dve.wait_ge(prod_done, g * UNITS + u + 1)
                        src = prod[j]
                    dve.wait_ge(wt_ready, g * n_exp + e + 1)
                    after(dve, hid_used, g * UNITS + max(u - 1, 0))
                    nc.vector.tensor_tensor(hid[j][:, :], src[:, :], wt_ps[e % 2][:, 0:GT], ALU.mult).then_inc(hid_ready, 1)
                dve.wait_ge(hid_used, (g + 1) * UNITS)
                part = bass.ds(g * GT, GT)
                nc.vector.tensor_tensor(xT[:, part], xT[:, part], out_ps[:, 0:GT], ALU.add).then_inc(out_added, 1)
                dve.wait_ge(out_added, g + 1)

            group(0)
            with dve.Fori(1, NG) as g:
                group(g)


def stage_ffn0(nc, G, I):
    layer_norm(nc, "s2ln", G, G["xT"], G["xn"])
    with nc.sbuf_tensor("s2_comb", [128, TOK], F32) as combT:
        top2_weights(nc, "s2r", G, G["xn"], I["L0_ffn_router_w"], None, 0, 0, combT)
        experts_ffn(nc, "s2f", G, G["xT"], G["xn"], combT, I["L0_ffn_w1"], I["L0_ffn_w2"], 8, 256, True, None, None)


def stage_ffn1(nc, G, I):
    layer_norm(nc, "s5ln", G, G["xT"], G["xn"])
    with nc.sbuf_tensor("s5_comb", [128, TOK], F32) as combT:
        top2_weights(nc, "s5r", G, G["xn"], I["L1_ffn_router_w"], I["L1_ffn_router_b"], 1, 1, combT)
        experts_ffn(nc, "s5f", G, G["xT"], G["xn"], combT, I["L1_ffn_w1"], I["L1_ffn_w2"], 9, 512, False,
                    I["L1_ffn_b1"], I["L1_ffn_b2"])


KC = 128
NCH = -(-S2 // KC)
LAST = S2 - (NCH - 1) * KC
SEG = 482
SEGS = [(n * SEG, min(SEG, S2 - n * SEG)) for n in range(3)]
TERMS = [(0, 0), (0, 1), (1, 0), (1, 1), (0, 2), (2, 0)]
TWO_ONES = float(np.array([0x3F803F80], np.uint32).view(np.float32)[0])
NEVER = -1e30
MASKED = -float(2 ** 51)


def cross_attention(nc, name, G, I, acc, src, H, wq, bq, wk, bk, wv, bv, wo, bo, masked):
    d = D // H
    RQ = len(TERMS) * d
    SR = 96
    RS = SR + 3
    NE = H * NCH // 8
    NQ = H // 4
    RU = 6 + 3 * H
    VU = 3
    KU = RU - 3
    TAIL = 3
    FULL = S2 if len(TERMS) * d == SR else 0
    CLEARS = 11
    scale = 1.0 / float(np.sqrt(d))
    with Stage(nc, name) as st:
        wk_sb, wv_sb, wo_sb = (st.sb(n, [128, D]) for n in ("wk", "wv", "wo"))
        bias = st.sb("bias", [128, 4])
        bv_sb = st.sb("bv", [128, D])
        kst = [st.sb(f"kst{j}", [RS, H, NCH * KC], BF16) for j in range(2)]
        v1_all = [st.sb(f"v{j}", [KC, NCH * H * (d + 1) + 32]) for j in range(2)]
        v1 = [v[:, 0:NCH * H * (d + 1)].rearrange("p (c h f) -> p c h f", c=NCH, h=H) for v in v1_all]
        qst = [st.sb(f"qst{j}", [RS, H, S], BF16) for j in range(2)]
        spart_all = st.sb("spart", [S, 128], BF16)
        with Stage(nc, name + "q") as sq:
            wq_sb = sq.sb("wq", [128, D])
            q_ps = [sq.ps(f"ps{j}", [128, BANK]) for j in range(2)]
            q = sq.sb("q", [128, TOK])
            qpart = [sq.sb(f"q{n}", [128, TOK], BF16) for n in range(3)]
            q_out = sq.sem("q_out")
            loaded, q_ready, q_copied, part_done = (sq.sem(n) for n in ("loaded", "q_ready", "q_copied", "part_done"))
            loads = [(wq_sb[:, :], wq), (wk_sb[:, :], wk), (wv_sb[:, :], wv), (wo_sb[:, :], wo)]
            if bq is not None:
                loads += [(bias[:, 0:1], bq), (bias[:, 1:2], bk), (bias[:, 2:3], bo), (bv_sb[:, :], bv.partition_broadcast(128))]
            pads_set, cleared = sq.sem("pads_set"), sq.sem("cleared")
            block = sq.ctx.enter_context(nc.Block())

            @block.gpsimd
            def _(pool):
                link = Link(pool, pads_set, 6, 0)
                for j in range(2):
                    if FULL:
                        link(nc.gpsimd.memset(kst[j][0:SR, :, FULL:NCH * KC], 0.0))
                    else:
                        link(nc.gpsimd.memset(kst[j][0:SR, :, :].rearrange("p h n -> p (h n)").bitcast(F32), 0.0))
                    link(nc.gpsimd.memset(kst[j][SR:RS, :, 0:S2].bitcast(F32), TWO_ONES))
                    link(nc.gpsimd.memset(kst[j][SR:RS, :, S2:NCH * KC], 0.0))
                link.end()

            @block.sync
            def _(sp):
                for dst, s in loads:
                    sp.dma_start(dst, s).then_inc(loaded, 16)
                sp.wait_ge(loaded, 16 * len(loads))
                sp.wait_ge(part_done, 5 * NG)
                for n in range(3):
                    sp.dma_start(G["q_dram"][n], qpart[n][:, :]).then_inc(q_out, 16)
                sp.wait_ge(q_out, 48)

            @block.tensor
            def _(pe):
                pe.wait_ge(loaded, 16 * len(loads))
                for g in range(NG):
                    after(pe, q_copied, g - 1)
                    nc.tensor.matmul(q_ps[g % 2][:, 0:GT], wq_sb[:, :], src[:, g * GT:(g + 1) * GT],
                                     start=True, stop=True).then_inc(q_ready, 1)

            @block.vector
            def _(dve):
                dve.wait_ge(loaded, 16 * len(loads))
                for g in range(NG):
                    part = slice(g * GT, (g + 1) * GT)
                    dve.wait_ge(q_ready, g + 1)
                    if bq is not None:
                        nc.vector.tensor_scalar(q[:, part], q_ps[g % 2][:, 0:GT], bias[:, 0:1], None, ALU.add).then_inc(q_copied, 1)
                    else:
                        nc.vector.tensor_copy(q[:, part], q_ps[g % 2][:, 0:GT]).then_inc(q_copied, 1)
                    dve.wait_ge(q_copied, g + 1)
                    nc.vector.tensor_copy(qpart[0][:, part], q[:, part]).then_inc(part_done, 1)
                    dve.wait_ge(part_done, 5 * g + 1)
                    nc.vector.tensor_tensor(q[:, part], q[:, part], qpart[0][:, part], ALU.subtract).then_inc(part_done, 1)
                    dve.wait_ge(part_done, 5 * g + 2)
                    nc.vector.tensor_copy(qpart[1][:, part], q[:, part]).then_inc(part_done, 1)
                    dve.wait_ge(part_done, 5 * g + 3)
                    nc.vector.tensor_tensor(q[:, part], q[:, part], qpart[1][:, part], ALU.subtract).then_inc(part_done, 1)
                    dve.wait_ge(part_done, 5 * g + 4)
                    nc.vector.tensor_copy(qpart[2][:, part], q[:, part]).then_inc(part_done, 1)
                link = Link(dve, cleared, CLEARS, 0)
                for j in range(2):
                    link(nc.vector.memset(qst[j][0:SR, :, :], 0.0))
                    link(nc.vector.memset(v1_all[j][:, :], 1.0))
                    link(nc.vector.memset(v1[j][:, NCH - 1, :, :], 0.0))
                    link(nc.vector.memset(v1[j][0:32, NCH - 1, :, d:d + 1], 1.0))
                    link(nc.vector.memset(v1[j][32:LAST, NCH - 1, :, d:d + 1], 1.0))
                link(nc.vector.memset(spart_all[:, :], 0.0))
                link.end()

        ctx = [st.sb(f"ctx{j}", [128, S2]) for j in range(2)]
        k = st.sb("k", [128, S2])
        krest = st.sb("krest", [128, S2])
        kpart = [st.sb(f"k{n}", [128, S2], BF16) for n in range(3)]
        p = [st.sb(f"p{j}", [KC, 2, 4 * S]) for j in range(3)]
        seg_max = st.sb("seg_max", [S, H, 3])
        shift = st.sb("shift", [S, H])
        srest = st.sb("srest", [S, H])
        spart = spart_all[:, 0:3 * H].rearrange("p (a h) -> p a h", a=3)
        shiftT = st.sb("shiftT", [3 * H, S], BF16)
        inv = st.sb("inv", [S, H])
        z = st.sb("z", [S, D])
        zT = st.sb("zT", [128, S])
        zraw = st.sb("zraw", [128, 4 * S])
        if masked:
            mask8 = st.sb("mask8", [S, S2], U8)
            mask8T = st.sb("mask8T", [KC, NCH, S], U8)
            maskb = st.sb("maskb", [S, S2], BF16)
            maskbT = [st.sb(f"maskbT{j}", [KC, NCH, S], BF16) for j in range(2)]
            junk = [st.sb(f"junk{j}", [S, SEG]) for j in range(2)]
        ring = [st.ps(f"ring{j}", [128, BANK]) for j in range(2)]
        sc = [st.ps(f"sc{j}", [128, 2, BANK]) for j in range(2)]
        zps = st.ps("zps", [128, BANK])
        misc = st.ps("misc", [128, BANK])
        shiftT_ps = misc[:, 0:S // 2].bitcast(BF16)
        zT_ps, o_ps = misc[:, 128:128 + S], misc[:, 256:256 + S]
        (ring_full, ring_read, k_used, part_ready, qst_in, shift_step, shift_turned, shiftT_done,
         shift_in, sc_full, exp_done, pv_done, z_step, z_turned, zT_done, o_full, o_added, mask_done, kpart_out, zraw_done, zraw_turned) = (
            st.sem(n) for n in ("ring_full", "ring_read", "k_used", "part_ready", "qst_in",
                                "shift_step", "shift_turned", "shiftT_done", "shift_in", "sc_full", "exp_done", "pv_done",
                                "z_step", "z_turned", "zT_done", "o_full", "o_added", "mask_done", "kpart_out", "zraw_done", "zraw_turned"))
        block = st.ctx.enter_context(nc.Block())

        ctx_in = [st.sem(f"ctx_in{j}") for j in range(2)]
        kst_in = [st.sem(f"kst_in{n}") for n in range(NQ)]
        mask_in = st.sem("mask_in")

        passed = [st.sem(f"passed{n}") for n in range(3)]

        def ctx_loads(b, j):
            return 8 * (b - j) + 16

        def has_keys(t):
            return not (isinstance(t, int) and t >= B - 2)

        def skipped(t):
            return 3 if isinstance(t, int) and t == B - 1 else 0

        def ring_no(t, u):
            return 6 + t * RU + u - skipped(t)

        def keys_copied(b):
            return 3 * (b + 1) if isinstance(b, int) and b < 2 else ring_no(b - 2, RU)

        def bank_of(t, u):
            return ring[(u + skipped(t)) % 2]

        def slot_units(t, g, quarters=(0, 1, 2, 3)):
            if g >= NE - TAIL:
                u = KU + g - (NE - TAIL)
                return [u] if has_keys(t) and u < RU and 2 in quarters else []
            steps = 4 * (NE - TAIL)
            return [x for q in quarters for x in range((4 * g + q) * KU // steps, (4 * g + q + 1) * KU // steps)]

        def batches(eng, body):
            body(0, 0, True, False)
            with eng.Fori(0, (B - 4) // 2) as i:
                body(2 * i + 1, 1, True, True)
                body(2 * i + 2, 0, True, True)
            body(B - 3, 1, True, True)
            body(B - 2, 0, True, True)
            body(B - 1, 1, False, True)

        @block.sync
        def _(sp):
            def load_ctx(b, j):
                if not (isinstance(b, int) and b < 2):
                    sp.wait_ge(ring_full, ring_no(b - 2, VU))
                    sp.sem_inc(passed[2], 1)
                sp.dma_start(ctx[j][:, :], I["ctxT"][bass.ds(b, 1), :, :].rearrange("a p n -> p (a n)")).then_inc(ctx_in[j], 16)

            def load_masks(b):
                if masked:
                    after(sp, mask_done, 2 * b)
                    sp.sem_inc(passed[2], 1)
                    sp.dma_start(mask8[:, :], I["mask"][bass.ds(b, 1), :, :].rearrange("a p n -> p (a n)")).then_inc(mask_in, 16)
                    sp.dma_start(mask8T[:, :, :], I["maskT"][bass.ds(b, 1), :, :, :].rearrange("a p c n -> p (a c) n")).then_inc(mask_in, 16)

            def put_parts(b, j):
                for n in range(3):
                    sp.wait_ge(part_ready, 3 * b + n + 1)
                    sp.dma_start(G["k_dram"][j, n], kpart[n][:, :]).then_inc(kpart_out, 16)
                sp.wait_ge(kpart_out, 48 * b + 48)
                sp.sem_inc(passed[2], 1)

            def stack_keys(b, j, quad):
                after(sp, kst_in[quad], 16 * len(TERMS) * b)
                sp.sem_inc(passed[2], 1)
                after(sp, sc_full, (b - 2) * NE + 6 * (quad + 1))
                for t, (_, pk) in enumerate(TERMS):
                    sp.dma_start(kst[j][t * d:(t + 1) * d, 4 * quad:4 * quad + 4, 0:S2],
                                 G["k_dram"][j, pk, 4 * d * quad:4 * d * (quad + 1), :].rearrange("(h f) n -> f h n", f=d)).then_inc(kst_in[quad], 16)

            def stack_queries(b, j):
                after(sp, shiftT_done, b)
                sp.sem_inc(passed[2], 1)
                after(sp, sc_full, (b - 1) * NE)
                sp.sem_inc(passed[2], 1)
                for t, (pq, _) in enumerate(TERMS):
                    sp.dma_start(qst[j][t * d:(t + 1) * d, :, :],
                                 G["q_dram"][pq, :, bass.ds(b * S, S)].rearrange("(h f) n -> f h n", f=d)).then_inc(qst_in, 16)

            def around(t, j, load=True):
                if load:
                    load_ctx(t + 2, j)
                load_masks(t + 1)
                put_parts(t + 1, 1 - j)
                for quad in range(NQ - 1):
                    stack_keys(t + 1, 1 - j, quad)
                stack_queries(t + 1, 1 - j)
                stack_keys(t + 1, 1 - j, NQ - 1)

            load_ctx(0, 0)
            load_ctx(1, 1)
            load_masks(0)
            stack_queries(0, 0)
            put_parts(0, 0)
            for quad in range(NQ):
                stack_keys(0, 0, quad)
            around(0, 0)
            around(1, 1)
            with sp.Fori(0, (B - 4) // 2) as i:
                around(2 * i + 2, 0)
                around(2 * i + 3, 1)
            around(B - 2, 0, load=False)

        @block.tensor
        def _(pe):
            def project_keys(b, j, u, no, bank):
                if u == 0:
                    pe.wait_ge(ctx_in[j], ctx_loads(b, j))
                after(pe, ring_read, no - 1)
                at, n = SEGS[u]
                nc.tensor.matmul(bank[:, 0:n], wk_sb[:, :], ctx[j][:, at:at + n], start=True, stop=True).then_inc(ring_full, 1)

            def ring_unit(t, j, u):
                no, bank = ring_no(t, u), bank_of(t, u)
                if u >= KU:
                    project_keys(t + 2, j, u - KU, no, bank)
                    return
                after(pe, ring_read, no - 1)
                if u < VU:
                    for c in range(4):
                        cc = u * 4 + c
                        n = KC if cc < NCH - 1 else LAST
                        m = nc.tensor.matmul(bank[0:n, c * D:(c + 1) * D], ctx[j][:, cc * KC:cc * KC + n], wv_sb[:, :],
                                             start=True, stop=True)
                else:
                    h, (at, n) = (u - VU) // 3, SEGS[(u - VU) % 3]
                    if u == VU:
                        pe.wait_ge(qst_in, 16 * len(TERMS) * (t + 1))
                    if (u - VU) % 12 == 0:
                        pe.wait_ge(kst_in[h // 4], 16 * len(TERMS) * (t + 1))
                    m = nc.tensor.matmul(bank[0:S, 0:n], qst[j][0:SR, h, :], kst[j][0:SR, h, at:at + n], start=True, stop=True)
                m.then_inc(ring_full, 1)

            def turn_shift(b, j):
                pe.wait_ge(shift_step, 6 * (b + 1))
                nc.tensor.transpose(shiftT_ps, spart_all[:, :], G["ident_bf"][0:S, 0:S]).then_inc(shift_turned, 1)

            def scores(b, j, g, k2):
                if k2 == 0:
                    if g == 0:
                        pe.wait_ge(shift_in, 48 * (b + 1))
                        if masked:
                            pe.wait_ge(mask_done, 2 * (b + 1))
                    after(pe, exp_done, b * NE + g - 1)
                quad, c = g // 6, 2 * (g % 6) + k2
                if masked:
                    nc.tensor.matmul(sc[g % 2][:, k2, 0:4 * S].rearrange("p (h n) -> p h n", n=S), G["ident_bf"][:, :],
                                     maskbT[j][:, c:c + 1, :].to_broadcast([KC, 4, S]), start=True, stop=False,
                                     skip_group_check=True)
                for n in range(4):
                    h = 4 * quad + n
                    m = nc.tensor.matmul(sc[g % 2][:, k2, n * S:(n + 1) * S], kst[j][:, h, c * KC:(c + 1) * KC],
                                         qst[j][:, h, :], start=not masked, stop=True, skip_group_check=masked)
                if k2 == 1:
                    m.then_inc(sc_full, 1)

            def values(b, j, g, k2):
                if k2 == 0:
                    pe.wait_ge(exp_done, b * NE + g + 1)
                    if g == 0:
                        after(pe, z_step, 2 * b)
                        pe.wait_ge(ring_read, ring_no(b, VU))
                quad, c = g // 6, 2 * (g % 6) + k2
                for n in range(4):
                    at = (c * H + 4 * quad + n) * (d + 1)
                    m = nc.tensor.matmul(zps[32 * n:32 * n + 32, quad * S:(quad + 1) * S], v1_all[j][:, at:at + 32],
                                         p[g % 3][:, k2, n * S:(n + 1) * S], start=(c == 0), stop=(c == NCH - 1))
                if k2 == 1:
                    m.then_inc(pv_done, 1)

            def turn_sums(b):
                pe.wait_ge(zraw_done, b + 1)
                for quad in range(H // 4):
                    m = nc.tensor.transpose(zps[0:S, quad * 128:(quad + 1) * 128], zraw[:, quad * S:(quad + 1) * S], G["ident"][:, :])
                m.then_inc(zraw_turned, 1)

            def turn_z(b):
                pe.wait_ge(z_step, 2 * (b + 1))
                nc.tensor.transpose(zT_ps, z[:, :], G["ident"][0:S, 0:S]).then_inc(z_turned, 1)

            def project_out(b):
                pe.wait_ge(zT_done, b + 1)
                nc.tensor.matmul(o_ps, wo_sb[:, :], zT[:, :], start=True, stop=True).then_inc(o_full, 1)

            for b in range(2):
                for u in range(3):
                    project_keys(b, b, u, 3 * b + u, ring[(b + u) % 2])
            for u in range(RU):
                ring_unit(0, 0, u)
            turn_shift(0, 0)

            def body(b, j, has_next, has_prev):
                def units(g, quarters):
                    if has_next:
                        for u in slot_units(b + 1, g, quarters):
                            ring_unit(b + 1, 1 - j, u)

                for g in range(NE + 1):
                    if g == 0:
                        units(g, (0, 1, 2, 3))
                    for k2 in range(2):
                        if g:
                            units(g, (k2,))
                        if g < NE:
                            scores(b, j, g, k2)
                    if has_prev and g == 0:
                        turn_sums(b - 1)
                    if has_next and g == NE - TAIL + 1:
                        turn_shift(b + 1, 1 - j)
                    for k2 in range(2):
                        if g:
                            units(g, (2 + k2,))
                            values(b, j, g - 1, k2)
                    if has_prev and g == 2:
                        turn_z(b - 1)
                    if has_prev and g == 3:
                        project_out(b - 1)

            batches(pe, body)
            turn_sums(B - 1)
            turn_z(B - 1)
            project_out(B - 1)

        @block.scalar
        def _(act):
            def part(b, n):
                after(act, kpart_out, 48 * b)
                if n == 0:
                    act.wait_ge(ring_read, keys_copied(b))
                    nc.scalar.activation(kpart[0][:, :], k[:, :], ACT.Copy).then_inc(part_ready, 1)
                else:
                    act.wait_ge(k_used, 2 * b + 1)
                    nc.scalar.activation(kpart[1][:, :], krest[:, :], ACT.Copy).then_inc(part_ready, 1)

            def copy_shift(b, j):
                act.wait_ge(shift_turned, b + 1)
                after(act, shift_in, 48 * b)
                nc.scalar.activation(shiftT[:, :], shiftT_ps[0:3 * H, :], ACT.Copy).then_inc(shiftT_done, 1)
                act.wait_ge(shiftT_done, b + 1)
                for n in range(3):
                    act.dma_start(qst[j][SR + n:SR + n + 1, :, :], shiftT[n * H:(n + 1) * H, :]).then_inc(shift_in, 16)

            def copy_z(b):
                act.wait_ge(z_turned, b + 1)
                nc.scalar.activation(zT[:, :], zT_ps, ACT.Copy).then_inc(zT_done, 1)

            for b in range(2):
                part(b, 0)
                part(b, 1)
            copy_shift(0, 0)

            def copy_sums(b):
                act.wait_ge(pv_done, (b + 1) * NE)
                n = H // 4 * S
                nc.scalar.activation(zraw[:, 0:n], zps[:, 0:n], ACT.Copy).then_inc(zraw_done, 1)

            def body(b, j, has_next, has_prev):
                if has_prev:
                    copy_sums(b - 1)
                for g in range(NE):
                    act.wait_ge(sc_full, b * NE + g + 1)
                    after(act, pv_done, b * NE + g - 2)
                    nc.scalar.activation(p[g % 3][:, :, :], sc[g % 2][:, :, 0:4 * S], ACT.Exp, scale=scale).then_inc(exp_done, 1)
                    if has_prev and g == 2:
                        copy_z(b - 1)
                    if has_keys(b) and g == 1:
                        part(b + 2, 0)
                    if has_keys(b) and g == 4:
                        part(b + 2, 1)
                    if has_next and g == NE - TAIL + 1:
                        copy_shift(b + 1, 1 - j)

            batches(act, body)
            copy_sums(B - 1)
            copy_z(B - 1)

        @block.gpsimd
        def _(pool):
            def rest(b):
                pool.wait_ge(part_ready, 3 * b + 1)
                nc.gpsimd.tensor_tensor(krest[:, :], k[:, :], kpart[0][:, :], ALU.subtract).then_inc(k_used, 1)
                pool.wait_ge(part_ready, 3 * b + 2)
                pool.wait_ge(k_used, 2 * b + 1)
                after(pool, kpart_out, 48 * b)
                nc.gpsimd.tensor_tensor(kpart[2][:, :], krest[:, :], kpart[1][:, :], ALU.subtract).then_inc(part_ready, 1)
                pool.wait_ge(part_ready, 3 * b + 3)
                pool.sem_inc(k_used, 1)

            def masks(b, j):
                pool.wait_ge(mask_in, 32 * (b + 1))
                if not (isinstance(b, int) and b == 0):
                    pool.wait_ge(ring_read, ring_no(b - 1, KU))
                pool.sem_inc(passed[1], 1)
                nc.gpsimd.tensor_scalar(maskb[:, :], mask8[:, :], MASKED, None, ALU.mult).then_inc(mask_done, 1)
                after(pool, sc_full, (b - 1) * NE)
                pool.sem_inc(passed[1], 1)
                nc.gpsimd.tensor_scalar(maskbT[j][:, :, :], mask8T[:, :, :], MASKED, None, ALU.mult).then_inc(mask_done, 1)

            rest(0)
            if masked:
                masks(0, 0)
            rest(1)

            def body(b, j, has_next, has_prev):
                if has_next:
                    if masked:
                        masks(b + 1, 1 - j)
                    if has_keys(b):
                        rest(b + 2)

            batches(pool, body)

        @block.vector
        def _(dve):
            def copy_keys(b, u, no, bank):
                dve.wait_ge(ring_full, no + 1)
                at, n = SEGS[u]
                after(dve, k_used, 2 * b)
                if bk is not None:
                    nc.vector.tensor_scalar(k[:, at:at + n], bank[:, 0:n], bias[:, 1:2], None, ALU.add).then_inc(ring_read, 1)
                else:
                    nc.vector.tensor_copy(k[:, at:at + n], bank[:, 0:n]).then_inc(ring_read, 1)

            def ring_unit(b, j, u):
                no, bank = ring_no(b, u), bank_of(b, u)
                if u >= KU:
                    copy_keys(b + 2, u - KU, no, bank)
                    return
                dve.wait_ge(ring_full, no + 1)
                if u < VU:
                    if u == 0:
                        after(dve, pv_done, (b - 1) * NE)
                    c0 = u * 4
                    for n, c1, c2 in ((KC, 0, 3), (LAST, 3, 4)) if u == VU - 1 else ((KC, 0, 4),):
                        dst = v1[j][0:n, c0 + c1:c0 + c2, :, 0:d].rearrange("p c h f -> p (c h) f")
                        s = bank[0:n, c1 * D:c2 * D].rearrange("p (x f) -> p x f", f=d)
                        if bv is not None:
                            for c in range(c1, c2):
                                m = nc.vector.tensor_tensor(v1[j][0:n, c0 + c, :, 0:d], bank[0:n, c * D:(c + 1) * D].rearrange("p (h f) -> p h f", f=d),
                                                            bv_sb[0:n, :].rearrange("p (h f) -> p h f", f=d), ALU.add)
                        else:
                            m = nc.vector.tensor_copy(dst, s)
                else:
                    h, sg = (u - VU) // 3, (u - VU) % 3
                    at, n = SEGS[sg]
                    if u == VU:
                        after(dve, shift_step, 6 * b)
                    if masked:
                        if u == VU:
                            dve.wait_ge(mask_done, 2 * b + 1)
                        dve.wait_ge(ring_read, no - 1)
                        dve.sem_inc(passed[0], 1)
                        m = nc.vector.tensor_tensor_reduce(junk[u % 2][:, 0:n], bank[0:S, 0:n], maskb[:, at:at + n], 1.0, -3.0e38,
                                                           ALU.add, ALU.max, seg_max[:, h, sg:sg + 1])
                    else:
                        m = nc.vector.tensor_reduce(seg_max[:, h, sg:sg + 1], bank[0:S, 0:n], AX.X, ALU.max)
                m.then_inc(ring_read, 1)

            def make_shift(b):
                dve.wait_ge(ring_read, ring_no(b, KU))
                after(dve, shift_turned, b)
                nc.vector.tensor_reduce(shift[:, :], seg_max[:, :, :], AX.X, ALU.max, negate=True).then_inc(shift_step, 1)
                dve.wait_ge(shift_step, 6 * b + 1)
                nc.vector.tensor_copy(spart[:, 0, :], shift[:, :]).then_inc(shift_step, 1)
                dve.wait_ge(shift_step, 6 * b + 2)
                nc.vector.tensor_tensor(srest[:, :], shift[:, :], spart[:, 0, :], ALU.subtract).then_inc(shift_step, 1)
                dve.wait_ge(shift_step, 6 * b + 3)
                nc.vector.tensor_copy(spart[:, 1, :], srest[:, :]).then_inc(shift_step, 1)
                dve.wait_ge(shift_step, 6 * b + 4)
                nc.vector.tensor_tensor(shift[:, :], srest[:, :], spart[:, 1, :], ALU.subtract).then_inc(shift_step, 1)
                dve.wait_ge(shift_step, 6 * b + 5)
                nc.vector.tensor_copy(spart[:, 2, :], shift[:, :]).then_inc(shift_step, 1)

            def normalise(b):
                dve.wait_ge(zraw_turned, b + 1)
                zv = zps[0:S, 0:H * 32].rearrange("p (h f) -> p h f", f=32)
                nc.vector.reciprocal(inv[:, :].unsqueeze(2), zv[:, :, d:d + 1]).then_inc(z_step, 1)
                dve.wait_ge(z_step, 2 * b + 1)
                nc.vector.tensor_tensor(z[:, :].rearrange("p (h f) -> p h f", f=d), zv[:, :, 0:d],
                                        inv[:, :].unsqueeze(2).to_broadcast([S, H, d]), ALU.mult).then_inc(z_step, 1)

            def add_out(b):
                dve.wait_ge(o_full, b + 1)
                part = acc[:, bass.ds(b * S, S)]
                if bo is not None:
                    nc.vector.scalar_tensor_tensor(out=part, in0=o_ps, scalar=bias[:, 2:3], in1=part,
                                                   op0=ALU.add, op1=ALU.add).then_inc(o_added, 1)
                else:
                    nc.vector.tensor_tensor(part, part, o_ps, ALU.add).then_inc(o_added, 1)

            for b in range(2):
                for u in range(3):
                    copy_keys(b, u, 3 * b + u, ring[(b + u) % 2])
            for u in range(KU):
                ring_unit(0, 0, u)
            make_shift(0)
            for u in range(KU, RU):
                ring_unit(0, 0, u)

            def body(b, j, has_next, has_prev):
                for g in range(NE):
                    if has_next and g == NE - TAIL:
                        make_shift(b + 1)
                    if has_next:
                        for u in slot_units(b + 1, g):
                            ring_unit(b + 1, 1 - j, u)
                    if has_prev and g == 0:
                        normalise(b - 1)
                    if has_prev and g == 3:
                        add_out(b - 1)

            batches(dve, body)
            normalise(B - 1)
            add_out(B - 1)


def stage_cross0(nc, G, I):
    layer_norm(nc, "s1ln", G, G["xT"], G["xn"])
    wq = I["L0_xattn_Wq"]
    cross_attention(nc, "s1x", G, I, G["xT"], G["xn"], 16, wq, None, wq, None, wq, None, I["L0_xattn_Wo"], None, False)


def stage_cross1(nc, G, I):
    layer_norm(nc, "s4ln", G, G["xT"], G["xn"])
    w = {n: I["L1_xattn_" + n] for n in ("Wq", "bq", "Wk", "bk", "Wv", "bv", "Wo", "bo")}
    cross_attention(nc, "s4x", G, I, G["xT"], G["xn"], 16, w["Wq"], w["bq"], w["Wk"], w["bk"], w["Wv"], w["bv"],
                    w["Wo"], w["bo"], True)


class HeadPlan:

    def __init__(self, d):
        self.d = d
        self.inner = 16 * d
        self.pairs = max(1, self.inner // 128)
        self.per_bank = min(4, self.pairs)
        n = self.pairs // self.per_bank
        nv = max(1, self.inner // BANK)
        self.proj = [("q", c) for c in range(n)] + [("k", c) for c in range(n)] + [("v", c) for c in range(nv)]
        self.n_qk, self.nv, self.nt = 2 * n, nv, n
        self.vw = min(BANK, self.inner)
        self.last_use = []
        for u in range(len(self.proj)):
            m = [x for x in range(u) if x % 2 == u % 2]
            if m:
                self.last_use.append((0, m[-1]))
            else:
                m = [x for x in range(len(self.proj)) if x % 2 == u % 2]
                self.last_use.append((1, m[-1]))


def self_attention(nc, name, G, acc, src, d, wq, wk, wv, wo, bq, bk, bv, bo, mode, table):
    H, NB4 = 16, 4
    plan = HeadPlan(d)
    NU, PAIRS, PB, VW = len(plan.proj), plan.pairs, plan.per_bank, plan.vw
    inner = plan.inner
    scale = 1.0 / float(np.sqrt(d))
    tabled = mode is not None
    WIDE = max(d, 32)
    PER = 128 // WIDE
    OB = H // PER
    ZB = OB // 4
    with Stage(nc, name) as st:
        wq_sb, wk_sb, wv_sb = (st.sb(n, [128, inner]) for n in ("wq", "wk", "wv"))
        wo_sb = st.sb("wo", [128, OB, D])
        bqk = st.sb("bqk", [128, 2, PAIRS])
        bv_sb = st.sb("bv", [S, inner])
        bo_sb = st.sb("bo", [128, 1])
        tab = st.sb("tab", [S, table[1], S]) if tabled else None
        block_mask = st.sb("block_mask", [128, H]) if d == 8 else None
        loads = [(wq_sb[:, :], wq), (wk_sb[:, :], wk), (wv_sb[:, :], wv), (wo_sb[:, :, :], wo)]
        if bq is not None:
            loads += [(bqk[:, 0, :], bq), (bqk[:, 1, :], bk), (bv_sb[:, :], bv.partition_broadcast(S))]
        if bo is not None:
            loads += [(bo_sb[:, :], bo)]
        if tabled:
            loads += [(tab[:, :, :], table[0])]
        if d == 8:
            loads += [(block_mask[:, :], G["block_mask_dram"])]
        xs = st.sb("xs", [128, S])
        qT = st.sb("qT", [128, PAIRS, S])
        kT = st.sb("kT", [128, H, S])
        v = st.sb("v", [S, inner + WIDE - d])
        t = st.sb("t", [S, H, S]) if tabled else None
        pr = st.sb("pr", [S, H, S])
        prT = st.sb("prT", [S, H, S])
        low = st.sb("low", [S, H])
        tot = st.sb("tot", [S, H])
        inv = st.sb("inv", [S, H])
        zT = st.sb("zT", [128, OB, S])
        aps = [st.ps(f"a{j}", [128, BANK]) for j in range(2)]
        bps = [st.ps(f"b{j}", [128, BANK]) for j in range(NB4)]
        cps = [st.ps(f"c{j}", [128, BANK]) for j in range(2)]
        (loaded, xs_ready, proj_full, proj_read, s_full, t_ready, low_ready, exp_done, turned, prT_ready, z_full,
         zT_ready, o_full, o_added, inv_ready, pr_ready) = (
            st.sem(n) for n in ("loaded", "xs_ready", "proj_full", "proj_read", "s_full", "t_ready", "low_ready", "exp_done",
                                "turned", "prT_ready", "z_full", "zT_ready", "o_full", "o_added",
                                "inv_ready", "pr_ready"))
        cleared = st.sem("cleared")
        LOWS = 1 if tabled else 2
        block = st.ctx.enter_context(nc.Block())

        def batches(eng, body):
            body(0, True, False)
            with eng.Fori(1, B - 1) as b:
                body(b, True, True)
            body(B - 1, False, True)

        @block.sync
        def _(sp):
            for dst, s in loads:
                sp.dma_start(dst, s).then_inc(loaded, 16)
            sp.wait_ge(loaded, 16 * len(loads))

        @block.tensor
        def _(pe):
            pe.wait_ge(loaded, 16 * len(loads))

            def project(b, u):
                kind, c = plan.proj[u]
                back, lu = plan.last_use[u]
                after(pe, proj_read, (b - back) * NU + lu + 1)
                bank = aps[u % 2]
                if kind == "v":
                    if c == 0:
                        pe.wait_ge(xs_ready, b + 1)
                    m = nc.tensor.matmul(bank[0:S, 0:VW], xs[:, :], wv_sb[:, c * VW:(c + 1) * VW], start=True, stop=True)
                else:
                    w = wq_sb if kind == "q" else wk_sb
                    for n in range(PB):
                        p = c * PB + n
                        m = nc.tensor.matmul(bank[:, n * S:(n + 1) * S], w[:, p * 128:(p + 1) * 128], src[:, bass.ds(b * S, S)],
                                             start=True, stop=True)
                m.then_inc(proj_full, 1)

            def scores(b, g):
                if g == 0:
                    pe.wait_ge(proj_read, b * NU + plan.n_qk)
                after(pe, prT_ready, (b - 1) * NB4 + g + 1)
                if d == 8:
                    m = nc.tensor.matmul(bps[g][0:S, 0:4 * S], qT[:, 0, :], kT[:, 4 * g:4 * g + 4, :].rearrange("p h n -> p (h n)"),
                                         start=True, stop=True)
                else:
                    for n in range(2):
                        p = 2 * g + n
                        m = nc.tensor.matmul(bps[g][0:S, 2 * n * S:2 * (n + 1) * S], qT[:, p, :],
                                             kT[:, 2 * p:2 * p + 2, :].rearrange("p h n -> p (h n)"), start=True, stop=True)
                m.then_inc(s_full, 1)

            def turn(b, g):
                pe.wait_ge(pr_ready, b * NB4 + g + 1)
                for n in range(4):
                    m = nc.tensor.transpose(bps[g][0:S, n * S:(n + 1) * S], pr[:, 4 * g + n, :], G["ident"][0:S, 0:S])
                m.then_inc(turned, 1)

            def values(b, c):
                if c == 0:
                    pe.wait_ge(proj_read, (b + 1) * NU)
                    after(pe, o_added, b)
                for h in range(c * 4 * PER, (c + 1) * 4 * PER):
                    if h % 4 == 0:
                        pe.wait_ge(prT_ready, b * NB4 + h // 4 + 1)
                    place, block = h % PER, h // PER % 4
                    m = nc.tensor.matmul(cps[c][place * WIDE:(place + 1) * WIDE, block * S:(block + 1) * S],
                                         v[:, h * d:h * d + WIDE], prT[:, h, :], start=True, stop=True)
                m.then_inc(z_full, 1)

            def project_out(b):
                pe.wait_ge(zT_ready, (b + 1) * ZB)
                for p in range(OB):
                    m = nc.tensor.matmul(cps[0][:, 0:S], wo_sb[:, p, :], zT[:, p, :], start=(p == 0), stop=(p == OB - 1))
                m.then_inc(o_full, 1)

            for u in range(NU):
                project(0, u)

            def body(b, has_next, has_prev):
                for g in range(NB4):
                    scores(b, g)
                if has_next:
                    for u in range(plan.n_qk // 2):
                        project(b + 1, u)
                if has_prev:
                    project_out(b - 1)
                if has_next:
                    for u in range(plan.n_qk // 2, plan.n_qk):
                        project(b + 1, u)
                for g in range(NB4):
                    turn(b, g)
                for c in range(ZB):
                    values(b, c)
                if has_next:
                    for u in range(plan.n_qk, NU):
                        project(b + 1, u)

            batches(pe, body)
            project_out(B - 1)

        @block.gpsimd
        def _(pool):
            def copy_x(b):
                after(pool, proj_full, b * NU)
                nc.gpsimd.tensor_copy(xs[:, :], src[:, bass.ds(b * S, S)]).then_inc(xs_ready, 1)

            def divide(b, g):
                pool.wait_ge(inv_ready, b * NB4 + g + 1)
                heads = slice(4 * g, 4 * g + 4)
                nc.gpsimd.tensor_tensor(pr[:, heads, :], pr[:, heads, :], inv[:, heads].unsqueeze(2).to_broadcast([S, 4, S]),
                                        ALU.mult).then_inc(pr_ready, 1)

            def body(b):
                copy_x(b)
                for g in range(NB4):
                    divide(b, g)

            body(0)
            with pool.Fori(1, B) as b:
                body(b)

        @block.scalar
        def _(act):
            def softmax(b, g):
                act.wait_ge(low_ready, (b * NB4 + g + 1) * LOWS)
                after(act, turned, (b - 1) * NB4 + g + 1)
                for n in range(4):
                    h = 4 * g + n
                    if tabled:
                        e = nc.scalar.activation(pr[:, h, :], t[:, h, :], ACT.Exp, bias=low[:, h:h + 1], accum_out=tot[:, h:h + 1])
                    else:
                        e = nc.scalar.activation(pr[:, h, :], bps[g][0:S, n * S:(n + 1) * S], ACT.Exp, bias=low[:, h:h + 1],
                                                 scale=scale, accum_out=tot[:, h:h + 1])
                    e.then_inc(exp_done, 1)

            def copy_turned(b, g):
                act.wait_ge(turned, b * NB4 + g + 1)
                after(act, z_full, b * ZB)
                nc.scalar.activation(prT[:, 4 * g:4 * g + 4, :], bps[g][0:S, 0:4 * S].rearrange("p (h n) -> p h n", n=S),
                                     ACT.Copy).then_inc(prT_ready, 1)

            def copy_z(b):
                for c in range(ZB):
                    act.wait_ge(z_full, b * ZB + c + 1)
                    after(act, o_full, b)
                    nc.scalar.activation(zT[:, 4 * c:4 * c + 4, :], cps[c][:, 0:4 * S].rearrange("p (h n) -> p h n", n=S),
                                         ACT.Copy).then_inc(zT_ready, 1)

            def body(b, has_next, has_prev):
                softmax(b, 0)
                softmax(b, 1)
                softmax(b, 2)
                softmax(b, 3)
                for g in range(NB4):
                    copy_turned(b, g)
                copy_z(b)

            batches(act, body)

        @block.vector
        def _(dve):
            dve.wait_ge(loaded, 16 * len(loads))

            def read_proj(b, u):
                kind, c = plan.proj[u]
                bank = aps[u % 2]
                dve.wait_ge(proj_full, b * NU + u + 1)
                if kind == "v":
                    after(dve, z_full, b * ZB)
                    part = slice(c * VW, (c + 1) * VW)
                    if bv is not None:
                        m = nc.vector.tensor_tensor(v[:, part], bank[0:S, 0:VW], bv_sb[:, part], ALU.add)
                    else:
                        m = nc.vector.tensor_copy(v[:, part], bank[0:S, 0:VW])
                else:
                    after(dve, s_full, b * NB4)
                    ps = bank[:, 0:PB * S].rearrange("p (h n) -> p h n", n=S)
                    if kind == "k" and d == 8:
                        m = nc.vector.tensor_tensor(kT[:, :, :], bank[:, 0:S].unsqueeze(1).to_broadcast([128, H, S]),
                                                    block_mask[:, :].unsqueeze(2).to_broadcast([128, H, S]), ALU.mult)
                    else:
                        blocks = slice(c * PB, (c + 1) * PB)
                        if kind == "q":
                            places = [(slice(0, 128), qT[:, blocks, :])]
                        else:
                            places = [(slice(64 * x, 64 * x + 64), kT[64 * x:64 * x + 64, :, :].rearrange(
                                "p (y two) n -> p y two n", two=2)[:, blocks, x, :]) for x in range(2)]
                        for rows, dst in places:
                            if bq is not None:
                                bias = bqk[rows, 0 if kind == "q" else 1, blocks]
                                m = nc.vector.tensor_tensor(dst, ps[rows], bias.unsqueeze(2).to_broadcast([bias.shape[0], PB, S]), ALU.add)
                            else:
                                m = nc.vector.tensor_copy(dst, ps[rows])
                m.then_inc(proj_read, 1)

            def lowest(b, g):
                dve.wait_ge(s_full, b * NB4 + g + 1)
                after(dve, exp_done, (b - 1) * H + 4 * (g + 1))
                ps = bps[g][0:S, 0:4 * S].rearrange("p (h n) -> p h n", n=S)
                heads = slice(4 * g, 4 * g + 4)
                if tabled:
                    tb = tab[:, heads, :] if table[1] == H else tab[:, 0:1, :].to_broadcast([S, 4, S])
                    nc.vector.scalar_tensor_tensor(out=t[:, heads, :], in0=ps, scalar=scale, in1=tb, op0=ALU.mult,
                                                   op1=ALU.mult if mode == "mul" else ALU.add).then_inc(t_ready, 1)
                    dve.wait_ge(t_ready, b * NB4 + g + 1)
                    nc.vector.tensor_reduce(low[:, heads], t[:, heads, :], AX.X, ALU.max, negate=True).then_inc(low_ready, 1)
                else:
                    nc.vector.tensor_reduce(low[:, heads], ps, AX.X, ALU.max, negate=True).then_inc(low_ready, 1)
                    dve.wait_ge(low_ready, 2 * (b * NB4 + g) + 1)
                    nc.vector.tensor_scalar(low[:, heads], low[:, heads], scale, None, ALU.mult).then_inc(low_ready, 1)

            def add_out(b):
                dve.wait_ge(o_full, b + 1)
                part = acc[:, bass.ds(b * S, S)]
                if bo is not None:
                    nc.vector.scalar_tensor_tensor(out=part, in0=cps[0][:, 0:S], scalar=bo_sb[:, :], in1=part,
                                                   op0=ALU.add, op1=ALU.add).then_inc(o_added, 1)
                else:
                    nc.vector.tensor_tensor(part, part, cps[0][:, 0:S], ALU.add).then_inc(o_added, 1)

            def invert(b, g):
                dve.wait_ge(exp_done, b * H + 4 * (g + 1))
                nc.vector.reciprocal(inv[:, 4 * g:4 * g + 4], tot[:, 4 * g:4 * g + 4]).then_inc(inv_ready, 1)

            if d == 8:
                nc.vector.memset(v[:, inner:inner + WIDE - d], 0.0).then_inc(cleared, 1)
            else:
                nc.vector.memset(kT[:, :, :], 0.0).then_inc(cleared, 1)
            dve.wait_ge(cleared, 1)
            for u in range(NU):
                read_proj(0, u)

            def body(b, has_next, has_prev):
                for g in range(NB4):
                    lowest(b, g)
                half = plan.n_qk // 2
                for u in range(half):
                    if has_next:
                        read_proj(b + 1, u)
                    invert(b, u)
                for g in range(half, 3):
                    invert(b, g)
                if has_prev:
                    add_out(b - 1)
                invert(b, 3)
                if has_next:
                    for u in range(half, plan.n_qk):
                        read_proj(b + 1, u)
                if has_next:
                    for u in range(plan.n_qk, NU):
                        read_proj(b + 1, u)

            batches(dve, body)
            add_out(B - 1)


def load_columns(nc, name, pairs):
    with Stage(nc, name) as st:
        loaded = st.sem("loaded")
        block = st.ctx.enter_context(nc.Block())

        @block.sync
        def _(sp):
            for dst, src in pairs:
                sp.dma_start(dst, src).then_inc(loaded, 16)
            sp.wait_ge(loaded, 16 * len(pairs))


def add_to(nc, name, dst, src):
    with Stage(nc, name) as st:
        added = st.sem("added")
        block = st.ctx.enter_context(nc.Block())

        @block.vector
        def _(dve):
            nc.vector.tensor_tensor(dst[:, :], dst[:, :], src[:, :], ALU.add).then_inc(added, 1)
            dve.wait_ge(added, 1)


def stage_self0(nc, G, I):
    with Stage(nc, "s0") as st:
        xa = st.sb("xa", [128, TOK])
        cols = st.sb("cols", [128, 4])
        load_columns(nc, "s0c", [(cols[:, :], I["L0_ln"])])
        layer_norm(nc, "s0ln", G, G["xT"], G["xn"])
        layer_norm(nc, "s0ln1", G, G["xn"], xa, cols[:, 0:1], cols[:, 1:2])
        w = {n: I["L0_attn_" + n] for n in ("W_Q", "W_K", "W_V", "W_O", "b_Q", "b_K", "b_V", "b_O")}
        self_attention(nc, "s0a", G, G["xn"], xa, 64, w["W_Q"], w["W_K"], w["W_V"], w["W_O"], w["b_Q"], w["b_K"], w["b_V"],
                       w["b_O"], "mul", (I["c_causal01"], 1))
        layer_norm(nc, "s0ln2", G, G["xn"], xa, cols[:, 2:3], cols[:, 3:4])
        add_to(nc, "s0p", G["xT"], G["xn"])
        add_to(nc, "s0r", G["xT"], xa)


def stage_self1(nc, G, I):
    layer_norm(nc, "s3ln", G, G["xT"], G["xn"])
    self_attention(nc, "s3a", G, G["xT"], G["xn"], 64, I["L1_attn_Wq"], I["L1_attn_Wk"], I["L1_attn_Wv"], I["L1_attn_Wo"],
                   None, None, None, I["L1_attn_bo"], None, None)


def stage_self2(nc, G, I):
    layer_norm(nc, "s6ln", G, G["xT"], G["xn"])
    self_attention(nc, "s6a", G, G["xT"], G["xn"], 8, I["L2_attn_wq"], I["L2_attn_wk"], I["L2_attn_wv"], I["L2_attn_wo"],
                   None, None, None, None, "add", (I["c_alibi"], 16))


def stage_self3(nc, G, I):
    layer_norm(nc, "s9ln", G, G["xT"], G["xn"])
    self_attention(nc, "s9a", G, G["xT"], G["xn"], 64, I["L3_attn_wq"], I["L3_attn_wk"], I["L3_attn_wv"], I["L3_attn_wo"],
                   None, None, None, None, "add", (I["c_causal"], 1))


def expert_heads(nc, name, G, I, acc, src):
    H, R, d = 16, 4, 64
    WC = 258
    Q0, K0, V0, BV0 = 0, 65, 130, 194
    idx_dram = nc.dram_tensor(name + "_idx", (B, 8), mybir.dt.uint32, kind="Internal").ap()
    with Stage(nc, name) as st:
        g2 = st.sb("g2", [128, B, R])
        g1 = st.sb("g1", [128, B, R])
        with Stage(nc, name + "r") as sr:
            wr = sr.sb("wr", [128, H])
            br = sr.sb("br", [B, H])
            xm = sr.sb("xm", [128, B])
            dist = sr.sb("dist", [B, H])
            top = sr.sb("top", [B, 8])
            idx = sr.sb("idx", [B, 8], mybir.dt.uint32)
            col = sr.sb("col", [B, 8])
            spread = sr.sb("spread", [B, 2, B, R])
            ones = sr.sb("ones", [B, 128])
            ps = sr.ps("ps", [128, BANK])
            ps2 = sr.ps("ps2", [128, BANK])
            loaded, mean_ready, logits_ready, chain, shifted, exp_done, shifted2, exp2_done, spread_ready, bcast, kept = (
                sr.sem(n) for n in ("loaded", "mean_ready", "logits_ready", "chain", "shifted", "exp_done", "shifted2",
                                    "exp2_done", "spread_ready", "bcast", "kept"))
            block = sr.ctx.enter_context(nc.Block())

            @block.sync
            def _(sp):
                sp.dma_start(wr[:, :], I["L2_ffn_Wr"]).then_inc(loaded, 16)
                sp.dma_start(br[:, :], I["L2_ffn_br"].partition_broadcast(B)).then_inc(loaded, 16)
                sp.wait_ge(spread_ready, 1)
                sp.dma_start(idx_dram, idx[:, :]).then_inc(kept, 16)
                sp.wait_ge(kept, 16)

            @block.tensor
            def _(pe):
                pe.wait_ge(loaded, 32)
                pe.wait_ge(mean_ready, 1)
                nc.tensor.matmul(ps[0:B, 0:H], xm[:, :], wr[:, :], start=True, stop=True).then_inc(logits_ready, 1)
                pe.wait_ge(spread_ready, 1)
                nc.tensor.matmul(ps2[:, 0:2 * B * R], ones[:, :], spread[:, :, :, :].rearrange("p a b k -> p (a b k)"),
                                 start=True, stop=True).then_inc(bcast, 1)

            @block.scalar
            def _(act):
                act.wait_ge(shifted, 1)
                nc.scalar.activation(dist[:, :], dist[:, :], ACT.Exp).then_inc(exp_done, 1)
                act.wait_ge(shifted2, 1)
                nc.scalar.activation(col[:, 0:5], col[:, 0:5], ACT.Exp).then_inc(exp2_done, 1)

            @block.vector
            def _(dve):
                link = Link(dve, chain, 18, 0)
                link(nc.vector.memset(ones[:, :], 1.0))
                link(nc.vector.tensor_reduce(xm[:, :], src[:, :].rearrange("p (b n) -> p b n", n=S), AX.X, ALU.add))
                nc.vector.tensor_scalar(xm[:, :], xm[:, :], 1.0 / S, None, ALU.mult).then_inc(mean_ready, 1)
                dve.wait_ge(loaded, 32)
                dve.wait_ge(logits_ready, 1)
                link(nc.vector.tensor_tensor(dist[:, :], ps[0:B, 0:H], br[:, :], ALU.add))
                link(nc.vector.tensor_reduce(col[:, 7:8], dist[:, :], AX.X, ALU.max))
                nc.vector.tensor_scalar(dist[:, :], dist[:, :], col[:, 7:8], None, ALU.subtract).then_inc(shifted, 1)
                dve.wait_ge(exp_done, 1)
                link(nc.vector.tensor_reduce(col[:, 7:8], dist[:, :], AX.X, ALU.add))
                link(nc.vector.reciprocal(col[:, 6:7], col[:, 7:8]))
                link(nc.vector.tensor_scalar(dist[:, :], dist[:, :], col[:, 6:7], None, ALU.mult))
                link(nc.vector.max(top[:, :], dist[:, :]))
                link(nc.vector.max_index(idx[:, :], top[:, :], dist[:, :]))
                link(nc.vector.memset(col[:, 0:5], 0.0))
                link(nc.vector.tensor_copy(col[:, 0:4], top[:, 0:4]))
                nc.vector.tensor_scalar(col[:, 0:5], col[:, 0:5], top[:, 0:1], None, ALU.subtract).then_inc(shifted2, 1)
                dve.wait_ge(exp2_done, 1)
                link(nc.vector.tensor_reduce(col[:, 7:8], col[:, 0:4], AX.X, ALU.add))
                link(nc.vector.scalar_tensor_tensor(out=col[:, 6:7], in0=col[:, 4:5], scalar=12.0, in1=col[:, 7:8],
                                                    op0=ALU.mult, op1=ALU.add))
                link(nc.vector.reciprocal(col[:, 5:6], col[:, 6:7]))
                link(nc.vector.tensor_scalar(col[:, 0:4], col[:, 0:4], col[:, 5:6], None, ALU.mult))
                diag = G["ident"][0:B, 0:B].unsqueeze(2).to_broadcast([B, B, R])
                gates = col[:, 0:4].unsqueeze(1).to_broadcast([B, B, R])
                link(nc.vector.tensor_tensor(spread[:, 0, :, :], diag, gates, ALU.mult))
                link(nc.vector.tensor_tensor(spread[:, 1, :, :], spread[:, 0, :, :], gates, ALU.mult))
                nc.vector.tensor_scalar(spread[:, 1, :, :], spread[:, 1, :, :], 1.0 / 8.0, None, ALU.mult).then_inc(spread_ready, 1)
                dve.wait_ge(bcast, 1)
                half = ps2[:, 0:2 * B * R].rearrange("p (a b k) -> p a b k", a=2, b=B)
                link(nc.vector.tensor_copy(g1[:, :, :], half[:, 0, :, :]))
                nc.vector.tensor_copy(g2[:, :, :], half[:, 1, :, :])
                link.end()

        w = [st.sb(f"w{j}", [128, R, WC]) for j in range(2)]
        wo_sb = st.sb("wo", [128, 2, D])
        bo_sb = st.sb("bo", [128, 1])
        xs = [st.sb(f"xs{j}", [128, S]) for j in range(2)]
        qT = st.sb("qT", [128, 2, S])
        kT = st.sb("kT", [128, 2, S])
        v = st.sb("v", [S, R, d])
        pr = st.sb("pr", [S, R, S])
        prT = st.sb("prT", [S, R, S])
        low, tot, inv = (st.sb(n, [S, R]) for n in ("low", "tot", "inv"))
        z = st.sb("z", [S, R * d])
        zT = st.sb("zT", [128, 2, S])
        qk_ps, v_ps, turn_ps, z_ps, zT_ps, o_ps = (st.ps(n, [128, BANK]) for n in ("qk", "v", "turn", "z", "zT", "o"))
        s_ps = [st.ps(f"s{j}", [128, BANK]) for j in range(2)]
        passed = st.sem("passed")
        w_in = [st.sem(f"w_in{j}") for j in range(2)]
        (loaded, xs_ready, qk_full, v_full, q_copied, k_copied, v_copied, s_full, low_step, exp_done, turned, prT_ready, z_full,
         z_step, z_turned, zT_ready, o_full, o_added) = (
            st.sem(n) for n in ("loaded", "xs_ready", "qk_full", "v_full", "q_copied", "k_copied", "v_copied", "s_full", "low_step",
                                "exp_done", "turned", "prT_ready", "z_full", "z_step", "z_turned", "zT_ready", "o_full", "o_added"))
        block = st.ctx.enter_context(nc.Block())

        def weights_by(b, j):
            return 8 * R * (b - j) + 16 * R

        def batches(eng, body):
            body(0, 0, True, False)
            with eng.Fori(0, (B - 2) // 2) as i:
                body(2 * i + 1, 1, True, True)
                body(2 * i + 2, 0, True, True)
            body(B - 1, 1, False, True)

        @block.sync
        def _(sp):
            sp.dma_start(wo_sb[:, :, :], I["L2_ffn_Wo"]).then_inc(loaded, 16)
            sp.dma_start(bo_sb[:, :], I["L2_ffn_bo"]).then_inc(loaded, 16)

            def load(b, j):
                for r in range(R):
                    head = sp.value_load(idx_dram[bass.ds(b, 1), r:r + 1], min_val=0, max_val=H - 1)
                    sp.dma_start(w[j][:, r, :], I["L2_ffn_heads"][bass.ds(head, 1), :, :].rearrange("a p n -> p (a n)")).then_inc(w_in[j], 16)

            load(0, 0)
            load(1, 1)

            def next_load(b, j):
                sp.wait_ge(v_copied, b - 1)
                sp.sem_inc(passed, 1)
                load(b, j)

            with sp.Fori(0, (B - 2) // 2) as i:
                next_load(2 * i + 2, 0)
                next_load(2 * i + 3, 1)

        @block.gpsimd
        def _(pool):
            def copy_x(b, j):
                after(pool, v_full, b - 1)
                nc.gpsimd.tensor_copy(xs[j][:, :], src[:, bass.ds(b * S, S)]).then_inc(xs_ready, 1)

            copy_x(0, 0)
            copy_x(1, 1)
            with pool.Fori(0, (B - 2) // 2) as i:
                copy_x(2 * i + 2, 0)
                copy_x(2 * i + 3, 1)

        @block.tensor
        def _(pe):
            pe.wait_ge(loaded, 32)

            def project_qk(b, j):
                pe.wait_ge(w_in[j], weights_by(b, j))
                after(pe, k_copied, 4 * b)
                pe.wait_ge(xs_ready, b + 1)
                for n, c0 in enumerate((Q0, K0)):
                    for r in range(R):
                        rows, at = slice(64 * (r % 2), 64 * (r % 2) + 64), (2 * n + r // 2) * S
                        m = nc.tensor.matmul(qk_ps[rows, at:at + S], w[j][:, r, c0:c0 + d], xs[j][:, :], start=True, stop=True)
                m.then_inc(qk_full, 1)

            def project_v(b, j):
                after(pe, v_copied, b)
                nc.tensor.matmul(v_ps[0:S, 0:R * d], xs[j][:, :], w[j][:, :, V0:V0 + d], start=True, stop=True).then_inc(v_full, 1)

            def scores(b):
                pe.wait_ge(k_copied, 4 * (b + 1))
                pe.wait_ge(q_copied, 4 * (b + 1))
                after(pe, exp_done, R * b)
                for r in range(R):
                    rows = slice(64 * (r % 2), 64 * (r % 2) + 64)
                    m = nc.tensor.matmul(s_ps[r % 2][0:S, (r // 2) * S:(r // 2 + 1) * S], qT[rows, r // 2, :], kT[rows, r // 2, :],
                                         start=True, stop=True)
                m.then_inc(s_full, 1)

            def turn(b):
                after(pe, prT_ready, b)
                for r in range(R):
                    pe.wait_ge(exp_done, R * b + r + 1)
                    m = nc.tensor.transpose(turn_ps[0:S, r * S:(r + 1) * S], pr[:, r, :], G["ident"][0:S, 0:S])
                m.then_inc(turned, 1)

            def values(b):
                pe.wait_ge(prT_ready, b + 1)
                pe.wait_ge(v_copied, b + 1)
                after(pe, z_step, 3 * b)
                for r in range(R):
                    m = nc.tensor.matmul(z_ps[0:S, r * d:(r + 1) * d], prT[:, r, :], v[:, r, :], start=True, stop=True)
                m.then_inc(z_full, 1)

            def turn_z(b):
                pe.wait_ge(z_step, 3 * (b + 1))
                for p in range(2):
                    m = nc.tensor.transpose(zT_ps[:, p * S:(p + 1) * S], z[:, p * 128:(p + 1) * 128], G["ident"][0:S, 0:S])
                m.then_inc(z_turned, 1)

            def project_out(b):
                pe.wait_ge(zT_ready, b + 1)
                for p in range(2):
                    m = nc.tensor.matmul(o_ps[:, 0:S], wo_sb[:, p, :], zT[:, p, :], start=(p == 0), stop=(p == 1))
                m.then_inc(o_full, 1)

            project_qk(0, 0)
            project_v(0, 0)

            def body(b, j, has_next, has_prev):
                scores(b)
                if has_prev:
                    turn_z(b - 1)
                if has_next:
                    project_qk(b + 1, 1 - j)
                if has_prev:
                    project_out(b - 1)
                turn(b)
                values(b)
                if has_next:
                    project_v(b + 1, 1 - j)

            batches(pe, body)
            turn_z(B - 1)
            project_out(B - 1)

        @block.scalar
        def _(act):
            def body(b, j, has_next, has_prev):
                act.wait_ge(low_step, 3 * (b + 1))
                after(act, turned, b)
                for r in range(R):
                    nc.scalar.activation(pr[:, r, :], s_ps[r % 2][0:S, (r // 2) * S:(r // 2 + 1) * S], ACT.Exp, bias=low[:, r:r + 1],
                                         scale=g2[0:S, bass.ds(b, 1), r:r + 1].rearrange("p a r -> p (a r)"),
                                         accum_out=tot[:, r:r + 1]).then_inc(exp_done, 1)
                if has_prev:
                    act.wait_ge(z_turned, b)
                    nc.scalar.activation(zT[:, :, :], zT_ps[:, 0:2 * S].rearrange("p (a n) -> p a n", n=S), ACT.Copy).then_inc(zT_ready, 1)
                act.wait_ge(turned, b + 1)
                after(act, z_full, b)
                nc.scalar.activation(prT[:, :, :], turn_ps[0:S, 0:R * S].rearrange("p (a n) -> p a n", n=S), ACT.Copy).then_inc(prT_ready, 1)

            batches(act, body)
            act.wait_ge(z_turned, B)
            nc.scalar.activation(zT[:, :, :], zT_ps[:, 0:2 * S].rearrange("p (a n) -> p a n", n=S), ACT.Copy).then_inc(zT_ready, 1)

        @block.vector
        def _(dve):
            dve.wait_ge(loaded, 32)

            def copy_qk(b, j):
                dve.wait_ge(qk_full, b + 1)
                dve.wait_ge(w_in[j], weights_by(b, j))
                after(dve, s_full, b)
                for n, (dst, c0, copied) in enumerate(((qT, Q0, q_copied), (kT, K0, k_copied))):
                    for r in range(R):
                        rows = slice(64 * (r % 2), 64 * (r % 2) + 64)
                        nc.vector.tensor_scalar(dst[rows, r // 2, :], qk_ps[rows, (2 * n + r // 2) * S:(2 * n + r // 2 + 1) * S],
                                                w[j][rows, r, c0 + d:c0 + d + 1], None, ALU.add).then_inc(copied, 1)

            def copy_v(b, j):
                dve.wait_ge(v_full, b + 1)
                after(dve, z_full, b)
                nc.vector.tensor_tensor(v[:, :, :], v_ps[0:S, 0:R * d].rearrange("p (r f) -> p r f", f=d), w[j][0:S, :, BV0:BV0 + d],
                                        ALU.add).then_inc(v_copied, 1)

            def lowest(b):
                dve.wait_ge(s_full, b + 1)
                after(dve, exp_done, R * b)
                for half in range(2):
                    nc.vector.tensor_reduce(low[:, half::2], s_ps[half][0:S, 0:2 * S].rearrange("p (r n) -> p r n", n=S), AX.X, ALU.max,
                                            negate=True).then_inc(low_step, 1)
                dve.wait_ge(low_step, 3 * b + 2)
                nc.vector.tensor_tensor(low[:, :], low[:, :], g2[0:S, bass.ds(b, 1), :].rearrange("p a r -> p (a r)"),
                                        ALU.mult).then_inc(low_step, 1)

            def normalise(b):
                dve.wait_ge(exp_done, R * (b + 1))
                nc.vector.reciprocal(inv[:, :], tot[:, :]).then_inc(z_step, 1)
                dve.wait_ge(z_step, 3 * b + 1)
                nc.vector.tensor_tensor(inv[:, :], inv[:, :], g1[0:S, bass.ds(b, 1), :].rearrange("p a r -> p (a r)"),
                                        ALU.mult).then_inc(z_step, 1)
                dve.wait_ge(z_step, 3 * b + 2)
                dve.wait_ge(z_full, b + 1)
                after(dve, z_turned, b)
                nc.vector.tensor_tensor(z[:, :].rearrange("p (r f) -> p r f", f=d), z_ps[0:S, 0:R * d].rearrange("p (r f) -> p r f", f=d),
                                        inv[:, :].unsqueeze(2).to_broadcast([S, R, d]), ALU.mult).then_inc(z_step, 1)

            def add_out(b):
                dve.wait_ge(o_full, b + 1)
                part = acc[:, bass.ds(b * S, S)]
                nc.vector.scalar_tensor_tensor(out=part, in0=o_ps[:, 0:S], scalar=bo_sb[:, :], in1=part,
                                               op0=ALU.add, op1=ALU.add).then_inc(o_added, 1)

            copy_qk(0, 0)
            copy_v(0, 0)

            def body(b, j, has_next, has_prev):
                lowest(b)
                if has_next:
                    copy_qk(b + 1, 1 - j)
                if has_prev:
                    add_out(b - 1)
                normalise(b)
                if has_next:
                    copy_v(b + 1, 1 - j)

            batches(dve, body)
            add_out(B - 1)


def stage_ffn2(nc, G, I):
    layer_norm(nc, "s8ln", G, G["xT"], G["xn"])
    expert_heads(nc, "s8a", G, I, G["xT"], G["xn"])


def dense_ffn(nc, name, acc, src, w1, w2, b1, b2, low_rank):
    HC = 4
    with Stage(nc, name) as st:
        h_ps = [st.ps(f"h{j}", [128, BANK]) for j in range(2)]
        o_ps = st.ps("o", [128, BANK])
        lr_ps = st.ps("lr", [128, BANK])
        t1, t2 = st.sb("t1", [16, GT]), st.sb("t2", [16, GT])
        hid = [st.sb(f"hid{j}", [128, GT]) for j in range(2)]
        rel = [st.sb(f"rel{j}", [128, GT]) for j in range(2)]
        h_full, h_read, hid_ready, hid_used, o_added, lr_full, lr_read = (
            st.sem(n) for n in ("h_full", "h_read", "hid_ready", "hid_used", "o_added", "lr_full", "lr_read"))
        block = st.ctx.enter_context(nc.Block())

        @block.tensor
        def _(pe):
            def group(g):
                x = src[:, bass.ds(g * GT, GT)]
                if low_rank:
                    vT, fbT, uT, _ = low_rank
                    after(pe, lr_read, 2 * g)
                    nc.tensor.matmul(lr_ps[:, 0:GT], vT, x, start=True, stop=True).then_inc(lr_full, 1)
                    pe.wait_ge(lr_read, 2 * g + 1)
                    nc.tensor.matmul(lr_ps[:, 0:GT], fbT, t1[:, :], start=True, stop=True).then_inc(lr_full, 1)
                    pe.wait_ge(lr_read, 2 * g + 2)
                for c in range(HC + 1):
                    if c < HC:
                        after(pe, h_read, g * HC + c - 1)
                        m = nc.tensor.matmul(h_ps[c % 2][:, 0:GT], w1[:, c, :], x, start=True, stop=not low_rank)
                        if low_rank:
                            m = nc.tensor.matmul(h_ps[c % 2][:, 0:GT], uT[:, c * 128:(c + 1) * 128], t2[:, :], start=False, stop=True)
                        m.then_inc(h_full, 1)
                    if c:
                        if c == 1:
                            after(pe, o_added, g)
                        pe.wait_ge(hid_ready, g * HC + c)
                        nc.tensor.matmul(o_ps[:, 0:GT], w2[:, c - 1, :], hid[(c - 1) % 2][:, :], start=(c == 1), stop=(c == HC)).then_inc(hid_used, 1)

            group(0)
            with pe.Fori(1, NG) as g:
                group(g)

        @block.scalar
        def _(act):
            def group(g):
                if low_rank:
                    act.wait_ge(lr_full, 2 * g + 1)
                    nc.scalar.activation(t1[:, :], lr_ps[0:16, 0:GT], ACT.Copy).then_inc(lr_read, 1)
                    act.wait_ge(lr_full, 2 * g + 2)
                    after(act, h_full, g * HC)
                    nc.scalar.activation(t2[:, :], lr_ps[0:16, 0:GT], ACT.Identity, scale=low_rank[3]).then_inc(lr_read, 1)
                for c in range(HC):
                    act.wait_ge(h_full, g * HC + c + 1)
                    if low_rank:
                        after(act, hid_ready, g * HC + c - 1)
                        nc.scalar.activation(rel[c % 2][:, :], h_ps[c % 2][:, 0:GT], ACT.Relu).then_inc(h_read, 1)
                    else:
                        after(act, hid_used, g * HC + c - 1)
                        nc.scalar.activation(hid[c % 2][:, :], h_ps[c % 2][:, 0:GT], ACT.Relu, bias=b1[:, c:c + 1]).then_inc(h_read, 1)
                        act.wait_ge(h_read, g * HC + c + 1)
                        act.sem_inc(hid_ready, 1)

            group(0)
            with act.Fori(1, NG) as g:
                group(g)

        @block.vector
        def _(dve):
            def group(g):
                if low_rank:
                    for c in range(HC):
                        dve.wait_ge(h_read, g * HC + c + 1)
                        after(dve, hid_used, g * HC + c - 1)
                        nc.vector.tensor_tensor(hid[c % 2][:, :], rel[c % 2][:, :], rel[c % 2][:, :], ALU.mult).then_inc(hid_ready, 1)
                dve.wait_ge(hid_used, (g + 1) * HC)
                part = acc[:, bass.ds(g * GT, GT)]
                if b2 is None:
                    nc.vector.tensor_tensor(part, part, o_ps[:, 0:GT], ALU.add).then_inc(o_added, 1)
                else:
                    nc.vector.scalar_tensor_tensor(out=part, in0=o_ps[:, 0:GT], scalar=b2, in1=part, op0=ALU.add, op1=ALU.add).then_inc(o_added, 1)

            group(0)
            with dve.Fori(1, NG) as g:
                group(g)


def diagonal_attention(nc, name, G, I, acc, src):
    scale = float(np.sqrt(D))
    with Stage(nc, name) as st:
        w = st.sb("w", [128, 4, D])
        cols = st.sb("cols", [128, 3])
        bv = st.sb("bv", [S, D])
        mask = st.sb("mask", [S, 1, S])
        xs = st.sb("xs", [128, GT])
        qT, kT, zT = (st.sb(n, [128, GT]) for n in ("qT", "kT", "zT"))
        v = st.sb("v", [S, GB, D])
        t, pr, prT = (st.sb(n, [S, GB, S]) for n in ("t", "pr", "prT"))
        low, tot, inv = (st.sb(n, [S, GB]) for n in ("low", "tot", "inv"))
        q_ps, k_ps, v_ps, s_ps, t_ps, z_ps, o_ps = (st.ps(n, [128, BANK]) for n in ("q", "k", "v", "s", "t", "z", "o"))
        loaded, xs_ready, proj_full, proj_copied, s_full, soft, exp_done, turned, prT_ready, z_full, zT_ready, o_full, o_added = (
            st.sem(n) for n in ("loaded", "xs_ready", "proj_full", "proj_copied", "s_full", "soft", "exp_done", "turned",
                                "prT_ready", "z_full", "zT_ready", "o_full", "o_added"))
        block = st.ctx.enter_context(nc.Block())

        def groups(eng, body):
            body(0)
            with eng.Fori(1, NG) as g:
                body(g)

        @block.sync
        def _(sp):
            for dst, s in ((w[:, :, :], I["L3_sa_w"]), (cols[:, :], I["L3_sa_cols"]), (bv[:, :], I["L3_sa_bv"].partition_broadcast(S)),
                           (mask[:, :, :], I["c_diagonal"])):
                sp.dma_start(dst, s).then_inc(loaded, 16)

        @block.gpsimd
        def _(pool):
            def body(g):
                after(pool, proj_full, 3 * g)
                nc.gpsimd.tensor_copy(xs[:, :], src[:, bass.ds(g * GT, GT)]).then_inc(xs_ready, 1)

            groups(pool, body)

        @block.tensor
        def _(pe):
            pe.wait_ge(loaded, 64)

            def body(g):
                pe.wait_ge(xs_ready, g + 1)
                after(pe, proj_copied, 3 * g)
                nc.tensor.matmul(q_ps[:, 0:GT], w[:, 0, :], xs[:, :], start=True, stop=True).then_inc(proj_full, 1)
                nc.tensor.matmul(k_ps[:, 0:GT], w[:, 1, :], xs[:, :], start=True, stop=True).then_inc(proj_full, 1)
                for n in range(GB):
                    m = nc.tensor.matmul(v_ps[0:S, n * D:(n + 1) * D], xs[:, n * S:(n + 1) * S], w[:, 2, :], start=True, stop=True)
                m.then_inc(proj_full, 1)
                pe.wait_ge(proj_copied, 3 * g + 2)
                after(pe, soft, 4 * g)
                for n in range(GB):
                    part = slice(n * S, (n + 1) * S)
                    m = nc.tensor.matmul(s_ps[0:S, part], qT[:, part], kT[:, part], start=True, stop=True)
                m.then_inc(s_full, 1)
                pe.wait_ge(soft, 4 * g + 4)
                for n in range(GB):
                    m = nc.tensor.transpose(t_ps[0:S, n * S:(n + 1) * S], pr[:, n, :], G["ident"][0:S, 0:S])
                m.then_inc(turned, 1)
                pe.wait_ge(prT_ready, g + 1)
                pe.wait_ge(proj_copied, 3 * g + 3)
                for n in range(GB):
                    m = nc.tensor.matmul(z_ps[:, n * S:(n + 1) * S], v[:, n, :], prT[:, n, :], start=True, stop=True)
                m.then_inc(z_full, 1)
                pe.wait_ge(zT_ready, g + 1)
                after(pe, o_added, g)
                nc.tensor.matmul(o_ps[:, 0:GT], w[:, 3, :], zT[:, :], start=True, stop=True).then_inc(o_full, 1)

            groups(pe, body)

        @block.scalar
        def _(act):
            def body(g):
                act.wait_ge(soft, 4 * g + 2)
                for n in range(GB):
                    nc.scalar.activation(pr[:, n, :], t[:, n, :], ACT.Exp, bias=low[:, n:n + 1], accum_out=tot[:, n:n + 1]).then_inc(exp_done, 1)
                act.wait_ge(turned, g + 1)
                nc.scalar.activation(prT[:, :, :], t_ps[0:S, 0:GT].rearrange("p (a n) -> p a n", n=S), ACT.Copy).then_inc(prT_ready, 1)
                act.wait_ge(z_full, g + 1)
                nc.scalar.activation(zT[:, :], z_ps[:, 0:GT], ACT.Copy).then_inc(zT_ready, 1)

            groups(act, body)

        @block.vector
        def _(dve):
            dve.wait_ge(loaded, 64)

            def body(g):
                dve.wait_ge(proj_full, 3 * g + 1)
                nc.vector.tensor_scalar(qT[:, :], q_ps[:, 0:GT], cols[:, 0:1], None, ALU.add).then_inc(proj_copied, 1)
                dve.wait_ge(proj_full, 3 * g + 2)
                nc.vector.tensor_scalar(kT[:, :], k_ps[:, 0:GT], cols[:, 1:2], None, ALU.add).then_inc(proj_copied, 1)
                dve.wait_ge(proj_full, 3 * g + 3)
                nc.vector.tensor_tensor(v[:, :, :], v_ps[0:S, :].rearrange("p (a n) -> p a n", n=D),
                                        bv[:, :].unsqueeze(1).to_broadcast([S, GB, D]), ALU.add).then_inc(proj_copied, 1)
                dve.wait_ge(s_full, g + 1)
                nc.vector.scalar_tensor_tensor(out=t[:, :, :], in0=s_ps[0:S, 0:GT].rearrange("p (a n) -> p a n", n=S), scalar=scale,
                                               in1=mask[:, 0:1, :].to_broadcast([S, GB, S]), op0=ALU.mult, op1=ALU.add).then_inc(soft, 1)
                dve.wait_ge(soft, 4 * g + 1)
                nc.vector.tensor_reduce(low[:, :], t[:, :, :], AX.X, ALU.max, negate=True).then_inc(soft, 1)
                dve.wait_ge(exp_done, GB * (g + 1))
                nc.vector.reciprocal(inv[:, :], tot[:, :]).then_inc(soft, 1)
                dve.wait_ge(soft, 4 * g + 3)
                nc.vector.tensor_tensor(pr[:, :, :], pr[:, :, :], inv[:, :].unsqueeze(2).to_broadcast([S, GB, S]), ALU.mult).then_inc(soft, 1)
                dve.wait_ge(o_full, g + 1)
                part = acc[:, bass.ds(g * GT, GT)]
                nc.vector.scalar_tensor_tensor(out=part, in0=o_ps[:, 0:GT], scalar=cols[:, 2:3], in1=part, op0=ALU.add, op1=ALU.add).then_inc(o_added, 1)

            groups(dve, body)


def stage_cross3(nc, G, I):
    with Stage(nc, "s10") as st:
        cols = st.sb("cols", [128, 11])
        load_columns(nc, "s10c", [(cols[:, :], I["L3_cols"])])
        layer_norm(nc, "s10ln", G, G["xT"], G["xn"])
        diagonal_attention(nc, "s10s", G, I, G["xn"], G["xn"])
        layer_norm(nc, "s10ln1", G, G["xn"], G["xn"], cols[:, 0:1], cols[:, 1:2])
        w = {n: I["L3_x_" + n] for n in ("wq", "bq", "wk", "bk", "wv", "bv", "wo", "bo")}
        cross_attention(nc, "s10x", G, I, G["xn"], G["xn"], 8, w["wq"], w["bq"], w["wk"], w["bk"], w["wv"], w["bv"],
                        w["wo"], w["bo"], False)
        layer_norm(nc, "s10ln2", G, G["xn"], G["xn"], cols[:, 2:3], cols[:, 3:4])
        w1, w2 = st.sb("w1", [128, 4, 128]), st.sb("w2", [128, 4, 128])
        load_columns(nc, "s10w", [(w1[:, :, :], I["L3_lin1_w"]), (w2[:, :, :], I["L3_lin2_w"])])
        dense_ffn(nc, "s10f", G["xn"], G["xn"], w1, w2, cols[:, 6:10], cols[:, 10:11], None)
        layer_norm(nc, "s10ln3", G, G["xn"], G["xn"], cols[:, 4:5], cols[:, 5:6])
        add_to(nc, "s10p", G["xT"], G["xn"])


def ternary_weights(nc, name, G, natural, n_blocks, n_scales, turned):
    BIG = float(3 << 22)
    row = n_blocks * 128 // n_scales
    with Stage(nc, name) as st:
        mean, inv = st.sb("mean", [128, n_scales]), st.sb("inv", [128, n_scales])
        w = natural[:, :, :].rearrange("p c n -> p (c n)").rearrange("p (s n) -> p s n", s=n_scales)
        shape = [128, n_scales, row]
        tern = st.sb("tern", shape)
        ps = st.ps("ps", [128, BANK])
        chain, ready, turned_ps = st.sem("chain"), st.sem("ready"), st.sem("turned")
        block = st.ctx.enter_context(nc.Block())

        @block.vector
        def _(dve):
            link = Link(dve, chain, 9, 0)
            link(nc.vector.tensor_reduce(mean[:, :], w, AX.X, ALU.add, apply_absolute_value=True))
            link(nc.vector.tensor_scalar(mean[:, :], mean[:, :], 1.0 / row, 1e-5, ALU.mult, ALU.max))
            link(nc.vector.reciprocal(inv[:, :], mean[:, :]))
            link(nc.vector.tensor_tensor(tern[:, :, :], w, inv[:, :].unsqueeze(2).to_broadcast(shape), ALU.mult))
            link(nc.vector.tensor_scalar(tern[:, :, :], tern[:, :, :], BIG, BIG, ALU.add, ALU.subtract))
            link(nc.vector.tensor_scalar(tern[:, :, :], tern[:, :, :], 1.0, -1.0, ALU.min, ALU.max))
            link(nc.vector.tensor_tensor(tern[:, :, :], tern[:, :, :], w, ALU.subtract))
            link(nc.vector.tensor_tensor(tern[:, :, :], tern[:, :, :], w, ALU.add))
            nc.vector.tensor_tensor(tern[:, :, :], tern[:, :, :], mean[:, :].unsqueeze(2).to_broadcast(shape), ALU.mult).then_inc(ready, 1)
            dve.wait_ge(turned_ps, 1)
            link(nc.vector.tensor_copy(turned[:, :, :], ps[:, :].rearrange("p (c n) -> p c n", c=n_blocks)))
            link.end()

        @block.tensor
        def _(pe):
            pe.wait_ge(ready, 1)
            flat = tern[:, :, :].rearrange("p s n -> p (s n)")
            for c in range(n_blocks):
                m = nc.tensor.transpose(ps[:, c * 128:(c + 1) * 128], flat[:, c * 128:(c + 1) * 128], G["ident"][:, :])
            m.then_inc(turned_ps, 1)


def stage_ffn3(nc, G, I):
    layer_norm(nc, "s11ln", G, G["xT"], G["xn"])
    with Stage(nc, "s11") as st:
        fc, proj, fcT, projT = (st.sb(n, [128, 4, 128]) for n in ("fc", "proj", "fcT", "projT"))
        vT = st.sb("vT", [128, 128])
        fbT = st.sb("fbT", [16, 128])
        uT = st.sb("uT", [16, 512])
        gate = st.sb("gate", [16, 1])
        load_columns(nc, "s11w", [(fc[:, :, :], I["L3_ffn_w_fc"]), (proj[:, :, :], I["L3_ffn_w_proj"]), (vT[:, :], I["L3_ffn_v"]),
                                  (fbT[:, :], I["L3_ffn_fast_b"]), (uT[:, :], I["L3_ffn_u"]),
                                  (gate[:, :], I["L3_ffn_gate"].partition_broadcast(16))])
        ternary_weights(nc, "s11a", G, fc, 4, 4, fcT)
        ternary_weights(nc, "s11b", G, proj, 4, 1, projT)
        dense_ffn(nc, "s11f", G["xT"], G["xn"], fcT, projT, None, None, (vT[:, :], fbT[:, :], uT, gate[:, :]))


def bidirectional_attention(nc, name, G, I, acc, src):
    with Stage(nc, name) as st:
        cols = st.sb("cols", [128, 4])
        consts = st.sb("consts", [S, 3])
        wl = st.sb("wl", [128, 4, D])
        a_all = st.sb("a_all", [128, TOK])
        peak = st.sb("peak", [S, B])
        with Stage(nc, name + "a") as sa:
            ctxT = [sa.sb(f"ctxT{j}", [128, S2]) for j in range(2)]
            ctx = [sa.sb(f"ctx{j}", [KC, NCH, D]) for j in range(2)]
            cs = sa.sb("cs", [128, S])
            xs = sa.sb("xs", [128, S])
            pr = sa.sb("pr", [S, NCH * KC])
            prT = sa.sb("prT", [KC, NCH, S])
            m3, t3 = sa.sb("m3", [S, 4]), sa.sb("t3", [S, 3])
            low, tot, inv = (sa.sb(n, [S, 1]) for n in ("low", "tot", "inv"))
            z = sa.sb("z", [S, D])
            s_ps = [sa.ps(f"s{n}", [128, BANK]) for n in range(3)]
            t_ps = [sa.ps(f"t{n}", [128, BANK]) for n in range(2)]
            z_ps, zT_ps, r_ps = sa.ps("z", [128, BANK]), sa.ps("zT", [128, BANK]), sa.ps("r", [128, BANK])
            ctxT_in = [sa.sem(f"ctxT_in{j}") for j in range(2)]
            ctx_in = [sa.sem(f"ctx_in{j}") for j in range(2)]
            passed = sa.sem("passed")
            (loaded, cs_ready, xs_ready, s_full, r_full, max_step, exp_done, turned, prT_ready, z_full, z_step, z_turned, a_ready,
             padded) = (
                sa.sem(n) for n in ("loaded", "cs_ready", "xs_ready", "s_full", "r_full", "max_step", "exp_done", "turned", "prT_ready",
                                    "z_full", "z_step", "z_turned", "a_ready", "padded"))
            tot_step = sa.sem("tot_step")
            block = sa.ctx.enter_context(nc.Block())

            def loaded_by(b, j):
                return 8 * (b - j) + 16

            def batches(eng, body):
                body(0, 0, True, False)
                with eng.Fori(0, (B - 2) // 2) as i:
                    body(2 * i + 1, 1, True, True)
                    body(2 * i + 2, 0, True, True)
                body(B - 1, 1, False, True)

            @block.sync
            def _(sp):
                for dst, s in ((cols[:, :], I["L2_x_cols"]), (consts[:, :], I["L2_x_consts"].partition_broadcast(S)), (wl[:, :, :], I["L2_x_wl"])):
                    sp.dma_start(dst, s).then_inc(loaded, 16)

                def load(b, j):
                    after(sp, s_full, 3 * (b - 1))
                    sp.sem_inc(passed, 1)
                    sp.dma_start(ctxT[j][:, :], I["ctxT"][bass.ds(b, 1), :, :].rearrange("a p n -> p (a n)")).then_inc(ctxT_in[j], 16)
                    after(sp, z_full, b - 1)
                    sp.sem_inc(passed, 1)
                    sp.dma_start(ctx[j][:, :, :], I["ctx"][bass.ds(b, 1), :, :, :].rearrange("a p c n -> p (a c) n")).then_inc(ctx_in[j], 16)

                load(0, 0)
                load(1, 1)
                with sp.Fori(0, (B - 2) // 2) as i:
                    load(2 * i + 2, 0)
                    load(2 * i + 3, 1)

            @block.gpsimd
            def _(pool):
                def copy_x(b):
                    after(pool, r_full, b)
                    nc.gpsimd.tensor_copy(xs[:, :], src[:, bass.ds(b * S, S)]).then_inc(xs_ready, 1)

                copy_x(0)
                with pool.Fori(1, B) as b:
                    copy_x(b)

            @block.tensor
            def _(pe):
                pe.wait_ge(loaded, 48)
                pe.wait_ge(padded, 1)

                def scores(b, j):
                    pe.wait_ge(ctxT_in[j], loaded_by(b, j))
                    pe.wait_ge(cs_ready, b + 1)
                    for n, (at, w) in enumerate(SEGS):
                        after(pe, exp_done, 3 * (b - 1) + n + 1)
                        nc.tensor.matmul(s_ps[n][0:S, 0:w], cs[:, :], ctxT[j][:, at:at + w], start=True, stop=True).then_inc(s_full, 1)
                    pe.wait_ge(xs_ready, b + 1)
                    after(pe, max_step, 4 * b)
                    nc.tensor.matmul(r_ps[0:S, 0:1], xs[:, :], cols[:, 2:3], start=True, stop=True).then_inc(r_full, 1)

                def turn_z(b):
                    pe.wait_ge(z_step, 2 * (b + 1))
                    after(pe, a_ready, b)
                    nc.tensor.transpose(zT_ps[:, 0:S], z[:, :], G["ident"][0:S, 0:S]).then_inc(z_turned, 1)

                def body(b, j, has_next, has_prev):
                    if has_next:
                        scores(b + 1, 1 - j)
                    if has_prev:
                        turn_z(b - 1)
                    pe.wait_ge(exp_done, 3 * (b + 1))
                    for g in range(3):
                        after(pe, prT_ready, 3 * b + g - 1)
                        for c in range(4):
                            at = (4 * g + c) * KC
                            m = nc.tensor.transpose(t_ps[g % 2][0:KC, c * S:(c + 1) * S],
                                                    pr[:, at:at + KC], G["ident"][0:S, 0:S])
                        m.then_inc(turned, 1)
                    after(pe, z_step, 2 * b)
                    pe.wait_ge(ctx_in[j], loaded_by(b, j))
                    for c in range(NCH):
                        if c % 4 == 0:
                            pe.wait_ge(prT_ready, 3 * b + c // 4 + 1)
                        n = KC if c < NCH - 1 else LAST
                        m = nc.tensor.matmul(z_ps[0:S, 0:D], prT[0:n, c, :], ctx[j][0:n, c, :], start=(c == 0), stop=(c == NCH - 1))
                    m.then_inc(z_full, 1)

                scores(0, 0)
                batches(pe, body)
                turn_z(B - 1)

            @block.scalar
            def _(act):
                def copy_z(b):
                    act.wait_ge(z_turned, b + 1)
                    nc.scalar.activation(a_all[:, bass.ds(b * S, S)], zT_ps[:, 0:S], ACT.Copy).then_inc(a_ready, 1)

                def body(b, j, has_next, has_prev):
                    act.wait_ge(max_step, 4 * b + 3)
                    after(act, turned, 3 * b)
                    for n, (at, w) in enumerate(SEGS):
                        nc.scalar.activation(pr[:, at:at + w], s_ps[n][0:S, 0:w], ACT.Exp, bias=low[:, :], accum_out=t3[:, n:n + 1]).then_inc(exp_done, 1)
                    if has_prev:
                        copy_z(b - 1)
                    for g in range(3):
                        act.wait_ge(turned, 3 * b + g + 1)
                        after(act, z_full, b)
                        nc.scalar.activation(prT[:, 4 * g:4 * g + 4, :], t_ps[g % 2][0:KC, 0:4 * S].rearrange("p (c n) -> p c n", n=S),
                                             ACT.Copy).then_inc(prT_ready, 1)

                batches(act, body)
                copy_z(B - 1)

            @block.vector
            def _(dve):
                nc.vector.memset(pr[:, S2:NCH * KC], 0.0).then_inc(padded, 1)
                dve.wait_ge(loaded, 48)

                def scale_queries(b):
                    after(dve, s_full, 3 * b)
                    nc.vector.tensor_scalar(cs[:, :], src[:, bass.ds(b * S, S)], cols[:, 0:1], cols[:, 1:2], ALU.mult, ALU.add).then_inc(cs_ready, 1)

                def maxima(b):
                    for n, (at, w) in enumerate(SEGS):
                        dve.wait_ge(s_full, 3 * b + n + 1)
                        m = nc.vector.tensor_reduce(m3[:, n:n + 1], s_ps[n][0:S, 0:w], AX.X, ALU.max)
                    m.then_inc(max_step, 1)
                    dve.wait_ge(max_step, 4 * b + 1)
                    nc.vector.tensor_reduce(m3[:, 3:4], m3[:, 0:3], AX.X, ALU.max).then_inc(max_step, 1)
                    dve.wait_ge(max_step, 4 * b + 2)
                    after(dve, exp_done, 3 * b)
                    nc.vector.tensor_scalar(low[:, :], m3[:, 3:4], -1.0, None, ALU.mult).then_inc(max_step, 1)
                    dve.wait_ge(r_full, b + 1)
                    nc.vector.tensor_tensor(peak[:, bass.ds(b, 1)], m3[:, 3:4], r_ps[0:S, 0:1], ALU.add).then_inc(max_step, 1)
                    dve.wait_ge(max_step, 4 * b + 4)

                def invert(b):
                    dve.wait_ge(exp_done, 3 * (b + 1))
                    nc.vector.tensor_reduce(tot[:, :], t3[:, :], AX.X, ALU.add).then_inc(tot_step, 1)
                    dve.wait_ge(tot_step, b + 1)
                    nc.vector.reciprocal(inv[:, :], tot[:, :]).then_inc(z_step, 1)

                def normalise(b):
                    dve.wait_ge(z_step, 2 * b + 1)
                    dve.wait_ge(z_full, b + 1)
                    after(dve, z_turned, b)
                    nc.vector.tensor_scalar(z[:, :], z_ps[0:S, 0:D], inv[:, :], None, ALU.mult).then_inc(z_step, 1)

                def body(b, j, has_next, has_prev):
                    if has_next:
                        scale_queries(b + 1)
                    invert(b)
                    if has_next:
                        maxima(b + 1)
                    normalise(b)

                scale_queries(0)
                maxima(0)
                batches(dve, body)

        with Stage(nc, name + "b") as sb:
            pc = sb.sb("pc", [S, B])
            rowT = sb.sb("rowT", [B, S])
            low, tot, inv = (sb.sb(n, [B, 1]) for n in ("low", "tot", "inv"))
            spread = sb.sb("spread", [B, B, S])
            ones = sb.sb("ones", [B, 128])
            q2c = sb.sb("q2c", [128, B])
            junk = [sb.sb(f"junk{j}", [128, GT]) for j in range(2)]
            ca = [sb.sb(f"ca{j}", [128, GT]) for j in range(2)]
            cq = [sb.sb(f"cq{j}", [128, GT]) for j in range(2)]
            p_ps = sb.ps("p", [128, BANK])
            b_ps = [sb.ps(f"b{j}", [128, BANK]) for j in range(2)]
            o_ps = [sb.ps(f"o{j}", [128, BANK]) for j in range(2)]
            chain, peak_ready, turned, shifted, exp_done, spread_ready, b_full, q2c_done, ca_ready, cq_ready, o_full, o_added = (
                sb.sem(n) for n in ("chain", "peak_ready", "turned", "shifted", "exp_done", "spread_ready", "b_full", "q2c_done",
                                    "ca_ready", "cq_ready", "o_full", "o_added"))
            summed = sb.sem("summed")
            block = sb.ctx.enter_context(nc.Block())

            @block.tensor
            def _(pe):
                pe.wait_ge(peak_ready, 1)
                nc.tensor.transpose(p_ps[0:B, 0:S], pc[:, :], G["ident"][0:S, 0:S]).then_inc(turned, 1)
                pe.wait_ge(spread_ready, 1)

                def group(g, j):
                    part = slice(g * GT, (g + 1) * GT)
                    after(pe, q2c_done, g - 1)
                    nc.tensor.matmul(b_ps[j][:, 0:GT], ones[:, :], spread[:, g * GB:(g + 1) * GB, :].rearrange("p b n -> p (b n)"),
                                     start=True, stop=True).then_inc(b_full, 1)
                    after(pe, o_added, g - 1)
                    nc.tensor.matmul(o_ps[j][:, 0:GT], wl[:, 0, :], src[:, part], start=True, stop=False)
                    nc.tensor.matmul(o_ps[j][:, 0:GT], wl[:, 1, :], a_all[:, part], start=False, stop=False)
                    pe.wait_ge(ca_ready, g + 1)
                    nc.tensor.matmul(o_ps[j][:, 0:GT], wl[:, 2, :], ca[j][:, :], start=False, stop=False)
                    pe.wait_ge(cq_ready, g + 1)
                    nc.tensor.matmul(o_ps[j][:, 0:GT], wl[:, 3, :], cq[j][:, :], start=False, stop=True).then_inc(o_full, 1)

                for g in range(NG):
                    group(g, g % 2)

            @block.scalar
            def _(act):
                act.wait_ge(shifted, 1)
                nc.scalar.activation(rowT[:, :], p_ps[0:B, 0:S], ACT.Exp, bias=low[:, :], accum_out=tot[:, :]).then_inc(exp_done, 1)

            @block.gpsimd
            def _(pool):
                for g in range(NG):
                    after(pool, o_full, g - 1)
                    part = slice(g * GT, (g + 1) * GT)
                    nc.gpsimd.tensor_tensor(ca[g % 2][:, :], src[:, part], a_all[:, part], ALU.mult).then_inc(ca_ready, 1)

            @block.vector
            def _(dve):
                link = Link(dve, chain, 4, 0)
                link(nc.vector.memset(ones[:, :], 1.0))
                link(nc.vector.tensor_scalar(pc[:, :], peak[:, :], consts[:, 0:1], consts[:, 1:2], ALU.add, ALU.add))
                nc.vector.tensor_scalar(pc[:, :], pc[:, :], consts[:, 2:3], None, ALU.add).then_inc(peak_ready, 1)
                dve.wait_ge(turned, 1)
                nc.vector.tensor_reduce(low[:, :], p_ps[0:B, 0:S], AX.X, ALU.max, negate=True).then_inc(shifted, 1)
                dve.wait_ge(exp_done, 1)
                link(nc.vector.reciprocal(inv[:, :], tot[:, :]))
                link(nc.vector.tensor_scalar(rowT[:, :], rowT[:, :], inv[:, :], None, ALU.mult))
                nc.vector.tensor_tensor(spread[:, :, :], rowT[:, :].unsqueeze(1).to_broadcast([B, B, S]),
                                        G["ident"][0:B, 0:B].unsqueeze(2).to_broadcast([B, B, S]), ALU.mult).then_inc(spread_ready, 1)
                for g in range(NG):
                    j, part = g % 2, slice(g * GT, (g + 1) * GT)
                    dve.wait_ge(b_full, g + 1)
                    after(dve, cq_ready, g - 1)
                    nc.vector.tensor_tensor(junk[j][:, :], src[:, part], b_ps[j][:, 0:GT], ALU.mult).then_inc(q2c_done, 1)
                    dve.wait_ge(q2c_done, g + 1)
                    nc.vector.tensor_reduce(q2c[:, g * GB:(g + 1) * GB], junk[j][:, :].rearrange("p (b n) -> p b n", n=S), AX.X,
                                            ALU.add).then_inc(summed, 1)
                    dve.wait_ge(summed, g + 1)
                    after(dve, o_full, g - 1)
                    nc.vector.tensor_tensor(cq[j][:, :].rearrange("p (b n) -> p b n", n=S), src[:, part].rearrange("p (b n) -> p b n", n=S),
                                            q2c[:, g * GB:(g + 1) * GB].unsqueeze(2).to_broadcast([128, GB, S]), ALU.mult).then_inc(cq_ready, 1)
                    dve.wait_ge(o_full, g + 1)
                    nc.vector.scalar_tensor_tensor(out=acc[:, part], in0=o_ps[j][:, 0:GT], scalar=cols[:, 3:4], in1=acc[:, part],
                                                   op0=ALU.add, op1=ALU.add).then_inc(o_added, 1)
                link.end()


def stage_cross2(nc, G, I):
    layer_norm(nc, "s7ln", G, G["xT"], G["xn"])
    bidirectional_attention(nc, "s7x", G, I, G["xT"], G["xn"])


STAGE_FUNCS = {7: stage_cross2, 8: stage_ffn2, 10: stage_cross3, 11: stage_ffn3, 0: stage_self0, 3: stage_self1, 6: stage_self2, 9: stage_self3, 1: stage_cross0, 4: stage_cross1, 2: stage_ffn0, 5: stage_ffn1}


def build(nc, I, out):
    ctx = ExitStack()
    with ctx:
        def sb(name, shape, dt=F32):
            return ctx.enter_context(nc.sbuf_tensor(name, list(shape), dt))

        G = {"xT": sb("xT", [128, TOK]), "xn": sb("xn", [128, TOK]), "ident": sb("ident", [128, 128]),
             "mean_mat": sb("mean_mat", [128, 128]),
             "mean_band": sb("mean_band", [128, 2 * 128 - 128 // NG]), "pick": sb("pick", [128, NG, 128]), "ident_bf": sb("ident_bf", [128, 128], BF16),
             "eps": sb("eps", [128, 1])}
        G["q_dram"] = nc.dram_tensor("q_parts", (3, D, TOK), BF16, kind="Internal").ap()
        G["k_dram"] = nc.dram_tensor("k_parts", (2, 3, D, S2), BF16, kind="Internal").ap()
        for k in ("earlier", "pick", "block_mask"):
            G[k + "_dram"] = I["c_" + k]
        with Stage(nc, "init") as st:
            loaded = st.sem("loaded")
            made = st.sem("made")
            block = st.ctx.enter_context(nc.Block())

            @block.sync
            def _(sp):
                sp.dma_start(G["xT"][:, :], I["x"]).then_inc(loaded, 16)
                sp.dma_start(G["ident"][:, :], I["c_ident"]).then_inc(loaded, 16)
                sp.wait_ge(loaded, 32)

            @block.vector
            def _(dve):
                rows = 128 // NG
                link = Link(dve, made, 5 + NG, 0)
                link(nc.vector.memset(G["mean_mat"][:, :], 1.0 / D))
                link(nc.vector.memset(G["eps"][:, :], EPS))
                link(nc.vector.memset(G["mean_band"][:, :], 0.0))
                link(nc.vector.memset(G["mean_band"][:, 128 - rows:128], 1.0 / D))
                dve.wait_ge(loaded, 32)
                link(nc.vector.tensor_copy(G["ident_bf"][:, :], G["ident"][:, :]))
                for g in range(NG):
                    link(nc.vector.tensor_copy(G["pick"][:, g, :], G["ident"][:, g * rows:g * rows + 1].to_broadcast([128, 128])))
                link.end()

        for s in STAGES:
            STAGE_FUNCS[s](nc, G, I)

        with Stage(nc, "fin") as st:
            saved = st.sem("saved")
            block = st.ctx.enter_context(nc.Block())

            @block.sync
            def _(sp):
                sp.dma_start(out, G["xT"][:, :]).then_inc(saved, 16)
                sp.wait_ge(saved, 16)


def lay_out(v):
    A = {}
    A["x"] = v["x"].transpose(2, 0, 1).reshape(D, TOK)
    A["c_ident"] = np.eye(128, dtype=np.float32)
    A["c_earlier"] = np.broadcast_to(np.tril(np.ones((8, 8), np.float32), -1), (S, 8, 8))
    A["c_pick"] = np.broadcast_to(np.eye(128, 9, dtype=np.float32)[:, :, None], (128, 9, 128))
    q, k = np.arange(S)[:, None], np.arange(S)[None, :]
    A["c_block_mask"] = (np.arange(128)[:, None] // 8 == np.arange(16)[None, :]).astype(np.float32)
    A["c_causal01"] = (k <= q).astype(np.float32)[:, None, :]
    A["c_causal"] = np.where(k <= q, 0.0, NEVER).astype(np.float32)[:, None, :]
    slope = (2.0 ** (-8.0 / 16 * (np.arange(16, dtype=np.float32) + 1.0))).astype(np.float32)
    alibi = slope[None, :, None] * (k - q).astype(np.float32)[:, None, :]
    A["c_alibi"] = np.where((k <= q)[:, None, :], alibi, NEVER).astype(np.float32)

    def rows(w):
        return w.reshape(-1, 128, w.shape[-1]).transpose(1, 0, 2)

    def columns(b):
        return b.reshape(-1, 128).T

    for n in "QKV":
        A["L0_attn_W_" + n] = v["L0_attn_W_" + n].transpose(1, 0, 2).reshape(D, 1024)
    A["L0_attn_W_O"] = rows(v["L0_attn_W_O"].reshape(1024, D))
    A["L0_attn_b_Q"], A["L0_attn_b_K"] = columns(v["L0_attn_b_Q"]), columns(v["L0_attn_b_K"])
    A["L0_attn_b_V"] = v["L0_attn_b_V"].reshape(-1)
    A["L0_attn_b_O"] = v["L0_attn_b_O"].reshape(D, 1)
    A["L0_ln"] = np.stack([v["L0_attn_" + n] for n in ("ln1_w", "ln1_b", "ln2_w", "ln2_b")], 1)
    A["L1_attn_Wq"] = v["L1_attn_Wq"]
    A["L1_attn_Wk"], A["L1_attn_Wv"] = v["L1_attn_Wkv"][:, :1024], v["L1_attn_Wkv"][:, 1024:]
    A["L1_attn_Wo"] = rows(v["L1_attn_Wo"])
    A["L1_attn_bo"] = v["L1_attn_bo"].reshape(D, 1)
    for m, n in enumerate(("wq", "wk", "wv")):
        A["L2_attn_" + n] = v["L2_attn_w_in"][m * D:(m + 1) * D].T
        A["L3_attn_" + n] = v["L3_attn_" + n].T
    wo = np.zeros((4, 4, 32, D), np.float32)
    wo[:, :, 0:8] = v["L2_attn_w_out"].T.reshape(4, 4, 8, D)
    A["L2_attn_wo"] = wo.reshape(4, 128, D).transpose(1, 0, 2)
    A["L3_attn_wo"] = rows(v["L3_attn_wo"].T)
    heads = []
    for h in range(16):
        f = slice(h * 64, h * 64 + 64)
        cols = []
        for n in "qk":
            cols += [v["L2_ffn_W" + n][:, f], np.tile(v["L2_ffn_b" + n][f], 2)[:, None]]
        cols += [v["L2_ffn_Wv"][:, f], np.broadcast_to(v["L2_ffn_bv"][f], (128, 64))]
        heads.append(np.concatenate(cols, 1))
    A["L2_ffn_heads"] = np.stack(heads)
    A["L2_ffn_Wr"], A["L2_ffn_br"] = v["L2_ffn_Wr"], v["L2_ffn_br"]
    A["L2_ffn_Wo"] = rows(v["L2_ffn_Wo"])
    A["L2_ffn_bo"] = v["L2_ffn_bo"].reshape(D, 1)
    A["c_diagonal"] = np.where(k == q, 0.0, NEVER).astype(np.float32)[:, None, :]
    qkv_b = v["L3_xattn_qkv_b"].reshape(3, D)
    A["L3_sa_w"] = np.stack([w.T for w in (*v["L3_xattn_qkv_w"].reshape(3, D, D), v["L3_xattn_sa_out_w"])], 1)
    A["L3_sa_cols"] = np.stack([qkv_b[0], qkv_b[1], v["L3_xattn_sa_out_b"]], 1)
    A["L3_sa_bv"] = qkv_b[2]
    A["L3_cols"] = np.concatenate([np.stack([v["L3_xattn_" + n] for n in ("ln1_g", "ln1_b", "ln2_g", "ln2_b", "ln3_g", "ln3_b")], 1),
                                   columns(v["L3_xattn_lin1_b"]), columns(v["L3_xattn_lin2_b"])], 1)
    for m, n in enumerate("qkv"):
        A["L3_x_w" + n] = v["L3_xattn_in_proj_w"][m * D:(m + 1) * D].T
        A["L3_x_b" + n] = v["L3_xattn_in_proj_b"][m * D:(m + 1) * D].reshape((D, 1) if n != "v" else (D,))
    A["L3_x_wo"] = v["L3_xattn_mha_out_w"].T
    A["L3_x_bo"] = v["L3_xattn_mha_out_b"].reshape(D, 1)
    A["L3_lin1_w"] = v["L3_xattn_lin1_w"].T.reshape(128, 4, 128)
    A["L3_lin2_w"] = rows(v["L3_xattn_lin2_w"].T)
    A["L3_ffn_w_fc"] = rows(v["L3_ffn_w_fc"])
    A["L3_ffn_w_proj"] = v["L3_ffn_w_proj"].reshape(128, 4, 128)
    A["L3_ffn_v"] = np.pad(v["L3_ffn_v"].T, ((0, 0), (0, 112)))
    A["L3_ffn_fast_b"] = np.pad(v["L3_ffn_fast_b"].T, ((0, 0), (0, 112)))
    A["L3_ffn_u"] = v["L3_ffn_u"].T
    A["L3_ffn_gate"] = v["L3_ffn_gate"].reshape(1)
    A["ctx"] = np.pad(v["ctx_1024"], ((0, 0), (0, NCH * KC - S2), (0, 0))).reshape(B, NCH, KC, D).transpose(0, 2, 1, 3)
    A["L2_x_cols"] = np.stack([v["L2_xattn_" + n] for n in ("w_cq", "w_q", "w_c", "b_l")], 1)
    A["L2_x_consts"] = np.stack([v["L2_xattn_" + n].reshape(()) for n in ("b_c", "b_q", "b_cq")])
    A["L2_x_wl"] = v["L2_xattn_W_l"].T.reshape(4, D, D).transpose(1, 0, 2)
    A["ctxT"] = v["ctx_1024"].transpose(0, 2, 1)
    mask = v["mask_Bx1xSxS2_bk1"][:, 0]
    A["mask"] = mask
    A["maskT"] = np.pad(mask, ((0, 0), (0, 0), (0, NCH * KC - S2))).reshape(B, S, NCH, KC).transpose(0, 3, 2, 1)
    A["L0_xattn_Wq"] = v["L0_xattn_Wq"].T
    A["L0_xattn_Wo"] = v["L0_xattn_Wo"].T
    for n in ("Wq", "Wk", "Wv", "Wo"):
        A["L1_xattn_" + n] = v["L1_xattn_" + n]
    for n in ("bq", "bk", "bo"):
        A["L1_xattn_" + n] = v["L1_xattn_" + n].reshape(D, 1)
    A["L1_xattn_bv"] = v["L1_xattn_bv"]
    A["L0_ffn_router_w"] = v["L0_ffn_router_w"].T
    A["L0_ffn_w1"] = v["L0_ffn_w1"].transpose(2, 0, 1)
    A["L0_ffn_w2"] = v["L0_ffn_w2"].reshape(8, 128, 2, 128).transpose(3, 0, 2, 1)
    A["L1_ffn_router_w"] = v["L1_ffn_router_w"].T
    A["L1_ffn_router_b"] = v["L1_ffn_router_b"]
    w1 = np.concatenate([v["L1_ffn_spec_w1"], v["L1_ffn_shared_w1"][None]])
    w2 = np.concatenate([v["L1_ffn_spec_w2"], v["L1_ffn_shared_w2"][None]])
    b1 = np.concatenate([v["L1_ffn_spec_b1"], v["L1_ffn_shared_b1"][None]])
    A["L1_ffn_w1"] = w1.transpose(2, 0, 1)
    A["L1_ffn_w2"] = w2.reshape(9, 128, 4, 128).transpose(3, 0, 2, 1)
    A["L1_ffn_b1"] = b1.reshape(36, 128).T
    A["L1_ffn_b2"] = np.concatenate([v["L1_ffn_spec_b2"], v["L1_ffn_shared_b2"][None]])
    return A


def kernel(**inputs):
    import concourse.bacc as bacc
    from concourse.bass_utils import run_bass_kernel_spmd

    nc = bacc.Bacc("TRN2", target_bir_lowering=False, num_devices=1)
    laid = lay_out({k: np.asarray(a) for k, a in inputs.items()})
    arrays, I = {}, {}
    for name, a in laid.items():
        a = np.ascontiguousarray(a)
        arrays[f"in_{name}"] = a
        I[name] = nc.dram_tensor(f"in_{name}", a.shape, mybir.dt.from_np(a.dtype), kind="ExternalInput").ap()
    out = nc.dram_tensor("out_xT", (D, TOK), F32, kind="ExternalOutput").ap()
    build(nc, I, out)
    r = run_bass_kernel_spmd(nc, [arrays], core_ids=[0])
    return r.results[0]["out_xT"].reshape(D, B, S).transpose(1, 2, 0)
```
